# Optimizing a Trainium2 kernel written in Bass

```python
import numpy as np
import jax
import jax.numpy as jnp

def _softmax(x, axis=-1):
    return jax.nn.softmax(x, axis=axis)

def _gelu(x):
    return jax.nn.gelu(x, approximate=True)

def _silu(x):
    return jax.nn.silu(x)

def _sigmoid(x):
    return jax.nn.sigmoid(x)

def _layernorm(x, axis=-1, eps=1e-05):
    m = jnp.mean(x, axis=axis, keepdims=True)
    v = jnp.var(x, axis=axis, keepdims=True)
    return (x - m) / jnp.sqrt(v + eps)

def _scatter_add(tgt, idx, src, axis=0):
    return tgt.at[idx].add(src)

def _segment_sum(src, seg, n):
    return jax.ops.segment_sum(src, seg, n)
kernel_name = 'mk_seq_postln_d1_jaxref_r8_7a7bdb'

def setup_inputs(seed: int=0):
    np.random.seed(seed)
    _w = jnp.asarray

    def _L0_attn_setup():
        import jax, jax.numpy as jnp
        import numpy as np
        import math
        N_EMBD = 128
        N_LAYER = 24
        LAYER_ID = 12
        B, T = (8, 256)

        def _init_params():
            C = N_EMBD
            ratio_0_to_1 = LAYER_ID / (N_LAYER - 1)
            ratio_1_to_almost0 = 1.0 - LAYER_ID / N_LAYER
            h = np.arange(C, dtype=np.float64)
            decay_speed = -5.0 + 8.0 * (h / (C - 1)) ** (0.7 + 1.3 * ratio_0_to_1)
            zigzag = ((np.arange(C) + 1) % 3 - 1) * 0.5
            time_first = np.ones(C) * math.log(0.3) + zigzag
            xline = (np.arange(C, dtype=np.float64) / C).reshape(1, 1, C)
            time_mix_k = xline ** ratio_1_to_almost0
            time_mix_v = xline ** ratio_1_to_almost0 + 0.3 * ratio_0_to_1
            time_mix_r = xline ** (0.5 * ratio_1_to_almost0)
            f32 = lambda a: jnp.asarray(a, dtype=jnp.float32)
            return (f32(decay_speed), f32(time_first), f32(time_mix_k), f32(time_mix_v), f32(time_mix_r))

        def _wkv(w, u, k, v):
            kT = jnp.swapaxes(k, 0, 1)
            vT = jnp.swapaxes(v, 0, 1)

            def step(carry, kv_t):
                p, q, o = carry
                kt, vt = kv_t
                no = jnp.maximum(o, u + kt)
                A = jnp.exp(o - no)
                Bc = jnp.exp(u + kt - no)
                y = (A * p + Bc * vt) / (A * q + Bc)
                no2 = jnp.maximum(w + o, kt)
                A2 = jnp.exp(w + o - no2)
                B2 = jnp.exp(kt - no2)
                return ((A2 * p + B2 * vt, A2 * q + B2, no2), y)
            z = jnp.zeros(k.shape[::2], dtype=k.dtype)
            init = (z, z, jnp.full_like(z, -1e+38))
            _, yT = jax.lax.scan(step, init, (kT, vT))
            return jnp.swapaxes(yT, 0, 1)
        key = jax.random.key(seed)
        kx, kk, kv, kr, ko = jax.random.split(key, 5)
        C = N_EMBD
        scale = 1.0 / np.sqrt(C)
        time_decay, time_first, tmk, tmv, tmr = _init_params()
        return {'x': jax.random.normal(kx, (B, T, C), dtype=jnp.float32), 'time_decay': time_decay, 'time_first': time_first, 'time_mix_k': tmk, 'time_mix_v': tmv, 'time_mix_r': tmr, 'W_key': jax.random.uniform(kk, (C, C), jnp.float32, -scale, scale), 'W_value': jax.random.uniform(kv, (C, C), jnp.float32, -scale, scale), 'W_receptance': jax.random.uniform(kr, (C, C), jnp.float32, -scale, scale), 'W_output': jax.random.uniform(ko, (C, C), jnp.float32, -scale, scale)}
    _L0_attn_in = _L0_attn_setup()

    def _L0_ffn_setup():
        import jax, jax.numpy as jnp
        import numpy as np
        D = 128
        F = 4 * D
        E = 8
        NS = 2
        TOP_K = 2
        B, S = (2, 128)
        key = jax.random.key(seed)
        ks = jax.random.split(key, 7)
        w = 1.0 / np.sqrt(D)
        wf = 1.0 / np.sqrt(F)
        return {'x': jax.random.normal(ks[0], (B, S, D), jnp.float32), 'centroids': jax.random.normal(ks[1], (E, D), jnp.float32) * w, 'routing_bias': jnp.zeros((E,), jnp.float32), 'Wfc_r': jax.random.normal(ks[2], (E, F, D), jnp.float32) * w, 'Wproj_r': jax.random.normal(ks[3], (E, D, F), jnp.float32) * wf, 'Wfc_sh': jax.random.normal(ks[4], (NS, F, D), jnp.float32) * w, 'Wproj_sh': jax.random.normal(ks[5], (NS, D, F), jnp.float32) * wf}
    _L0_ffn_in = _L0_ffn_setup()
    _d = {'L0_attn_x': _L0_attn_in['x'], 'L0_attn_time_decay': _L0_attn_in['time_decay'], 'L0_attn_time_first': _L0_attn_in['time_first'], 'L0_attn_time_mix_k': _L0_attn_in['time_mix_k'], 'L0_attn_time_mix_v': _L0_attn_in['time_mix_v'], 'L0_attn_time_mix_r': _L0_attn_in['time_mix_r'], 'L0_attn_W_key': _L0_attn_in['W_key'], 'L0_attn_W_value': _L0_attn_in['W_value'], 'L0_attn_W_receptance': _L0_attn_in['W_receptance'], 'L0_attn_W_output': _L0_attn_in['W_output'], 'L0_ffn_centroids': _L0_ffn_in['centroids'], 'L0_ffn_routing_bias': _L0_ffn_in['routing_bias'], 'L0_ffn_Wfc_r': _L0_ffn_in['Wfc_r'], 'L0_ffn_Wproj_r': _L0_ffn_in['Wproj_r'], 'L0_ffn_Wfc_sh': _L0_ffn_in['Wfc_sh'], 'L0_ffn_Wproj_sh': _L0_ffn_in['Wproj_sh']}
    _x0 = _d['L0_attn_x']
    _d['L0_attn_x'] = jax.random.normal(jax.random.fold_in(jax.random.key(seed), 1), (4, 1024, 128), dtype=_x0.dtype)
    del _x0
    return _d

def reference(L0_attn_x, L0_attn_time_decay, L0_attn_time_first, L0_attn_time_mix_k, L0_attn_time_mix_v, L0_attn_time_mix_r, L0_attn_W_key, L0_attn_W_value, L0_attn_W_receptance, L0_attn_W_output, L0_ffn_centroids, L0_ffn_routing_bias, L0_ffn_Wfc_r, L0_ffn_Wproj_r, L0_ffn_Wfc_sh, L0_ffn_Wproj_sh):

    def _L0_attn_ref(x, time_decay, time_first, time_mix_k, time_mix_v, time_mix_r, W_key, W_value, W_receptance, W_output):
        import jax, jax.numpy as jnp
        import numpy as np
        import math
        N_EMBD = 128
        N_LAYER = 24
        LAYER_ID = 12
        B, T = (8, 256)

        def _init_params():
            C = N_EMBD
            ratio_0_to_1 = LAYER_ID / (N_LAYER - 1)
            ratio_1_to_almost0 = 1.0 - LAYER_ID / N_LAYER
            h = np.arange(C, dtype=np.float64)
            decay_speed = -5.0 + 8.0 * (h / (C - 1)) ** (0.7 + 1.3 * ratio_0_to_1)
            zigzag = ((np.arange(C) + 1) % 3 - 1) * 0.5
            time_first = np.ones(C) * math.log(0.3) + zigzag
            xline = (np.arange(C, dtype=np.float64) / C).reshape(1, 1, C)
            time_mix_k = xline ** ratio_1_to_almost0
            time_mix_v = xline ** ratio_1_to_almost0 + 0.3 * ratio_0_to_1
            time_mix_r = xline ** (0.5 * ratio_1_to_almost0)
            f32 = lambda a: jnp.asarray(a, dtype=jnp.float32)
            return (f32(decay_speed), f32(time_first), f32(time_mix_k), f32(time_mix_v), f32(time_mix_r))

        def _wkv(w, u, k, v):
            kT = jnp.swapaxes(k, 0, 1)
            vT = jnp.swapaxes(v, 0, 1)

            def step(carry, kv_t):
                p, q, o = carry
                kt, vt = kv_t
                no = jnp.maximum(o, u + kt)
                A = jnp.exp(o - no)
                Bc = jnp.exp(u + kt - no)
                y = (A * p + Bc * vt) / (A * q + Bc)
                no2 = jnp.maximum(w + o, kt)
                A2 = jnp.exp(w + o - no2)
                B2 = jnp.exp(kt - no2)
                return ((A2 * p + B2 * vt, A2 * q + B2, no2), y)
            z = jnp.zeros(k.shape[::2], dtype=k.dtype)
            init = (z, z, jnp.full_like(z, -1e+38))
            _, yT = jax.lax.scan(step, init, (kT, vT))
            return jnp.swapaxes(yT, 0, 1)
        xx = jnp.concatenate([jnp.zeros_like(x[:, :1]), x[:, :-1]], axis=1)
        xk = x * time_mix_k + xx * (1.0 - time_mix_k)
        xv = x * time_mix_v + xx * (1.0 - time_mix_v)
        xr = x * time_mix_r + xx * (1.0 - time_mix_r)
        k = jnp.einsum('btc,dc->btd', xk, W_key)
        v = jnp.einsum('btc,dc->btd', xv, W_value)
        r = jnp.einsum('btc,dc->btd', xr, W_receptance)
        sr = jax.nn.sigmoid(r)
        w = -jnp.exp(time_decay)
        wkv = _wkv(w, time_first, k, v)
        return jnp.einsum('btc,dc->btd', sr * wkv, W_output)

    def _L0_ffn_ref(x, centroids, routing_bias, Wfc_r, Wproj_r, Wfc_sh, Wproj_sh):
        import jax, jax.numpy as jnp
        import numpy as np
        D = 128
        F = 4 * D
        E = 8
        NS = 2
        TOP_K = 2
        B, S = (2, 128)
        raw = jnp.einsum('bsd,ed->bse', x, centroids)
        routing_scores = jax.nn.sigmoid(raw)
        balanced = jax.nn.sigmoid(raw + routing_bias)
        _, top_idx = jax.lax.top_k(balanced, TOP_K)
        gathered = jnp.take_along_axis(routing_scores, top_idx, axis=-1)
        top_w = jax.nn.softmax(gathered, axis=-1)
        combine = jnp.sum(jax.nn.one_hot(top_idx, E, dtype=x.dtype) * top_w[..., None], axis=-2)
        h_sh = jax.nn.gelu(jnp.einsum('bsd,nfd->bsnf', x, Wfc_sh), approximate=False)
        shared_out = jnp.einsum('bsnf,ndf->bsd', h_sh, Wproj_sh)
        h_r = jax.nn.gelu(jnp.einsum('bsd,efd->bsef', x, Wfc_r), approximate=False)
        expert_out = jnp.einsum('bsef,edf->bsed', h_r, Wproj_r)
        routed_out = jnp.einsum('bsed,bse->bsd', expert_out, combine)
        return x + shared_out + routed_out
    x = L0_attn_x
    x = _layernorm(x + _L0_attn_ref(x, L0_attn_time_decay, L0_attn_time_first, L0_attn_time_mix_k, L0_attn_time_mix_v, L0_attn_time_mix_r, L0_attn_W_key, L0_attn_W_value, L0_attn_W_receptance, L0_attn_W_output), axis=-1)
    x = _layernorm(x + _L0_ffn_ref(x, L0_ffn_centroids, L0_ffn_routing_bias, L0_ffn_Wfc_r, L0_ffn_Wproj_r, L0_ffn_Wfc_sh, L0_ffn_Wproj_sh), axis=-1)
    return x

_drawn_inputs = setup_inputs


def setup_inputs(seed=0):
    import zlib

    import numpy as np

    out = dict(_drawn_inputs(seed))
    spreads = {'L0_ffn_routing_bias': (0.0, 0.1)}
    factors = {'L0_attn_time_first': 2.888, 'L0_attn_time_mix_k': 2.853, 'L0_attn_time_mix_r': 4.188}
    for name, (base, spread) in spreads.items():
        noise = np.random.default_rng([zlib.crc32(name.encode()), seed]).standard_normal(out[name].shape)
        drawn = base * np.exp(spread * noise) if base else spread * noise
        out[name] = jnp.asarray(drawn.astype(out[name].dtype))
    for name, factor in factors.items():
        out[name] = (out[name] * factor).astype(out[name].dtype)
    return out
```

```python
from contextlib import ExitStack

import numpy as np
import concourse.bass as bass
from concourse import mybir

ALU = mybir.AluOpType
ACT = mybir.ActivationFunctionType
AX_X = mybir.AxisListType.X
F32 = mybir.dt.float32
F16 = mybir.dt.float16
I32 = mybir.dt.int32
U32 = mybir.dt.uint32

P = 128
B, T, C = 4, 1024, 128
TOKENS = B * T
CH = 512
TILES = CH // P
CHUNKS = TOKENS // CH
HALVES = T // CH
NT = TOKENS // P
E = 8
NS = 2
TOP_K = 2
FF = 512
FC = FF // P
SF = NS * FC
UT = 256
UH = UT // P
CAP = TOKENS + UT
ROW = 2 * C + 2
DUMP = E * CAP
UNITS = 4 * -(-((TOP_K * TOKENS + E * (UT - 1)) // UT) // 4)
RING = 4
EPS = 1e-5
SW = 64.0
SX = 64.0
SH = 16.0

K_ID, K_I8, K_EB, K_EN, K_IU, K_END = np.cumsum([0, P, TILES * E, E, E, UNITS]).tolist()


class Chunk:

    def __init__(self, half, par):
        self.half, self.par, self.n = half, par, half * 2 + par


def build(nc, xT, w_att, vecs, w_sh, w_rt, cent, bias, kf, kh, kid, out):
    ctx = ExitStack()
    with ctx:
        def sb(name, shape, dt=F32):
            return ctx.enter_context(nc.sbuf_tensor(name, shape, dt))

        def sem(name):
            return ctx.enter_context(nc.semaphore(name))

        sorted_x = nc.dram_tensor("sorted_x", (DUMP + UT, ROW), F16, kind="Internal").ap()
        routed_y = nc.dram_tensor("routed_y", (TOKENS * TOP_K, C), F32, kind="Internal").ap()

        consts = sb("consts", [P, K_END])
        half_consts = sb("half_consts", [P, 3 * P], F16)
        row_ids = sb("row_ids", [P, NT, TOP_K], I32)
        ident = consts[:, K_ID:K_ID + P]
        iota8 = consts[:, K_I8:K_I8 + TILES * E]
        iota_u = consts[:, K_IU:K_IU + UNITS]
        ident_h = half_consts[:, 0:P]
        before = half_consts[:, P:2 * P]
        ones_h = half_consts[:, 2 * P:3 * P]
        vec = sb("vec", [P, 5])
        att_raw = sb("att_raw", [P, 4, C])
        one_minus = sb("one_minus", [P, 3])
        att_w = sb("att_w", [P, 3, 2, C])
        decay = sb("decay", [P, 1])
        neg_w = sb("neg_w", [P, 1])
        w_row = sb("w_row", [P, CH])
        sh_raw = sb("sh_raw", [P, 2, SF * P])
        sh_w = sb("sh_w", [P, 2, 2, SF * P], F16)
        cent_raw = sb("cent_raw", [P, E])
        cent_w = sb("cent_w", [P, 2, E], F16)
        bias_row = sb("bias_row", [P, TILES * E])
        stage = [sb(f"stage{i}", [P, 2 * FF]) for i in range(2)]
        rt_w = sb("rt_w", [P, E, 2, 2 * FF], F16)
        w_scale = sb("w_scale", [P, 1])
        xt = [sb(f"xt{i}", [P, CH + 1]) for i in range(2)]
        state = [sb(f"state{i}", [P, 3, CH + 1]) for i in range(2)]
        diff = sb("diff", [P, 2, CH])
        relu = sb("relu", [P, 2, 2, CH])
        expd = sb("expd", [P, 2, 2, CH])
        b2v = sb("b2v", [P, CH])
        bv = sb("bv", [P, CH])
        ap_ = sb("ap_", [P, CH])
        num = sb("num", [P, CH])
        aq = sb("aq", [P, CH])
        den = sb("den", [P, CH])
        ln_den = sb("ln_den", [P, CH])
        rec0 = sb("rec0", [P, CH])
        newton = sb("newton", [P, CH])
        neg_rec = sb("neg_rec", [P, CH])
        gate = sb("gate", [P, CH])
        wkv = sb("wkv", [P, CH])
        gated = sb("gated", [P, CH])
        bst = sb("bst", [P, TILES, 6])
        ln_m = sb("ln_m", [P, TILES])
        ln_d = sb("ln_d", [P, TILES])
        ln_s = sb("ln_s", [P, TILES])
        ln_q = sb("ln_q", [P, TILES])
        ln_e = sb("ln_e", [P, TILES])
        var_e = sb("var_e", [P, TILES])
        ln_v = sb("ln_v", [P, TILES])
        rs0 = sb("rs0", [P, TILES])
        rs_a = sb("rs_a", [P, TILES])
        rs_b = sb("rs_b", [P, TILES])
        rs_c = sb("rs_c", [P, TILES])
        rstd = sb("rstd", [P, TILES])
        shift = sb("shift", [P, TILES])
        x1 = [sb(f"x1_{i}", [P, TILES, C]) for i in range(2)]
        base = sb("base", [P, NT, C])
        rows = [sb(f"rows{i}", [P, TILES, ROW], F16) for i in range(2)]
        x1t = [sb(f"x1t{i}", [P, 2, CH], F16) for i in range(2)]
        logits = sb("logits", [P, 2, TILES * E])
        tanhs = sb("tanhs", [P, 2, TILES * E])
        scores = sb("scores", [P, 2, TILES * E])
        top = sb("top", [P, TILES, 8])
        top_i = sb("top_i", [P, TILES, 8], U32)
        top_f = sb("top_f", [P, TOP_K, TILES])
        hot = sb("hot", [P, TOP_K, TILES * E])
        chosen = sb("chosen", [P, TILES * E], F16)
        hot_s = sb("hot_s", [P, TOP_K, TILES * E])
        got = sb("got", [P, TOP_K, TILES])
        gap = sb("gap", [P, NT])
        gap_t = sb("gap_t", [P, NT])
        mix = sb("mix", [P, TOP_K, NT])
        slot_e = sb("slot_e", [P, TILES * E])
        taken = sb("taken", [P, E])
        hot_r = sb("hot_r", [P, TOP_K, TILES * E])
        slot_f = sb("slot_f", [P, TOP_K, TILES])
        slot = [sb(f"slot{i}", [P, TOP_K, TILES], I32) for i in range(2)]
        cnt_f = sb("cnt_f", [P, E])
        cnt_i = sb("cnt_i", [P, E], I32)
        tile_i = sb("tile_i", [P, E], I32)
        tile_f = sb("tile_f", [P, E])
        ones8 = sb("ones8", [P, E])
        cum = sb("cum", [P, E])
        past = sb("past", [P, UNITS, E])
        past_c = sb("past_c", [P, UNITS, E])
        unit_e = sb("unit_e", [P, UNITS])
        unit_s = sb("unit_s", [P, UNITS])
        unit_j = sb("unit_j", [P, UNITS])
        unit_r = sb("unit_r", [P, UNITS])
        unit_r2 = sb("unit_r2", [P, UNITS])
        unit_row = sb("unit_row", [P, UNITS], I32)
        unit_w = sb("unit_w", [P, UNITS], I32)
        end_row = sb("end_row", [P, E], I32)
        pad = sb("pad", [P, UH, ROW], F16)
        xs = [sb(f"xs{i}", [P, UH, ROW], F16) for i in range(RING)]
        ys = [sb(f"ys{i}", [P, UH, C]) for i in range(RING)]
        unit_id = [sb(f"unit_id{i}", [P, UH], I32) for i in range(RING)]
        no_ids = sb("no_ids", [P, UH], I32)
        hid = [sb(f"hid{i}", [P, FC * UT]) for i in range(2)]
        hid_h = [sb(f"hid_h{i}", [P, FC * UT], F16) for i in range(2)]
        hid_l = [sb(f"hid_l{i}", [P, FC * UT], F16) for i in range(2)]
        yl = [sb(f"yl{i}", [P, TILES, TOP_K * C]) for i in range(2)]
        acc = [sb(f"acc{i}", [P, TILES, C]) for i in range(2)]
        acc2 = [sb(f"acc2{i}", [P, TILES, C]) for i in range(2)]
        fin = [sb(f"fin{i}", [P, TILES, C]) for i in range(2)]

        ps = ctx.enter_context(nc.psum_tensor("ps", [P, 8, 512], F32))
        K, V, R, ATT = (ps[:, i, :] for i in range(4))
        TR = ps[:, 4, :].bitcast(F16).rearrange("p (s n) -> p s n", s=2)
        FCB = [ps[:, 5 + i, :] for i in range(2)]
        Y = ps[:, 7, :]
        LOGIT = ps[:, 3, 0:TILES * E]
        RANK = ps[:, 3, 64:64 + TILES * E]
        TOTAL = ps[:, 3, 128:128 + E]
        FCU = [ps[:, 2 * i:2 * i + 2, :].rearrange("p b n -> p (b n)") for i in range(2)]
        TRU = [ps[:, 4 + i, 0:UT].bitcast(F16).rearrange("p (s n) -> p s n", s=2) for i in range(2)]
        YU = [ps[:, 6 + i, 0:UH * C] for i in range(2)]

        consts_in = sem("consts_in")
        att_in = sem("att_in")
        shared_in = sem("shared_in")
        stage_in = [sem(f"stage_in{i}") for i in range(2)]
        xt_in = [sem(f"xt_in{i}") for i in range(2)]
        decay_done = sem("decay_done")
        prep = sem("prep")
        w_scaled = sem("w_scaled")
        w_high = sem("w_high")
        w_low = sem("w_low")
        scale_made = sem("scale_made")
        pad_made = sem("pad_made")
        pads_out = sem("pads_out")
        k_ready, v_ready, r_ready = sem("k_ready"), sem("v_ready"), sem("r_ready")
        carried = sem("carried")
        o_done, p_done, q_done = sem("o_done"), sem("p_done"), sem("q_done")
        diff_done = sem("diff_done")
        relu_done = sem("relu_done")
        exp_state = sem("exp_state")
        exp_out = sem("exp_out")
        b2v_done = sem("b2v_done")
        bv_done = sem("bv_done")
        ap_done = sem("ap_done")
        num_done = sem("num_done")
        aq_done = sem("aq_done")
        den_done = sem("den_done")
        ln_done = sem("ln_done")
        rec0_done = sem("rec0_done")
        newton_done = sem("newton_done")
        rec_done = sem("rec_done")
        gate_done = sem("gate_done")
        wkv_done = sem("wkv_done")
        gated_done = sem("gated_done")
        att_ready = sem("att_ready")
        bst_done = sem("bst_done")
        mv_done = sem("mv_done")
        var_done = sem("var_done")
        lnv_done = sem("lnv_done")
        rs0_done = sem("rs0_done")
        rs_step = sem("rs_step")
        norm_done = sem("norm_done")
        x1_done = sem("x1_done")
        high_done = sem("high_done")
        rows_done = sem("rows_done")
        turned = sem("turned")
        x1t_done = sem("x1t_done")
        logit_ready = sem("logit_ready")
        logits_done = sem("logits_done")
        tanh_done = sem("tanh_done")
        scores_done = sem("scores_done")
        top_done = sem("top_done")
        topi_done = sem("topi_done")
        topf_done = sem("topf_done")
        hot_done = sem("hot_done")
        chosen_done = sem("chosen_done")
        hots_done = sem("hots_done")
        got_done = sem("got_done")
        gap_done = sem("gap_done")
        rank_ready = sem("rank_ready")
        slote_done = sem("slote_done")
        taken_done = sem("taken_done")
        hotr_done = sem("hotr_done")
        slotf_done = sem("slotf_done")
        slot_done = sem("slot_done")
        ids_done = sem("ids_done")
        scattered = [sem(f"scattered{i}") for i in range(2)]
        fc_ready = sem("fc_ready")
        hid_done = sem("hid_done")
        hidh_done = sem("hidh_done")
        hidl_done = sem("hidl_done")
        proj_done = sem("proj_done")
        base_done = sem("base_done")
        table = sem("table")
        ends_ready = sem("ends_ready")
        table_ready = sem("table_ready")
        xs_in = [sem(f"xs_in{i}") for i in range(RING)]
        u_ids = sem("u_ids")
        u_turned = sem("u_turned")
        u_xt = sem("u_xt")
        u_fc = sem("u_fc")
        u_hid = sem("u_hid")
        u_hidh = sem("u_hidh")
        u_hidl = sem("u_hidl")
        u_y = sem("u_y")
        u_ys = sem("u_ys")
        y_out = [sem(f"y_out{i}") for i in range(RING)]
        gapt_done = sem("gapt_done")
        mix_done = sem("mix_done")
        yl_in = [sem(f"yl_in{i}") for i in range(2)]
        acc_step = sem("acc_step")
        f_bst = sem("f_bst")
        f_mv = sem("f_mv")
        f_var = sem("f_var")
        f_lnv = sem("f_lnv")
        f_rs0 = sem("f_rs0")
        f_rs = sem("f_rs")
        f_norm = sem("f_norm")
        fin_done = sem("fin_done")
        stored = [sem(f"stored{i}") for i in range(2)]

        block = ctx.enter_context(nc.Block())

        out_v = out.rearrange("b (h t p) d -> (b h) p t d", p=P, t=TILES)
        yl_v = routed_y.rearrange("(c t p k) d -> c p t (k d)", p=P, t=TILES, k=TOP_K)

        @block.sync
        def _(sp):
            def load_chunk(c):
                first = isinstance(c.half, int) and c.half == 0
                if not first:
                    sp.wait_ge(att_ready, c.n - 1)
                src = xT[:, bass.ds(c.half, 1), c.par * CH:c.par * CH + CH + 1]
                sp.dma_start(xt[c.par][:, :], src.rearrange("p a n -> p (a n)")).then_inc(xt_in[c.par], 16)
                if not first:
                    sp.wait_ge(w_low, (c.n - 1) * 2)
                sp.dma_start(stage[c.par][:, :],
                             w_rt[bass.ds(c.n, 1), :, :].rearrange("a p n -> (a p) n")).then_inc(stage_in[c.par], 16)

            sp.dma_start(att_raw[:, :, :], w_att).then_inc(att_in, 16)
            sp.dma_start(vec[:, :], vecs).then_inc(att_in, 16)
            load_chunk(Chunk(0, 0))
            sp.dma_start(consts[:, :], kf).then_inc(consts_in, 16)
            sp.dma_start(half_consts[:, :], kh).then_inc(consts_in, 16)
            sp.dma_start(row_ids[:, :, :], kid).then_inc(consts_in, 16)
            sp.dma_start(cent_raw[:, :], cent).then_inc(shared_in, 16)
            sp.dma_start(bias_row[:, :], bias).then_inc(shared_in, 16)
            sp.dma_start(sh_raw[:, :, :], w_sh).then_inc(shared_in, 16)
            load_chunk(Chunk(0, 1))
            sp.wait_ge(pad_made, 2)
            sp.dma_start(sorted_x[DUMP:DUMP + UT, :].rearrange("(j p) w -> p j w", p=P), pad[:, :, :]).then_inc(pads_out, 16)
            with sp.Fori(1, CHUNKS // 2) as h:
                load_chunk(Chunk(h, 0))
                load_chunk(Chunk(h, 1))

            sp.wait_ge(ends_ready, 1)
            with sp.Fori(0, E) as e:
                r = sp.value_load(end_row[0:1, bass.ds(e, 1)], min_val=0, max_val=DUMP)
                sp.dma_start(sorted_x[bass.ds(r, UT), :].rearrange("(j p) w -> p j w", p=P),
                             pad[:, :, :]).then_inc(pads_out, 16)

            def load_unit(u, g, j):
                r = sp.value_load(unit_row[0:1, bass.ds(u, 1)], min_val=0, max_val=DUMP)
                if not (isinstance(g, int) and g == 0):
                    sp.wait_ge(y_out[j], g * (16 * UH))
                sp.dma_start(xs[j][:, :, :], sorted_x[bass.ds(r, UT), :].rearrange("(j p) w -> p j w", p=P)).then_inc(xs_in[j], 16)

            sp.wait_ge(pads_out, 16 * (E + 1))
            for i in range(2):
                sp.wait_ge(scattered[i], CHUNKS // 2 * TILES * TOP_K * 16)
            sp.wait_ge(table_ready, 1)
            for j in range(RING):
                load_unit(j, 0, j)
            with sp.Fori(1, UNITS // RING) as g:
                for j in range(RING):
                    load_unit(g * RING + j, g, j)

            def load_results(c):
                if not (isinstance(c.half, int) and c.half == 0):
                    sp.wait_ge(acc_step, (c.n - 1) * (2 * TILES))
                sp.dma_start(yl[c.par][:, :, :], yl_v[bass.ds(c.n, 1)].rearrange("a p t n -> (a p) t n")).then_inc(yl_in[c.par], 16)

            for j in range(RING):
                sp.wait_ge(y_out[j], UNITS // RING * 16 * UH)
            load_results(Chunk(0, 0))
            load_results(Chunk(0, 1))
            with sp.Fori(1, CHUNKS // 2) as h:
                load_results(Chunk(h, 0))
                load_results(Chunk(h, 1))

        @block.tensor
        def _(pe):
            def mix_x(c, i, bank, ready):
                nc.tensor.matmul(bank, att_w[:, i, 0, :], xt[c.par][:, 1:CH + 1], start=True, stop=False)
                nc.tensor.matmul(bank, att_w[:, i, 1, :], xt[c.par][:, 0:CH], start=False, stop=True).then_inc(ready, 1)

            def turn(c):
                pe.wait_ge(rows_done, c.n + 1)
                for s in range(2):
                    for t in range(TILES):
                        mm = nc.tensor.transpose(TR[:, s, t * P:(t + 1) * P], rows[c.par][:, t, s * C:(s + 1) * C], ident_h)
                mm.then_inc(turned, 1)

            def route(c):
                pe.wait_ge(x1t_done, c.n + 1)
                for t in range(TILES):
                    for i, (s, w) in enumerate(((0, 0), (0, 1), (1, 0))):
                        mm = nc.tensor.matmul(LOGIT[:, t * E:(t + 1) * E], x1t[c.par][:, s, t * P:(t + 1) * P], cent_w[:, w, :],
                                              start=(t == 0 and i == 0), stop=(i == 2), skip_group_check=True)
                mm.then_inc(logit_ready, 1)

            def rank(c):
                pe.wait_ge(chosen_done, c.n + 1)
                for t in range(TILES):
                    for s in range(t + 1):
                        nc.tensor.matmul(RANK[:, t * E:(t + 1) * E], before if s == t else ones_h, chosen[:, s * E:(s + 1) * E],
                                         start=(t == 0), stop=(s == t), skip_group_check=True)
                for s in range(TILES):
                    mm = nc.tensor.matmul(TOTAL, ones_h, chosen[:, s * E:(s + 1) * E], start=False, stop=(s == TILES - 1),
                                          skip_group_check=True)
                mm.then_inc(rank_ready, 1)

            def shared_fc(c, f):
                n = c.n * SF + f
                if not (isinstance(n, int) and n < 2):
                    pe.wait_ge(hid_done, n - 1)
                for i, (w, s) in enumerate(((0, 0), (0, 1), (1, 0))):
                    mm = nc.tensor.matmul(FCB[f % 2], sh_w[:, 0, w, f * P:(f + 1) * P], x1t[c.par][:, s, :],
                                          start=(i == 0), stop=(i == 2))
                mm.then_inc(fc_ready, 1)

            def shared_proj(c, f):
                if f == 0 and not (isinstance(c.n, int) and c.n == 0):
                    pe.wait_ge(base_done, c.n)
                pe.wait_ge(hidl_done, c.n * SF + f + 1)
                for t in range(TILES):
                    h = [x[f % 2][:, t * P:(t + 1) * P] for x in (hid_h, hid_l)]
                    for i, (s, w) in enumerate(((0, 0), (0, 1), (1, 0))):
                        mm = nc.tensor.matmul(Y[:, t * C:(t + 1) * C], h[s], sh_w[:, 1, w, f * P:(f + 1) * P],
                                              start=(f == 0 and t == 0 and i == 0), stop=(f == SF - 1 and i == 2),
                                              skip_group_check=True)
                mm.then_inc(proj_done, 1)

            def attend_out(c):
                pe.wait_ge(gated_done, c.n + 1)
                if not (isinstance(c.n, int) and c.n == 0):
                    pe.wait_ge(taken_done, c.n)
                for t in range(TILES):
                    o = ATT[:, t * P:(t + 1) * P]
                    nc.tensor.matmul(o, gated[:, t * P:(t + 1) * P], att_raw[:, 3, :], start=(t == 0), stop=False, skip_group_check=True)
                    mm = nc.tensor.matmul(o, xt[c.par][:, 1 + t * P:1 + (t + 1) * P], ident, start=False, stop=True,
                                          skip_group_check=True)
                mm.then_inc(att_ready, 1)

            def step(c, q):
                if q is not None:
                    turn(q)
                if c is not None:
                    pe.wait_ge(xt_in[c.par], c.half * 16 + 16)
                    mix_x(c, 0, K, k_ready)
                if q is not None:
                    route(q)
                if c is not None:
                    mix_x(c, 1, V, v_ready)
                    mix_x(c, 2, R, r_ready)
                for f in range(SF + 1):
                    if q is not None:
                        if f < SF:
                            shared_fc(q, f)
                        if f > 0:
                            shared_proj(q, f - 1)
                        if f == 2:
                            rank(q)
                    if f == 6 and c is not None:
                        attend_out(c)

            pe.wait_ge(prep, 8)
            pe.wait_ge(consts_in, 48)
            step(Chunk(0, 0), None)
            pe.wait_ge(prep, PREP_ALL)
            step(Chunk(0, 1), Chunk(0, 0))
            with pe.Fori(1, CHUNKS // 2) as h:
                step(Chunk(h, 0), Chunk(h - 1, 1))
                step(Chunk(h, 1), Chunk(h, 0))
            step(None, Chunk(CHUNKS // 2 - 1, 1))

            def unit_turn(u, g, j):
                pe.wait_ge(xs_in[j], g * 16 + 16)
                if not (isinstance(u, int) and u < 2):
                    pe.wait_ge(u_xt, u - 1)
                for s in range(2):
                    for k in range(UH):
                        mm = nc.tensor.transpose(TRU[j % 2][:, s, k * P:(k + 1) * P], xs[j][:, k, s * C:(s + 1) * C], ident_h)
                mm.then_inc(u_turned, 1)

            def unit_fc(u, j):
                e = pe.value_load(unit_w[0:1, bass.ds(u, 1)], min_val=0, max_val=E - 1)
                w = [rt_w[:, bass.ds(e, 1), s, 0:FF].rearrange("p a n -> p (a n)") for s in range(2)]
                pe.wait_ge(u_xt, u + 1)
                if not (isinstance(u, int) and u < 2):
                    pe.wait_ge(u_hid, u - 1)
                for f in range(FC):
                    for i, (a, s) in enumerate(((0, 0), (0, 1), (1, 0))):
                        mm = nc.tensor.matmul(FCU[j % 2][:, f * UT:(f + 1) * UT], w[a][:, f * P:(f + 1) * P], x1t[j % 2][:, s, 0:UT],
                                              start=(f % 2 == 0 and i == 0), stop=(i == 2), skip_group_check=True)
                mm.then_inc(u_fc, 1)

            def unit_proj(u, j):
                e = pe.value_load(unit_w[0:1, bass.ds(u, 1)], min_val=0, max_val=E - 1)
                w = [rt_w[:, bass.ds(e, 1), s, FF:2 * FF].rearrange("p a n -> p (a n)") for s in range(2)]
                pe.wait_ge(u_hidl, u + 1)
                if not (isinstance(u, int) and u < 2):
                    pe.wait_ge(u_ys, u - 1)
                for f in range(FC):
                    for k in range(UH):
                        h = [x[j % 2][:, f * UT + k * P:f * UT + (k + 1) * P] for x in (hid_h, hid_l)]
                        for i, (s, a) in enumerate(((0, 0), (0, 1), (1, 0))):
                            mm = nc.tensor.matmul(YU[j % 2][:, k * C:(k + 1) * C], h[s], w[a][:, f * P:(f + 1) * P],
                                                  start=(f == 0 and k == 0 and i == 0), stop=(f == FC - 1 and i == 2),
                                                  skip_group_check=True)
                mm.then_inc(u_y, 1)

            pe.wait_ge(base_done, CHUNKS)
            pe.wait_ge(taken_done, CHUNKS)
            pe.wait_ge(w_low, E * 2)
            pe.wait_ge(table_ready, 1)
            unit_turn(0, 0, 0)
            for j in range(RING - 1):
                unit_turn(j + 1, 0, j + 1)
                unit_fc(j, j)
                if j > 0:
                    unit_proj(j - 1, j - 1)
            with pe.Fori(1, UNITS // RING) as g:
                for j in range(RING):
                    u = g * RING + j
                    unit_turn(u, g, j)
                    unit_fc(u - 1, (j - 1) % RING)
                    unit_proj(u - 2, (j - 2) % RING)
            unit_fc(UNITS - 1, RING - 1)
            unit_proj(UNITS - 2, RING - 2)
            unit_proj(UNITS - 1, RING - 1)

        @block.scalar
        def _(act):
            def exps(c):
                act.wait_ge(diff_done, c.n * 2 + 2)
                nc.scalar.activation(relu[:, 0, :, :], diff[:, :, :], ACT.Relu).then_inc(relu_done, 1)
                nc.scalar.activation(relu[:, 1, :, :], diff[:, :, :], ACT.Relu, scale=-1.0).then_inc(relu_done, 1)
                act.wait_ge(relu_done, c.n * 2 + 2)
                nc.scalar.activation(expd[:, :, 0, :], relu[:, :, 0, :], ACT.Exp, scale=-1.0).then_inc(exp_state, 1)
                nc.scalar.activation(expd[:, :, 1, :], relu[:, :, 1, :], ACT.Exp, scale=-1.0).then_inc(exp_out, 1)

            def gates(c):
                act.wait_ge(r_ready, c.n + 1)
                nc.scalar.activation(gate[:, :], R, ACT.Tanh, scale=0.5).then_inc(gate_done, 1)

            def reciprocals(c):
                act.wait_ge(den_done, c.n + 1)
                nc.scalar.activation(ln_den[:, :], den[:, :], ACT.Ln).then_inc(ln_done, 1)
                act.wait_ge(ln_done, c.n + 1)
                nc.scalar.activation(rec0[:, :], ln_den[:, :], ACT.Exp, scale=-1.0).then_inc(rec0_done, 1)

            def normalise(c):
                act.wait_ge(var_done, c.n + 1)
                nc.scalar.activation(ln_v[:, :], var_e[:, :], ACT.Ln).then_inc(lnv_done, 1)
                act.wait_ge(lnv_done, c.n + 1)
                nc.scalar.activation(rs0[:, :], ln_v[:, :], ACT.Exp, scale=-0.5).then_inc(rs0_done, 1)
                act.wait_ge(norm_done, c.n * 2 + 2)
                for t in range(TILES):
                    nc.scalar.activation(x1[c.par][:, t, :], ATT[:, t * P:(t + 1) * P], ACT.Identity,
                                         bias=shift[:, t:t + 1], scale=rstd[:, t:t + 1]).then_inc(x1_done, 1)

            def copy_turned(c):
                act.wait_ge(turned, c.n + 1)
                nc.scalar.activation(x1t[c.par][:, :, :], TR, ACT.Copy).then_inc(x1t_done, 1)

            def squash(c):
                act.wait_ge(logits_done, c.n * 2 + 2)
                nc.scalar.activation(tanhs[:, :, :], logits[:, :, :], ACT.Tanh, scale=0.5).then_inc(tanh_done, 1)

            def shared_gelu(c, f):
                n = c.n * SF + f
                act.wait_ge(fc_ready, n + 1)
                if not (isinstance(n, int) and n < 2):
                    act.wait_ge(hidl_done, n - 1)
                nc.scalar.activation(hid[f % 2][:, 0:CH], FCB[f % 2], ACT.Gelu, scale=1.0 / (SW * SX)).then_inc(hid_done, 1)

            def step(c, q):
                if q is not None:
                    copy_turned(q)
                if c is not None:
                    exps(c)
                if q is not None:
                    squash(q)
                if c is not None:
                    gates(c)
                if q is not None:
                    for f in range(4):
                        shared_gelu(q, f)
                if c is not None:
                    reciprocals(c)
                if q is not None:
                    for f in range(4, SF):
                        shared_gelu(q, f)
                if c is not None:
                    normalise(c)

            act.wait_ge(att_in, 32)
            nc.scalar.activation(decay[:, :], vec[:, 0:1], ACT.Exp).then_inc(decay_done, 1)
            step(Chunk(0, 0), None)
            step(Chunk(0, 1), Chunk(0, 0))
            with act.Fori(1, CHUNKS // 2) as h:
                step(Chunk(h, 0), Chunk(h - 1, 1))
                step(Chunk(h, 1), Chunk(h, 0))
            step(None, Chunk(CHUNKS // 2 - 1, 1))
            act.wait_ge(gap_done, CHUNKS)
            nc.scalar.activation(gap_t[:, :], gap[:, :], ACT.Tanh, scale=0.5).then_inc(gapt_done, 1)

            def unit_xt(u, j):
                act.wait_ge(u_turned, u + 1)
                if not (isinstance(u, int) and u < 2):
                    act.wait_ge(u_fc, u - 1)
                nc.scalar.activation(x1t[j % 2][:, :, 0:UT], TRU[j % 2], ACT.Copy).then_inc(u_xt, 1)

            def unit_gelu(u, j):
                act.wait_ge(u_fc, u + 1)
                if not (isinstance(u, int) and u < 2):
                    act.wait_ge(u_hidl, u - 1)
                nc.scalar.activation(hid[j % 2][:, :], FCU[j % 2], ACT.Gelu, scale=1.0 / (SW * SX)).then_inc(u_hid, 1)

            def unit_y(u, j):
                act.wait_ge(u_y, u + 1)
                nc.scalar.activation(ys[j][:, :, :], YU[j % 2], ACT.Copy, scale=1.0 / (SW * SH)).then_inc(u_ys, 1)

            act.wait_ge(hidl_done, CHUNKS * SF)
            act.wait_ge(proj_done, CHUNKS * SF)
            unit_xt(0, 0)
            for j in range(RING - 1):
                unit_xt(j + 1, j + 1)
                unit_gelu(j, j)
                if j > 0:
                    unit_y(j - 1, j - 1)
            with act.Fori(1, UNITS // RING) as g:
                for j in range(RING):
                    u = g * RING + j
                    unit_xt(u, j)
                    unit_gelu(u - 1, (j - 1) % RING)
                    unit_y(u - 2, (j - 2) % RING)
            unit_gelu(UNITS - 1, RING - 1)
            unit_y(UNITS - 2, RING - 2)
            unit_y(UNITS - 1, RING - 1)

            def finish(c):
                act.wait_ge(f_var, c.n + 1)
                nc.scalar.activation(ln_v[:, :], var_e[:, :], ACT.Ln).then_inc(f_lnv, 1)
                act.wait_ge(f_lnv, c.n + 1)
                nc.scalar.activation(rs0[:, :], ln_v[:, :], ACT.Exp, scale=-0.5).then_inc(f_rs0, 1)
                act.wait_ge(f_norm, c.n * 2 + 2)
                if not (isinstance(c.half, int) and c.half == 0):
                    act.wait_ge(stored[c.par], c.half * 16)
                for t in range(TILES):
                    nc.scalar.activation(fin[c.par][:, t, :], acc2[c.par][:, t, :], ACT.Identity,
                                         bias=shift[:, t:t + 1], scale=rstd[:, t:t + 1]).then_inc(fin_done, 1)
                act.wait_ge(fin_done, c.n * TILES + TILES)
                act.dma_start(out_v[bass.ds(c.n, 1)].rearrange("a p t n -> (a p) t n"), fin[c.par][:, :, :]).then_inc(stored[c.par], 16)

            finish(Chunk(0, 0))
            finish(Chunk(0, 1))
            with act.Fori(1, CHUNKS // 2) as h:
                finish(Chunk(h, 0))
                finish(Chunk(h, 1))
            for i in range(2):
                act.wait_ge(stored[i], CHUNKS // 2 * 16)

        @block.vector
        def _(dve):
            v = nc.vector

            def per_tile(x):
                return x.rearrange("p (t e) -> p t e", e=E)

            def scan_max(c):
                S = state[c.par]
                if c.par == 1:
                    dve.wait_ge(q_done, c.n)
                    v.tensor_copy(S[:, :, 0:1], state[0][:, :, CH:CH + 1]).then_inc(carried, 1)
                    dve.wait_ge(carried, c.half + 1)
                dve.wait_ge(k_ready, c.n + 1)
                v.tensor_tensor_scan(S[:, 0, 1:CH + 1], w_row[:, :], K, S[:, 0, 0:1], ALU.add, ALU.max).then_inc(o_done, 1)
                dve.wait_ge(o_done, c.n + 1)
                v.scalar_tensor_tensor(out=diff[:, 0, :], in0=S[:, 0, 0:CH], scalar=neg_w[:, 0:1], in1=K,
                                       op0=ALU.add, op1=ALU.subtract).then_inc(diff_done, 1)
                v.scalar_tensor_tensor(out=diff[:, 1, :], in0=K, scalar=vec[:, 1:2], in1=S[:, 0, 0:CH],
                                       op0=ALU.add, op1=ALU.subtract).then_inc(diff_done, 1)

            def values(c):
                dve.wait_ge(v_ready, c.n + 1)
                dve.wait_ge(exp_state, c.n + 1)
                v.tensor_tensor(b2v[:, :], V, expd[:, 0, 0, :], ALU.mult).then_inc(b2v_done, 1)
                dve.wait_ge(exp_out, c.n + 1)
                v.tensor_tensor(bv[:, :], V, expd[:, 1, 1, :], ALU.mult).then_inc(bv_done, 1)

            def scan_p(c):
                S = state[c.par]
                dve.wait_ge(b2v_done, c.n + 1)
                v.tensor_tensor_scan(S[:, 1, 1:CH + 1], expd[:, 1, 0, :], b2v[:, :], S[:, 1, 0:1], ALU.mult, ALU.add).then_inc(p_done, 1)

            def scan_q(c):
                S = state[c.par]
                v.tensor_tensor_scan(S[:, 2, 1:CH + 1], expd[:, 1, 0, :], expd[:, 0, 0, :], S[:, 2, 0:1], ALU.mult, ALU.add).then_inc(q_done, 1)

            def denominators(c):
                dve.wait_ge(q_done, c.n + 1)
                v.tensor_tensor(aq[:, :], state[c.par][:, 2, 0:CH], expd[:, 0, 1, :], ALU.mult).then_inc(aq_done, 1)
                dve.wait_ge(aq_done, c.n + 1)
                v.tensor_tensor(den[:, :], aq[:, :], expd[:, 1, 1, :], ALU.add).then_inc(den_done, 1)

            def refine(c):
                dve.wait_ge(rec0_done, c.n + 1)
                v.tensor_tensor(newton[:, :], den[:, :], rec0[:, :], ALU.mult).then_inc(newton_done, 1)
                dve.wait_ge(newton_done, c.n + 1)
                v.scalar_tensor_tensor(out=neg_rec[:, :], in0=newton[:, :], scalar=2.0, in1=rec0[:, :],
                                       op0=ALU.subtract, op1=ALU.mult).then_inc(rec_done, 1)

            def gated_out(c):
                dve.wait_ge(num_done, c.n + 1)
                dve.wait_ge(rec_done, c.n + 1)
                v.scalar_tensor_tensor(out=wkv[:, :], in0=num[:, :], scalar=-0.5, in1=neg_rec[:, :],
                                       op0=ALU.mult, op1=ALU.mult).then_inc(wkv_done, 1)
                dve.wait_ge(wkv_done, c.n + 1)
                dve.wait_ge(gate_done, c.n + 1)
                v.scalar_tensor_tensor(out=gated[:, :], in0=gate[:, :], scalar=1.0, in1=wkv[:, :],
                                       op0=ALU.add, op1=ALU.mult).then_inc(gated_done, 1)

            def stats(c, src, eps, bst_s, mv_s, var_s):
                for t in range(TILES):
                    v.bn_stats(bst[:, t, :], src[t]).then_inc(bst_s, 1)
                dve.wait_ge(bst_s, c.n * TILES + TILES)
                v.tensor_tensor(ln_d[:, :], bst[:, :, 1], bst[:, :, 4], ALU.subtract).then_inc(mv_s, 1)
                v.tensor_tensor(ln_s[:, :], bst[:, :, 2], bst[:, :, 5], ALU.add).then_inc(mv_s, 1)
                v.tensor_tensor(ln_m[:, :], bst[:, :, 1], bst[:, :, 4], ALU.add).then_inc(mv_s, 1)
                dve.wait_ge(mv_s, c.n * 5 + 1)
                v.tensor_tensor(ln_q[:, :], ln_d[:, :], ln_d[:, :], ALU.mult).then_inc(mv_s, 1)
                dve.wait_ge(mv_s, c.n * 5 + 2)
                v.tensor_scalar(ln_e[:, :], ln_s[:, :], 1.0 / C, eps, ALU.mult, ALU.add).then_inc(mv_s, 1)
                dve.wait_ge(mv_s, c.n * 5 + 5)
                v.scalar_tensor_tensor(out=var_e[:, :], in0=ln_q[:, :], scalar=0.25, in1=ln_e[:, :],
                                       op0=ALU.mult, op1=ALU.add).then_inc(var_s, 1)

            def rsqrt(c, rs0_s, rs_s, norm_s):
                dve.wait_ge(rs0_s, c.n + 1)
                v.tensor_tensor(rs_a[:, :], var_e[:, :], rs0[:, :], ALU.mult).then_inc(rs_s, 1)
                dve.wait_ge(rs_s, c.n * 3 + 1)
                v.tensor_tensor(rs_b[:, :], rs_a[:, :], rs0[:, :], ALU.mult).then_inc(rs_s, 1)
                dve.wait_ge(rs_s, c.n * 3 + 2)
                v.tensor_scalar(rs_c[:, :], rs_b[:, :], -0.5, 1.5, ALU.mult, ALU.add).then_inc(rs_s, 1)
                dve.wait_ge(rs_s, c.n * 3 + 3)
                v.tensor_tensor(rstd[:, :], rs_c[:, :], rs0[:, :], ALU.mult).then_inc(norm_s, 1)
                dve.wait_ge(norm_s, c.n * 2 + 1)
                v.scalar_tensor_tensor(out=shift[:, :], in0=ln_m[:, :], scalar=-0.5, in1=rstd[:, :],
                                       op0=ALU.mult, op1=ALU.mult).then_inc(norm_s, 1)

            def norm_stats(c):
                dve.wait_ge(att_ready, c.n + 1)
                stats(c, [ATT[:, t * P:(t + 1) * P] for t in range(TILES)], EPS, bst_done, mv_done, var_done)

            def split_rows(c):
                dve.wait_ge(x1_done, c.n * TILES + TILES)
                if not (isinstance(c.half, int) and c.half == 0):
                    dve.wait_ge(scattered[c.par], c.half * (TILES * TOP_K * 16))
                x = x1[c.par][:, :, :]
                v.tensor_scalar(rows[c.par][:, :, 0:C], x, SX, None, ALU.mult).then_inc(high_done, 1)
                dve.wait_ge(high_done, c.n + 1)
                v.scalar_tensor_tensor(out=rows[c.par][:, :, C:2 * C], in0=x, scalar=SX, in1=rows[c.par][:, :, 0:C],
                                       op0=ALU.mult, op1=ALU.subtract).then_inc(rows_done, 1)

            def take_logits(c):
                dve.wait_ge(logit_ready, c.n + 1)
                v.tensor_scalar(logits[:, 0, :], LOGIT, 1.0 / (SW * SX), None, ALU.mult).then_inc(logits_done, 1)
                v.scalar_tensor_tensor(out=logits[:, 1, :], in0=LOGIT, scalar=1.0 / (SW * SX), in1=bias_row[:, :],
                                       op0=ALU.mult, op1=ALU.add).then_inc(logits_done, 1)

            def choose(c):
                dve.wait_ge(tanh_done, c.n + 1)
                v.tensor_scalar(scores[:, :, :], tanhs[:, :, :], 0.5, 0.5, ALU.mult, ALU.add).then_inc(scores_done, 1)
                dve.wait_ge(scores_done, c.n + 1)

            def choose_max(c):
                for t in range(TILES):
                    v.max(top[:, t, :], scores[:, 1, t * E:(t + 1) * E]).then_inc(top_done, 1)
                dve.wait_ge(top_done, c.n * TILES + TILES)

            def choose_index(c):
                for t in range(TILES):
                    v.max_index(top_i[:, t, :], top[:, t, :], scores[:, 1, t * E:(t + 1) * E]).then_inc(topi_done, 1)
                dve.wait_ge(topi_done, c.n * TILES + TILES)
                v.tensor_copy(top_f[:, :, :].rearrange("p k t -> p t k"), top_i[:, :, 0:TOP_K]).then_inc(topf_done, 1)
                dve.wait_ge(topf_done, c.n + 1)
                for k in range(TOP_K):
                    v.tensor_tensor(per_tile(hot[:, k, :]), per_tile(iota8),
                                    top_f[:, k, :].unsqueeze(2).to_broadcast([P, TILES, E]), ALU.is_equal).then_inc(hot_done, 1)
                dve.wait_ge(hot_done, c.n * 2 + 2)
                v.tensor_tensor(chosen[:, :], hot[:, 0, :], hot[:, 1, :], ALU.add).then_inc(chosen_done, 1)

            def gaps(c):
                v.tensor_tensor(hot_s[:, :, :], hot[:, :, :],
                                scores[:, 0:1, :].to_broadcast([P, TOP_K, TILES * E]), ALU.mult).then_inc(hots_done, 1)
                dve.wait_ge(hots_done, c.n + 1)
                v.tensor_reduce(got[:, :, :], hot_s[:, :, :].rearrange("p k (t e) -> p k t e", e=E), AX_X, ALU.add).then_inc(got_done, 1)
                dve.wait_ge(got_done, c.n + 1)
                v.tensor_tensor(gap[:, bass.ds(c.n * TILES, TILES)], got[:, 0, :], got[:, 1, :], ALU.subtract).then_inc(gap_done, 1)

            def slots(c):
                dve.wait_ge(rank_ready, c.n + 1)
                if not (isinstance(c.n, int) and c.n == 0):
                    dve.wait_ge(taken_done, c.n)
                v.tensor_tensor(per_tile(slot_e[:, :]), per_tile(RANK), taken[:, :].unsqueeze(1).to_broadcast([P, TILES, E]),
                                ALU.add).then_inc(slote_done, 1)
                dve.wait_ge(slote_done, c.n + 1)
                v.tensor_tensor(taken[:, :], TOTAL, taken[:, :], ALU.add).then_inc(taken_done, 1)
                v.tensor_tensor(hot_r[:, :, :], hot[:, :, :],
                                slot_e[:, :].unsqueeze(1).to_broadcast([P, TOP_K, TILES * E]), ALU.mult).then_inc(hotr_done, 1)
                dve.wait_ge(hotr_done, c.n + 1)
                v.tensor_reduce(slot_f[:, :, :], hot_r[:, :, :].rearrange("p k (t e) -> p k t e", e=E), AX_X, ALU.add).then_inc(slotf_done, 1)
                dve.wait_ge(slotf_done, c.n + 1)
                v.tensor_copy(slot[c.par][:, :, :], slot_f[:, :, :]).then_inc(slot_done, 1)

            def split_hidden(c, f):
                n = c.n * SF + f
                dve.wait_ge(hid_done, n + 1)
                if not (isinstance(n, int) and n < 2):
                    dve.wait_ge(proj_done, n - 1)
                h = hid[f % 2][:, 0:CH]
                v.tensor_scalar(hid_h[f % 2][:, 0:CH], h, SH, None, ALU.mult).then_inc(hidh_done, 1)
                dve.wait_ge(hidh_done, n + 1)
                v.scalar_tensor_tensor(out=hid_l[f % 2][:, 0:CH], in0=h, scalar=SH, in1=hid_h[f % 2][:, 0:CH],
                                       op0=ALU.mult, op1=ALU.subtract).then_inc(hidl_done, 1)

            def add_shared(c):
                dve.wait_ge(proj_done, c.n * SF + SF)
                v.scalar_tensor_tensor(out=base[:, bass.ds(c.n * TILES, TILES), :], in0=Y.rearrange("p (t d) -> p t d", d=C),
                                       scalar=0.5 / (SW * SH), in1=x1[c.par][:, :, :],
                                       op0=ALU.mult, op1=ALU.add).then_inc(base_done, 1)

            def step(c, q):
                if c is not None:
                    scan_max(c)
                if q is not None:
                    take_logits(q)
                if c is not None:
                    values(c)
                    scan_p(c)
                if q is not None:
                    choose(q)
                    split_hidden(q, 0)
                    choose_max(q)
                if c is not None:
                    scan_q(c)
                if q is not None:
                    split_hidden(q, 1)
                    choose_index(q)
                if c is not None:
                    denominators(c)
                if q is not None:
                    split_hidden(q, 2)
                    gaps(q)
                    slots(q)
                    split_hidden(q, 3)
                if c is not None:
                    refine(c)
                    gated_out(c)
                if q is not None:
                    split_hidden(q, 4)
                    split_hidden(q, 5)
                    split_hidden(q, 6)
                if c is not None:
                    norm_stats(c)
                if q is not None:
                    split_hidden(q, 7)
                    add_shared(q)
                if c is not None:
                    rsqrt(c, rs0_done, rs_step, norm_done)
                    split_rows(c)

            count = [0]

            def counted(ins):
                ins.then_inc(prep, 1)
                count[0] += 1

            dve.wait_ge(att_in, 32)
            counted(v.tensor_scalar(one_minus[:, :], vec[:, 2:5], -1.0, 1.0, ALU.mult, ALU.add))
            dve.wait_ge(prep, 1)
            for i in range(3):
                counted(v.tensor_scalar(att_w[:, i, 0, :], att_raw[:, i, :], vec[:, 2 + i:3 + i], None, ALU.mult))
                counted(v.tensor_scalar(att_w[:, i, 1, :], att_raw[:, i, :], one_minus[:, i:i + 1], None, ALU.mult))
            counted(v.memset(w_row[:, :], 0.0))
            counted(v.memset(state[0][:, 0, 0:1], -1e38))
            counted(v.memset(state[0][:, 1:3, 0:1], 0.0))
            counted(v.memset(ones8[:, :], 1.0))
            dve.wait_ge(decay_done, 1)
            counted(v.tensor_scalar(neg_w[:, :], decay[:, :], -1.0, None, ALU.mult))
            dve.wait_ge(prep, count[0])
            counted(v.tensor_scalar(w_row[:, :], w_row[:, :], neg_w[:, 0:1], None, ALU.add))
            dve.wait_ge(prep, count[0])
            step(Chunk(0, 0), None)
            dve.wait_ge(consts_in, 48)
            dve.wait_ge(shared_in, 48)
            counted(v.tensor_copy(taken[:, :], consts[:, K_EB:K_EB + E]))
            counted(v.tensor_scalar(cent_w[:, 0, :], cent_raw[:, :], SW, None, ALU.mult))
            for i in range(2):
                counted(v.tensor_scalar(sh_w[:, i, 0, :], sh_raw[:, i, :], SW, None, ALU.mult))
            dve.wait_ge(prep, count[0])
            counted(v.scalar_tensor_tensor(out=cent_w[:, 1, :], in0=cent_raw[:, :], scalar=SW, in1=cent_w[:, 0, :],
                                           op0=ALU.mult, op1=ALU.subtract))
            for i in range(2):
                counted(v.scalar_tensor_tensor(out=sh_w[:, i, 1, :], in0=sh_raw[:, i, :], scalar=SW, in1=sh_w[:, i, 0, :],
                                               op0=ALU.mult, op1=ALU.subtract))
            assert count[0] == PREP_ALL, count[0]
            step(Chunk(0, 1), Chunk(0, 0))
            with dve.Fori(1, CHUNKS // 2) as h:
                step(Chunk(h, 0), Chunk(h - 1, 1))
                step(Chunk(h, 1), Chunk(h, 0))
            step(None, Chunk(CHUNKS // 2 - 1, 1))

            tab = [0]

            def link(ins):
                ins.then_inc(table, 1)
                tab[0] += 1
                dve.wait_ge(table, tab[0])

            dve.wait_ge(taken_done, CHUNKS)
            v.tensor_copy(end_row[:, :], taken[:, :]).then_inc(ends_ready, 1)
            link(v.tensor_tensor(cnt_f[:, :], taken[:, :], consts[:, K_EN:K_EN + E], ALU.add))
            link(v.tensor_copy(cnt_i[:, :], cnt_f[:, :]))
            link(v.tensor_scalar(tile_i[:, :], cnt_i[:, :], UT.bit_length() - 1, None, ALU.logical_shift_right))
            link(v.tensor_copy(tile_f[:, :], tile_i[:, :]))
            link(v.tensor_tensor_scan(cum[:, :], ones8[:, :], tile_f[:, :], 0.0, ALU.mult, ALU.add))
            cum_b = cum[:, :].unsqueeze(1).to_broadcast([P, UNITS, E])
            link(v.tensor_tensor(past[:, :, :], iota_u.unsqueeze(2).to_broadcast([P, UNITS, E]), cum_b, ALU.is_ge))
            link(v.tensor_reduce(unit_e[:, :], past[:, :, :], AX_X, ALU.add))
            link(v.tensor_tensor(past_c[:, :, :], past[:, :, :], cum_b, ALU.mult))
            link(v.tensor_reduce(unit_s[:, :], past_c[:, :, :], AX_X, ALU.max))
            link(v.tensor_tensor(unit_j[:, :], iota_u, unit_s[:, :], ALU.subtract))
            link(v.tensor_scalar(unit_r[:, :], unit_e[:, :], float(CAP), None, ALU.mult))
            link(v.scalar_tensor_tensor(out=unit_r2[:, :], in0=unit_j[:, :], scalar=float(UT), in1=unit_r[:, :],
                                        op0=ALU.mult, op1=ALU.add))
            link(v.tensor_scalar(unit_row[:, :], unit_r2[:, :], float(DUMP), None, ALU.min))
            v.tensor_scalar(unit_w[:, :], unit_e[:, :], float(E - 1), None, ALU.min).then_inc(table_ready, 1)

            dve.wait_ge(gapt_done, 1)
            v.tensor_scalar(mix[:, 0, :], gap_t[:, :], 0.25, 0.25, ALU.mult, ALU.add).then_inc(mix_done, 1)
            v.tensor_scalar(mix[:, 1, :], gap_t[:, :], -0.25, 0.25, ALU.mult, ALU.add).then_inc(mix_done, 1)

            def unit_split(u, j):
                dve.wait_ge(u_hid, u + 1)
                if not (isinstance(u, int) and u < 2):
                    dve.wait_ge(u_y, u - 1)
                v.tensor_scalar(hid_h[j % 2][:, :], hid[j % 2][:, :], SH, None, ALU.mult).then_inc(u_hidh, 1)
                dve.wait_ge(u_hidh, u + 1)
                v.scalar_tensor_tensor(out=hid_l[j % 2][:, :], in0=hid[j % 2][:, :], scalar=SH, in1=hid_h[j % 2][:, :],
                                       op0=ALU.mult, op1=ALU.subtract).then_inc(u_hidl, 1)

            for j in range(RING):
                unit_split(j, j)
            with dve.Fori(1, UNITS // RING) as g:
                for j in range(RING):
                    unit_split(g * RING + j, j)

            def combine(c):
                dve.wait_ge(yl_in[c.par], c.half * 16 + 16)
                for t in range(TILES):
                    n = c.n * TILES + t
                    v.scalar_tensor_tensor(out=acc[c.par][:, t, :], in0=yl[c.par][:, t, 0:C], scalar=mix[:, 0, bass.ds(n, 1)],
                                           in1=base[:, bass.ds(n, 1), :].rearrange("p a d -> p (a d)"),
                                           op0=ALU.mult, op1=ALU.add).then_inc(acc_step, 1)
                for t in range(TILES):
                    n = c.n * TILES + t
                    dve.wait_ge(acc_step, c.n * (2 * TILES) + t + 1)
                    v.scalar_tensor_tensor(out=acc2[c.par][:, t, :], in0=yl[c.par][:, t, C:2 * C], scalar=mix[:, 1, bass.ds(n, 1)],
                                           in1=acc[c.par][:, t, :], op0=ALU.mult, op1=ALU.add).then_inc(acc_step, 1)
                dve.wait_ge(acc_step, (c.n + 1) * (2 * TILES))
                if not (isinstance(c.n, int) and c.n == 0):
                    dve.wait_ge(fin_done, c.n * TILES)
                stats(c, [acc2[c.par][:, t, :] for t in range(TILES)], EPS / 4, f_bst, f_mv, f_var)
                rsqrt(c, f_rs0, f_rs, f_norm)

            dve.wait_ge(mix_done, 2)
            combine(Chunk(0, 0))
            combine(Chunk(0, 1))
            with dve.Fori(1, CHUNKS // 2) as h:
                combine(Chunk(h, 0))
                combine(Chunk(h, 1))

        @block.gpsimd
        def _(pool):
            g_ = nc.gpsimd

            def scale_weights(c):
                s = stage[c.par][:, :]
                pool.wait_ge(stage_in[c.par], c.half * 16 + 16)
                g_.tensor_tensor(s, s, w_scale[:, :].to_broadcast([P, 2 * FF]), ALU.mult).then_inc(w_scaled, 1)

            def high_weights(c):
                pool.wait_ge(w_scaled, c.n + 1)
                g_.tensor_copy(rt_w[:, bass.ds(c.n, 1), 0, :].rearrange("p a n -> p (a n)"), stage[c.par][:, :]).then_inc(w_high, 1)

            def low_weights(c, i):
                part = slice(i * FF, (i + 1) * FF)
                high, low = (rt_w[:, bass.ds(c.n, 1), s, part].rearrange("p a n -> p (a n)") for s in range(2))
                pool.wait_ge(w_high, c.n + 1)
                g_.tensor_tensor(low, stage[c.par][:, part], high, ALU.subtract).then_inc(w_low, 1)

            def numerator_a(c):
                pool.wait_ge(p_done, c.n + 1)
                pool.wait_ge(exp_out, c.n + 1)
                g_.tensor_tensor(ap_[:, :], expd[:, 0, 1, :], state[c.par][:, 1, 0:CH], ALU.mult).then_inc(ap_done, 1)

            def numerator_b(c):
                pool.wait_ge(ap_done, c.n + 1)
                pool.wait_ge(bv_done, c.n + 1)
                g_.tensor_tensor(num[:, :], ap_[:, :], bv[:, :], ALU.add).then_inc(num_done, 1)

            def result_rows(c, k):
                if k == 0:
                    pool.wait_ge(rows_done, c.n + 1)
                    pool.wait_ge(slot_done, c.n + 1)
                    if not (isinstance(c.half, int) and c.half == 0):
                        pool.wait_ge(scattered[c.par], c.half * (TILES * TOP_K * 16))
                else:
                    pool.wait_ge(scattered[c.par], c.half * (TILES * TOP_K * 16) + TILES * 16)
                g_.tensor_copy(rows[c.par][:, :, 2 * C:ROW].bitcast(I32),
                               row_ids[:, bass.ds(c.n * TILES, TILES), k:k + 1]).then_inc(ids_done, 1)
                pool.wait_ge(ids_done, c.n * 2 + k + 1)

            def scatter(c, k):
                for t in range(TILES):
                    g_.indirect_dma_start(sorted_x, bass.IndirectOffsetOnAxis(ap=slot[c.par][:, k, t:t + 1].bitcast(U32), axis=0),
                                          rows[c.par][:, t, :], None).then_inc(scattered[c.par], 16)

            def step(c, q):
                if c is not None:
                    scale_weights(c)
                    high_weights(c)
                    numerator_a(c)
                    numerator_b(c)
                for k in range(TOP_K):
                    if q is not None:
                        result_rows(q, k)
                    if c is not None:
                        low_weights(c, k)
                    if q is not None:
                        scatter(q, k)

            pool.wait_ge(consts_in, 48)
            g_.memset(w_scale[:, :], SW).then_inc(scale_made, 1)
            pool.wait_ge(scale_made, 1)
            g_.memset(no_ids[:, :], 0).then_inc(scale_made, 1)
            g_.memset(pad[:, :, 0:2 * C], 0.0).then_inc(pad_made, 1)
            g_.memset(pad[:, :, 2 * C:ROW].bitcast(I32), TOKENS * TOP_K).then_inc(pad_made, 1)
            step(Chunk(0, 0), None)
            step(Chunk(0, 1), Chunk(0, 0))
            with pool.Fori(1, CHUNKS // 2) as h:
                step(Chunk(h, 0), Chunk(h - 1, 1))
                step(Chunk(h, 1), Chunk(h, 0))
            step(None, Chunk(CHUNKS // 2 - 1, 1))

            def unit_ids(u, g, j):
                pool.wait_ge(xs_in[j], g * 16 + 16)
                g_.tensor_tensor(unit_id[j][:, :], xs[j][:, :, 2 * C:ROW].bitcast(I32).rearrange("p k a -> p (k a)"),
                                 no_ids[:, :], ALU.add).then_inc(u_ids, 1)

            def put_results(j):
                for k in range(UH):
                    g_.indirect_dma_start(routed_y, bass.IndirectOffsetOnAxis(ap=unit_id[j][:, k:k + 1].bitcast(U32), axis=0),
                                          ys[j][:, k, :], None, bounds_check=TOKENS * TOP_K - 1,
                                          oob_is_err=False).then_inc(y_out[j], 16)

            unit_ids(0, 0, 0)
            for j in range(1, RING):
                pool.wait_ge(u_ids, j)
                pool.wait_ge(u_ys, j)
                unit_ids(j, 0, j)
                put_results(j - 1)
            with pool.Fori(1, UNITS // RING) as g:
                for j in range(RING):
                    u = g * RING + j
                    pool.wait_ge(u_ids, u)
                    pool.wait_ge(u_ys, u)
                    unit_ids(u, g, j)
                    put_results((j - 1) % RING)
            pool.wait_ge(u_ids, UNITS)
            pool.wait_ge(u_ys, UNITS)
            put_results(RING - 1)


PREP_ALL = 20


def kernel(**inputs):
    import numpy as _np
    import concourse.bacc as _bacc
    from concourse import mybir as _mybir
    from concourse.bass_utils import run_bass_kernel_spmd as _run

    a = {k: _np.asarray(x) for k, x in inputs.items()}
    x = a["L0_attn_x"]
    xT = _np.zeros((C, B, T + 1), _np.float32)
    xT[:, :, 1:] = x.transpose(2, 0, 1)
    w_att = _np.stack([a[f"L0_attn_W_{n}"].T for n in ("key", "value", "receptance", "output")], axis=1)
    vecs = _np.stack([a[f"L0_attn_time_{n}"].reshape(C) for n in ("decay", "first", "mix_k", "mix_v", "mix_r")], axis=1)

    def layers(fc, proj):
        n = fc.shape[0]
        one = fc.transpose(0, 2, 1)
        two = proj.reshape(n, C, FC, P).transpose(0, 3, 2, 1).reshape(n, P, FF)
        return _np.stack([one, two], axis=2)

    w_sh = layers(a["L0_ffn_Wfc_sh"], a["L0_ffn_Wproj_sh"]).transpose(1, 2, 0, 3).reshape(P, 2, SF * P)
    w_rt = layers(a["L0_ffn_Wfc_r"], a["L0_ffn_Wproj_r"]).reshape(E, P, 2 * FF)
    cent = a["L0_ffn_centroids"].T
    bias = _np.broadcast_to(a["L0_ffn_routing_bias"][None, None, :], (P, TILES, E)).reshape(P, TILES * E)
    kf = _np.zeros((P, K_END), _np.float32)
    kf[:, K_ID:K_ID + P] = _np.eye(P)
    kf[:, K_I8:K_I8 + TILES * E] = _np.tile(_np.arange(E), TILES)
    kf[:, K_EB:K_EB + E] = _np.arange(E) * CAP
    kf[:, K_EN:K_EN + E] = UT - 1 - _np.arange(E) * CAP
    kf[:, K_IU:K_IU + UNITS] = _np.arange(UNITS)
    kh = _np.concatenate([_np.eye(P), _np.triu(_np.ones((P, P)), 1), _np.ones((P, P))], axis=1).astype(_np.float16)
    token = _np.arange(NT)[None, :, None] * P + _np.arange(P)[:, None, None]
    kid = (token * TOP_K + _np.arange(TOP_K)[None, None, :]).astype(_np.int32)

    nc = _bacc.Bacc("TRN2", target_bir_lowering=False, num_devices=1)
    arrays, args = {}, []
    for name, arr in dict(xT=xT, w_att=w_att, vecs=vecs, w_sh=w_sh, w_rt=w_rt, cent=cent, bias=bias, kf=kf, kh=kh, kid=kid).items():
        arr = _np.ascontiguousarray(arr)
        arrays[f"in_{name}"] = arr
        args.append(nc.dram_tensor(f"in_{name}", arr.shape, _mybir.dt.from_np(arr.dtype), kind="ExternalInput").ap())
    args.append(nc.dram_tensor("out_0", (B, T, C), _mybir.dt.float32, kind="ExternalOutput").ap())
    build(nc, *args)
    r = _run(nc, [arrays], core_ids=[0])
    return r.results[0]["out_0"]
```

```python
from contextlib import ExitStack

import numpy as np
import concourse.bass as bass
from concourse import mybir

ALU = mybir.AluOpType
ACT = mybir.ActivationFunctionType
AX_X = mybir.AxisListType.X
F32 = mybir.dt.float32
F16 = mybir.dt.float16
I32 = mybir.dt.int32
U32 = mybir.dt.uint32

P = 128
B, T, C = 4, 1024, 128
TOKENS = B * T
CH = 512
TILES = CH // P
CHUNKS = TOKENS // CH
HALVES = T // CH
NT = TOKENS // P
E = 8
NS = 2
TOP_K = 2
FF = 512
FC = FF // P
SF = NS * FC
UT = 256
UH = UT // P
CAP = TOKENS + UT
ROW = 2 * C + 2
DUMP = E * CAP
UNITS = 4 * -(-((TOP_K * TOKENS + E * (UT - 1)) // UT) // 4)
RING = 4
EXPERT_BITS = E.bit_length() - 1
EPS = 1e-5
NEWTON = 3
SW = 64.0
SX = 64.0
SH = 16.0

K_ID, K_I8, K_EB, K_EN, K_IU, K_END = np.cumsum([0, P, TILES * E, E, E, UNITS]).tolist()


class Chunk:

    def __init__(self, half, par):
        self.half, self.par, self.n = half, par, half * 2 + par


LAST0, LAST1 = (Chunk(CHUNKS // 2 - 1, i) for i in range(2))


def build(nc, xT, w_att, vecs, w_sh, w_rt, cent, bias, kf, kh, kid, out):
    ctx = ExitStack()
    with ctx:
        def sb(name, shape, dt=F32):
            return ctx.enter_context(nc.sbuf_tensor(name, shape, dt))

        def sem(name):
            return ctx.enter_context(nc.semaphore(name))

        sorted_x = nc.dram_tensor("sorted_x", (DUMP + UT, ROW), F16, kind="Internal").ap()
        routed_y = nc.dram_tensor("routed_y", (TOKENS * TOP_K, C), F32, kind="Internal").ap()

        consts = sb("consts", [P, K_END])
        half_consts = sb("half_consts", [P, 3 * P], F16)
        row_ids = sb("row_ids", [P, NT, TOP_K], I32)
        ident = consts[:, K_ID:K_ID + P]
        iota8 = consts[:, K_I8:K_I8 + TILES * E]
        iota_u = consts[:, K_IU:K_IU + UNITS]
        ident_h = half_consts[:, 0:P]
        before = half_consts[:, P:2 * P]
        ones_h = half_consts[:, 2 * P:3 * P]
        vec = sb("vec", [P, 5])
        att_raw = sb("att_raw", [P, 4, C])
        one_minus = sb("one_minus", [P, 3])
        att_w = sb("att_w", [P, 3, 2, C])
        decay = sb("decay", [P, 1])
        neg_w = sb("neg_w", [P, 1])
        w_row = sb("w_row", [P, CH])
        sh_raw = sb("sh_raw", [P, 2, SF * P])
        sh_w = sb("sh_w", [P, 2, SF * P], F16)
        cent_raw = sb("cent_raw", [P, E])
        cent_w = sb("cent_w", [P, 2, E], F16)
        bias_row = sb("bias_row", [P, TILES * E])
        stage = [sb(f"stage{i}", [P, 2 * FF]) for i in range(2)]
        rt_w = sb("rt_w", [P, E, 2, 2 * FF], F16)
        xt = [sb(f"xt{i}", [P, CH + 1]) for i in range(2)]
        state = [sb(f"state{i}", [P, 3, CH + 1]) for i in range(2)]
        diff = sb("diff", [P, 2, CH])
        relu = sb("relu", [P, 2, 2, CH])
        expd = sb("expd", [P, 2, 2, CH])
        b2v = sb("b2v", [P, CH])
        bv = sb("bv", [P, CH])
        ap_ = sb("ap_", [P, CH])
        num = sb("num", [P, CH])
        aq = sb("aq", [P, CH])
        den = sb("den", [P, CH])
        exp_r = sb("exp_r", [P, CH])
        both = sb("both", [P, CH])
        inverse = sb("inverse", [P, CH])
        gated = sb("gated", [P, CH])
        bst = sb("bst", [P, TILES, 6])
        ln_m = sb("ln_m", [P, TILES])
        ln_d = sb("ln_d", [P, TILES])
        ln_s = sb("ln_s", [P, TILES])
        ln_q = sb("ln_q", [P, TILES])
        ln_e = sb("ln_e", [P, TILES])
        var_e = sb("var_e", [P, TILES])
        half_bits = sb("half_bits", [P, TILES], I32)
        root = sb("root", [P, TILES])
        rs_y = sb("rs_y", [P, TILES])
        rs_a = sb("rs_a", [P, TILES])
        rs_b = sb("rs_b", [P, TILES])
        rstd = sb("rstd", [P, TILES])
        shift = sb("shift", [P, TILES])
        x1 = [sb(f"x1_{i}", [P, TILES, C]) for i in range(2)]
        base = sb("base", [P, NT, C])
        rows = [sb(f"rows{i}", [P, TILES, ROW], F16) for i in range(2)]
        x1t = [sb(f"x1t{i}", [P, 2, CH], F16) for i in range(2)]
        logits = sb("logits", [P, 2, TILES * E])
        exps_l = sb("exps_l", [P, 2, TILES * E])
        exps_1 = sb("exps_1", [P, 2, TILES * E])
        scores = sb("scores", [P, 2, TILES * E])
        top = sb("top", [P, TILES, 8])
        top_i = sb("top_i", [P, TILES, 8], U32)
        top_f = sb("top_f", [P, TOP_K, TILES])
        hot = sb("hot", [P, TOP_K, TILES * E])
        chosen = sb("chosen", [P, TILES * E], F16)
        hot_s = sb("hot_s", [P, TOP_K, TILES * E])
        got = sb("got", [P, TOP_K, TILES])
        gap = sb("gap", [P, NT])
        gap_e = sb("gap_e", [P, NT])
        gap_1 = sb("gap_1", [P, NT])
        gap_r = sb("gap_r", [P, NT])
        mix = sb("mix", [P, TOP_K, NT])
        slot_e = sb("slot_e", [P, TILES * E])
        taken = sb("taken", [P, E])
        hot_r = sb("hot_r", [P, TOP_K, TILES * E])
        slot_f = sb("slot_f", [P, TOP_K, TILES])
        slot = [sb(f"slot{i}", [P, TOP_K, TILES], I32) for i in range(2)]
        cnt_f = sb("cnt_f", [P, E])
        cnt_i = sb("cnt_i", [P, E], I32)
        tile_i = sb("tile_i", [P, E], I32)
        tile_f = sb("tile_f", [P, E])
        ones8 = sb("ones8", [P, E])
        cum = sb("cum", [P, E])
        past = sb("past", [P, UNITS, E])
        past_c = sb("past_c", [P, UNITS, E])
        unit_e = sb("unit_e", [P, UNITS])
        unit_s = sb("unit_s", [P, UNITS])
        unit_j = sb("unit_j", [P, UNITS])
        unit_r = sb("unit_r", [P, UNITS])
        unit_r2 = sb("unit_r2", [P, UNITS])
        unit_row = sb("unit_row", [P, UNITS], I32)
        unit_w = sb("unit_w", [P, UNITS + RING])
        unit_w2 = sb("unit_w2", [P, UNITS + 2])
        unit_w4 = sb("unit_w4", [P, UNITS])
        unit_w5 = sb("unit_w5", [P, UNITS], I32)
        end_row = sb("end_row", [P, E], I32)
        pad = sb("pad", [P, UH, ROW], F16)
        xs = [sb(f"xs{i}", [P, UH, ROW], F16) for i in range(RING)]
        ys = [sb(f"ys{i}", [P, UH, C]) for i in range(RING)]
        unit_id = [sb(f"unit_id{i}", [P, UH], I32) for i in range(RING)]
        waiter = sb("waiter", [P, 3, UH], I32)
        no_ids = sb("no_ids", [P, UH], I32)
        hid = [sb(f"hid{i}", [P, FC * UT]) for i in range(2)]
        hid_h = [sb(f"hid_h{i}", [P, FC * UT], F16) for i in range(2)]
        hid_l = [sb(f"hid_l{i}", [P, FC * UT], F16) for i in range(2)]
        yl = rt_w.rearrange("p e s n -> p (e s n)").bitcast(F32).rearrange("p (n d) -> p n d", d=TOP_K * C)
        weighted = [sb(f"weighted{i}", [P, TILES, C]) for i in range(2)]
        acc = [sb(f"acc{i}", [P, TILES, C]) for i in range(2)]
        acc2 = [sb(f"acc2{i}", [P, TILES, C]) for i in range(2)]
        fin = [sb(f"fin{i}", [P, TILES, C]) for i in range(2)]

        ps = ctx.enter_context(nc.psum_tensor("ps", [P, 8, 512], F32))
        K, V, R, ATT = (ps[:, i, :] for i in range(4))
        HID = [hid[i // 2][:, i % 2 * CH:(i % 2 + 1) * CH] for i in range(4)]
        TR = ps[:, 4, :].bitcast(F16).rearrange("p (s n) -> p s n", s=2)
        FCB = [ps[:, 5 + i, :] for i in range(2)]
        Y = ps[:, 7, :]
        LOGIT = ps[:, 3, 0:TILES * E]
        RANK = ps[:, 2, 64:64 + TILES * E]
        TOTAL = ps[:, 2, 128:128 + E]
        FCU = [ps[:, 2 * i:2 * i + 2, :].rearrange("p b n -> p (b n)") for i in range(2)]
        TRU = [ps[:, 4 + i, 0:UT].bitcast(F16).rearrange("p (s n) -> p s n", s=2) for i in range(2)]
        YU = [ps[:, 6 + i, 0:UH * C] for i in range(2)]

        consts_in = sem("consts_in")
        att_in = sem("att_in")
        shared_in = sem("shared_in")
        stage_in = [sem(f"stage_in{i}") for i in range(2)]
        xt_in = [sem(f"xt_in{i}") for i in range(2)]
        decay_done = sem("decay_done")
        prep = sem("prep")
        w_high = sem("w_high")
        w_low = sem("w_low")
        ids_made = sem("ids_made")
        pad_made = sem("pad_made")
        pads_out = sem("pads_out")
        k_ready, v_ready, r_ready = sem("k_ready"), sem("v_ready"), sem("r_ready")
        carried = sem("carried")
        o_done, p_done, q_done = sem("o_done"), sem("p_done"), sem("q_done")
        diff_done = sem("diff_done")
        relu_done = sem("relu_done")
        exp_state = sem("exp_state")
        exp_out = sem("exp_out")
        b2v_done = sem("b2v_done")
        bv_done = sem("bv_done")
        ap_done = sem("ap_done")
        num_done = sem("num_done")
        aq_done = sem("aq_done")
        den_done = sem("den_done")
        both_done = sem("both_done")
        inverse_done = sem("inverse_done")
        gate_done = sem("gate_done")
        gated_done = sem("gated_done")
        att_ready = sem("att_ready")
        bst_done = sem("bst_done")
        mv_done = sem("mv_done")
        var_done = sem("var_done")
        rs_step = sem("rs_step")
        norm_done = sem("norm_done")
        x1_done = sem("x1_done")
        high_done = sem("high_done")
        rows_done = sem("rows_done")
        turned = sem("turned")
        x1t_done = sem("x1t_done")
        logit_ready = sem("logit_ready")
        logits_done = sem("logits_done")
        expl_done = sem("expl_done")
        exp1_done = sem("exp1_done")
        scores_done = sem("scores_done")
        top_done = sem("top_done")
        topi_done = sem("topi_done")
        topf_done = sem("topf_done")
        hot_done = sem("hot_done")
        chosen_done = sem("chosen_done")
        hots_done = sem("hots_done")
        got_done = sem("got_done")
        gap_done = sem("gap_done")
        rank_ready = sem("rank_ready")
        slote_done = sem("slote_done")
        taken_done = sem("taken_done")
        hotr_done = sem("hotr_done")
        slotf_done = sem("slotf_done")
        slot_done = sem("slot_done")
        ids_done = sem("ids_done")
        scattered = [sem(f"scattered{i}") for i in range(2)]
        fc_ready = sem("fc_ready")
        hid_done = sem("hid_done")
        proj_done = sem("proj_done")
        base_done = sem("base_done")
        table = sem("table")
        ends_ready = sem("ends_ready")
        table_ready = sem("table_ready")
        xs_in = [sem(f"xs_in{i}") for i in range(RING)]
        u_ids = sem("u_ids")
        u_turned = sem("u_turned")
        u_xt = sem("u_xt")
        u_fc = sem("u_fc")
        u_hid = sem("u_hid")
        u_hidh = sem("u_hidh")
        u_hidl = sem("u_hidl")
        u_y = sem("u_y")
        u_ys = sem("u_ys")
        y_out = [sem(f"y_out{i}") for i in range(RING)]
        gapt_done = sem("gapt_done")
        mix_step = sem("mix_step")
        mix_done = sem("mix_done")
        yl_in = [sem(f"yl_in{i}") for i in range(2)]
        weighted_done = sem("weighted_done")
        acc_done = sem("acc_done")
        acc2_done = sem("acc2_done")
        f_root = sem("f_root")
        f_rs = sem("f_rs")
        f_bst = sem("f_bst")
        f_mv = sem("f_mv")
        f_var = sem("f_var")
        f_norm = sem("f_norm")
        fin_done = sem("fin_done")
        stored = [sem(f"stored{i}") for i in range(2)]

        block = ctx.enter_context(nc.Block())

        out_v = out.rearrange("b (h t p) d -> (b h) p t d", p=P, t=TILES)
        yl_v = routed_y.rearrange("(c t p k) d -> c p t (k d)", p=P, t=TILES, k=TOP_K)

        @block.sync
        def _(sp):
            def load_chunk(c):
                first = isinstance(c.half, int) and c.half == 0
                if not first:
                    sp.wait_ge(att_ready, c.n - 1)
                src = xT[:, bass.ds(c.half, 1), c.par * CH:c.par * CH + CH + 1]
                sp.dma_start(xt[c.par][:, :], src.rearrange("p a n -> p (a n)")).then_inc(xt_in[c.par], 16)
                if not first:
                    sp.wait_ge(w_low, c.n - 1)
                sp.dma_start(stage[c.par][:, :],
                             w_rt[bass.ds(c.n, 1), :, :].rearrange("a p n -> (a p) n")).then_inc(stage_in[c.par], 16)

            sp.dma_start(att_raw[:, :, :], w_att).then_inc(att_in, 16)
            sp.dma_start(vec[:, :], vecs).then_inc(att_in, 16)
            load_chunk(Chunk(0, 0))
            sp.dma_start(consts[:, :], kf).then_inc(consts_in, 16)
            sp.dma_start(half_consts[:, :], kh).then_inc(consts_in, 16)
            sp.dma_start(row_ids[:, :, :], kid).then_inc(consts_in, 16)
            sp.dma_start(cent_raw[:, :], cent).then_inc(shared_in, 16)
            sp.dma_start(bias_row[:, :], bias).then_inc(shared_in, 16)
            sp.dma_start(sh_raw[:, :, :], w_sh).then_inc(shared_in, 16)
            load_chunk(Chunk(0, 1))
            sp.wait_ge(pad_made, 2)
            sp.dma_start(sorted_x[DUMP:DUMP + UT, :].rearrange("(j p) w -> p j w", p=P), pad[:, :, :]).then_inc(pads_out, 16)
            with sp.Fori(1, CHUNKS // 2) as h:
                load_chunk(Chunk(h, 0))
                load_chunk(Chunk(h, 1))

            sp.wait_ge(ends_ready, 1)
            ends = nc.values_load_multi_w_load_instructions(end_row[0:1, 0:E], engines=[mybir.EngineType.SP], min_val=0, max_val=DUMP)[1]
            for r in ends:
                sp.dma_start(sorted_x[bass.ds(r, UT), :].rearrange("(j p) w -> p j w", p=P),
                             pad[:, :, :]).then_inc(pads_out, 16)

            def load_unit(u, g, j):
                r = sp.value_load(unit_row[0:1, bass.ds(u, 1)], min_val=0, max_val=DUMP)
                if not (isinstance(g, int) and g == 0):
                    sp.wait_ge(u_turned, u - RING + 1)
                    sp.wait_ge(u_ids, u - RING + 1)
                sp.dma_start(xs[j][:, :, :], sorted_x[bass.ds(r, UT), :].rearrange("(j p) w -> p j w", p=P)).then_inc(xs_in[j], 16)

            sp.wait_ge(pads_out, 16 * (E + 1))
            for i in range(2):
                sp.wait_ge(scattered[i], CHUNKS // 2 * TILES * TOP_K * 16)
            sp.wait_ge(table_ready, 1)
            for j in range(RING):
                load_unit(j, 0, j)
            with sp.Fori(1, UNITS // RING) as g:
                for j in range(RING):
                    load_unit(g * RING + j, g, j)

            def load_results(c):
                if not (isinstance(c.half, int) and c.half == 0):
                    sp.wait_ge(yl_in[c.par], c.half * 16)
                sp.dma_start(yl[:, bass.ds(c.n * TILES, TILES), :],
                             yl_v[bass.ds(c.n, 1)].rearrange("a p t n -> (a p) t n")).then_inc(yl_in[c.par], 16)

            for j in range(RING):
                sp.wait_ge(y_out[j], UNITS // RING * 16 * UH)
            load_results(Chunk(0, 0))
            load_results(Chunk(0, 1))
            with sp.Fori(1, CHUNKS // 2) as h:
                load_results(Chunk(h, 0))
                load_results(Chunk(h, 1))

        @block.tensor
        def _(pe):
            def mix_x(c, i, bank, ready):
                nc.tensor.matmul(bank, att_w[:, i, 0, :], xt[c.par][:, 1:CH + 1], start=True, stop=False)
                nc.tensor.matmul(bank, att_w[:, i, 1, :], xt[c.par][:, 0:CH], start=False, stop=True).then_inc(ready, 1)

            def turn(c):
                pe.wait_ge(rows_done, c.n + 1)
                for s in range(2):
                    for t in range(TILES):
                        mm = nc.tensor.transpose(TR[:, s, t * P:(t + 1) * P], rows[c.par][:, t, s * C:(s + 1) * C], ident_h)
                mm.then_inc(turned, 1)

            def route(c):
                pe.wait_ge(x1t_done, c.n + 1)
                for t in range(TILES):
                    for i, (s, w) in enumerate(((0, 0), (0, 1), (1, 0))):
                        mm = nc.tensor.matmul(LOGIT[:, t * E:(t + 1) * E], x1t[c.par][:, s, t * P:(t + 1) * P], cent_w[:, w, :],
                                              start=(t == 0 and i == 0), stop=(i == 2), skip_group_check=True)
                mm.then_inc(logit_ready, 1)

            def rank(c):
                pe.wait_ge(chosen_done, c.n + 1)
                for t in range(TILES):
                    for s in range(t + 1):
                        nc.tensor.matmul(RANK[:, t * E:(t + 1) * E], before if s == t else ones_h, chosen[:, s * E:(s + 1) * E],
                                         start=(t == 0), stop=(s == t), skip_group_check=True)
                for s in range(TILES):
                    mm = nc.tensor.matmul(TOTAL, ones_h, chosen[:, s * E:(s + 1) * E], start=False, stop=(s == TILES - 1),
                                          skip_group_check=True)
                mm.then_inc(rank_ready, 1)

            def shared_fc(c, f):
                n = c.n * SF + f
                if not (isinstance(n, int) and n < 2):
                    pe.wait_ge(hid_done, n - 1)
                for i, (w, s) in enumerate(((0, 0), (0, 1), (1, 0))):
                    mm = nc.tensor.matmul(FCB[f % 2], sh_w[:, w, f * P:(f + 1) * P], x1t[c.par][:, s, :],
                                          start=(i == 0), stop=(i == 2))
                mm.then_inc(fc_ready, 1)

            def shared_proj(c, f):
                if f == 0 and not (isinstance(c.n, int) and c.n == 0):
                    pe.wait_ge(base_done, c.n)
                pe.wait_ge(hid_done, c.n * SF + f + 1)
                for t in range(TILES):
                    mm = nc.tensor.matmul(Y[:, t * C:(t + 1) * C], HID[f % 4][:, t * P:(t + 1) * P], sh_raw[:, 1, f * P:(f + 1) * P],
                                          start=(f == 0 and t == 0), stop=(f == SF - 1), skip_group_check=True)
                mm.then_inc(proj_done, 1)

            def attend_out(c):
                pe.wait_ge(gated_done, c.n + 1)
                for t in range(TILES):
                    o = ATT[:, t * P:(t + 1) * P]
                    nc.tensor.matmul(o, gated[:, t * P:(t + 1) * P], att_raw[:, 3, :], start=(t == 0), stop=False, skip_group_check=True)
                    mm = nc.tensor.matmul(o, xt[c.par][:, 1 + t * P:1 + (t + 1) * P], ident, start=False, stop=True,
                                          skip_group_check=True)
                mm.then_inc(att_ready, 1)

            def step(c, q, n):
                if q is not None:
                    route(q)
                for f in range(SF + 1):
                    if q is not None and f < SF:
                        shared_fc(q, f)
                    if f == 1 and n is not None:
                        mix_k(n)
                    if q is not None:
                        if f > 0:
                            shared_proj(q, f - 1)
                        if f == (4 if c is not None else 1):
                            rank(q)
                    if f == 5 and c is not None:
                        attend_out(c)
                if n is not None:
                    mix_x(n, 1, V, v_ready)
                if c is not None:
                    turn(c)
                if n is not None:
                    if q is not None:
                        pe.wait_ge(taken_done, q.n + 1)
                    mix_x(n, 2, R, r_ready)

            def mix_k(c):
                pe.wait_ge(xt_in[c.par], c.half * 16 + 16)
                if not (isinstance(c.n, int) and c.n == 0):
                    pe.wait_ge(diff_done, c.n * 2)
                mix_x(c, 0, K, k_ready)

            pe.wait_ge(prep, PREP_K)
            mix_k(Chunk(0, 0))
            pe.wait_ge(prep, PREP_MIX)
            mix_x(Chunk(0, 0), 2, R, r_ready)
            mix_x(Chunk(0, 0), 1, V, v_ready)
            pe.wait_ge(consts_in, 48)
            step(Chunk(0, 0), None, Chunk(0, 1))
            pe.wait_ge(prep, PREP_ALL)
            pe.wait_ge(shared_in, 48)
            step(Chunk(0, 1), Chunk(0, 0), Chunk(1, 0))
            with pe.Fori(1, CHUNKS // 2 - 1) as h:
                step(Chunk(h, 0), Chunk(h - 1, 1), Chunk(h, 1))
                step(Chunk(h, 1), Chunk(h, 0), Chunk(h + 1, 0))
            step(LAST0, Chunk(CHUNKS // 2 - 2, 1), LAST1)
            step(LAST1, LAST0, None)
            step(None, LAST1, None)

            def unit_turn(u, g, j):
                pe.wait_ge(xs_in[j], g * 16 + 16)
                if not (isinstance(u, int) and u < 2):
                    pe.wait_ge(u_xt, u - 1)
                for s in range(2):
                    for k in range(UH):
                        mm = nc.tensor.transpose(TRU[j % 2][:, s, k * P:(k + 1) * P], xs[j][:, k, s * C:(s + 1) * C], ident_h)
                mm.then_inc(u_turned, 1)

            def experts_of(u):
                packed = pe.value_load(unit_w5[0:1, bass.ds(u, 1)], min_val=0, max_val=E ** (RING + 1) - 1)
                return [(packed >> (EXPERT_BITS * i)) & (E - 1) for i in range(RING + 1)]

            def unit_fc(u, j, e):
                w = [rt_w[:, bass.ds(e, 1), s, 0:FF].rearrange("p a n -> p (a n)") for s in range(2)]
                pe.wait_ge(u_xt, u + 1)
                for f in range(FC):
                    if f % 2 == 0 and not (isinstance(u, int) and u < 2):
                        pe.wait_ge(u_hid, u * 2 - 3 + f // 2)
                    for i, (a, s) in enumerate(((0, 0), (0, 1), (1, 0))):
                        mm = nc.tensor.matmul(FCU[j % 2][:, f * UT:(f + 1) * UT], w[a][:, f * P:(f + 1) * P], x1t[j % 2][:, s, 0:UT],
                                              start=(f % 2 == 0 and i == 0), stop=(i == 2), skip_group_check=True)
                    if f % 2 == 1:
                        mm.then_inc(u_fc, 1)

            def unit_proj(u, j, e):
                w = [rt_w[:, bass.ds(e, 1), s, FF:2 * FF].rearrange("p a n -> p (a n)") for s in range(2)]
                if not (isinstance(u, int) and u < 2):
                    pe.wait_ge(u_ys, u - 1)
                for f in range(FC):
                    if f % 2 == 0:
                        pe.wait_ge(u_hidl, u * 2 + 1 + f // 2)
                    for k in range(UH):
                        h = [x[j % 2][:, f * UT + k * P:f * UT + (k + 1) * P] for x in (hid_h, hid_l)]
                        for i, (s, a) in enumerate(((0, 0), (0, 1), (1, 0))):
                            mm = nc.tensor.matmul(YU[j % 2][:, k * C:(k + 1) * C], h[s], w[a][:, f * P:(f + 1) * P],
                                                  start=(f == 0 and k == 0 and i == 0), stop=(f == FC - 1 and i == 2),
                                                  skip_group_check=True)
                mm.then_inc(u_y, 1)

            pe.wait_ge(base_done, CHUNKS)
            pe.wait_ge(taken_done, CHUNKS)
            pe.wait_ge(w_low, E)
            pe.wait_ge(table_ready, 1)
            first = experts_of(0)
            unit_turn(0, 0, 0)
            for j in range(RING - 1):
                unit_turn(j + 1, 0, j + 1)
                unit_fc(j, j, first[j])
                if j > 0:
                    unit_proj(j - 1, j - 1, first[j - 1])
            with pe.Fori(1, UNITS // RING) as g:
                e = experts_of(g * RING - 2)
                for j in range(RING):
                    u = g * RING + j
                    unit_turn(u, g, j)
                    unit_fc(u - 1, (j - 1) % RING, e[j + 1])
                    unit_proj(u - 2, (j - 2) % RING, e[j])
            last = experts_of(UNITS - 2)
            unit_fc(UNITS - 1, RING - 1, last[1])
            unit_proj(UNITS - 2, RING - 2, last[0])
            unit_proj(UNITS - 1, RING - 1, last[1])

        @block.scalar
        def _(act):
            def relus(c):
                act.wait_ge(diff_done, c.n * 2 + 2)
                nc.scalar.activation(relu[:, 0, :, :], diff[:, :, :], ACT.Relu).then_inc(relu_done, 1)
                nc.scalar.activation(relu[:, 1, :, :], diff[:, :, :], ACT.Relu, scale=-1.0).then_inc(relu_done, 1)

            def exps(c):
                act.wait_ge(relu_done, c.n * 2 + 2)
                nc.scalar.activation(expd[:, :, 0, :], relu[:, :, 0, :], ACT.Exp, scale=-1.0).then_inc(exp_state, 1)
                nc.scalar.activation(expd[:, :, 1, :], relu[:, :, 1, :], ACT.Exp, scale=-1.0).then_inc(exp_out, 1)

            def gates(c):
                act.wait_ge(r_ready, c.n + 1)
                nc.scalar.activation(exp_r[:, :], R, ACT.Exp, scale=-1.0).then_inc(gate_done, 1)

            def high_weights(c):
                act.wait_ge(stage_in[c.par], c.half * 16 + 16)
                nc.scalar.activation(rt_w[:, bass.ds(c.n, 1), 0, :].rearrange("p a n -> p (a n)"), stage[c.par][:, :],
                                     ACT.Copy, scale=SW).then_inc(w_high, 1)

            def normalise(c):
                act.wait_ge(norm_done, c.n * 2 + 2)
                for t in range(TILES):
                    nc.scalar.activation(x1[c.par][:, t, :], ATT[:, t * P:(t + 1) * P], ACT.Identity,
                                         bias=shift[:, t:t + 1], scale=rstd[:, t:t + 1]).then_inc(x1_done, 1)

            def copy_turned(c):
                act.wait_ge(turned, c.n + 1)
                nc.scalar.activation(x1t[c.par][:, :, :], TR, ACT.Copy).then_inc(x1t_done, 1)

            def squash(c):
                act.wait_ge(logits_done, c.n * 2 + 2)
                nc.scalar.activation(exps_l[:, :, :], logits[:, :, :], ACT.Exp, scale=-1.0).then_inc(expl_done, 1)

            def shared_gelu(c, f):
                n = c.n * SF + f
                act.wait_ge(fc_ready, n + 1)
                if not (isinstance(n, int) and n < 4):
                    act.wait_ge(proj_done, n - 3)
                nc.scalar.activation(HID[f % 4], FCB[f % 2], ACT.Gelu, scale=1.0 / (SW * SX)).then_inc(hid_done, 1)

            def step(c, q, n):
                if q is not None:
                    squash(q)
                    shared_gelu(q, 0)
                    shared_gelu(q, 1)
                if c is not None:
                    high_weights(c)
                if q is not None:
                    for f in range(2, SF - 1):
                        shared_gelu(q, f)
                if n is not None:
                    relus(n)
                if q is not None:
                    shared_gelu(q, SF - 1)
                if c is not None:
                    normalise(c)
                if n is not None:
                    exps(n)
                if c is not None:
                    copy_turned(c)
                if n is not None:
                    gates(n)

            act.wait_ge(att_in, 32)
            nc.scalar.activation(decay[:, :], vec[:, 0:1], ACT.Exp).then_inc(decay_done, 1)
            relus(Chunk(0, 0))
            exps(Chunk(0, 0))
            gates(Chunk(0, 0))
            step(Chunk(0, 0), None, Chunk(0, 1))
            step(Chunk(0, 1), Chunk(0, 0), Chunk(1, 0))
            with act.Fori(1, CHUNKS // 2 - 1) as h:
                step(Chunk(h, 0), Chunk(h - 1, 1), Chunk(h, 1))
                step(Chunk(h, 1), Chunk(h, 0), Chunk(h + 1, 0))
            step(LAST0, Chunk(CHUNKS // 2 - 2, 1), LAST1)
            step(LAST1, LAST0, None)
            step(None, LAST1, None)
            act.wait_ge(gap_done, CHUNKS)
            nc.scalar.activation(gap_e[:, :], gap[:, :], ACT.Exp, scale=-1.0).then_inc(gapt_done, 1)

            def unit_xt(u, j):
                act.wait_ge(u_turned, u + 1)
                if not (isinstance(u, int) and u < 2):
                    act.wait_ge(u_fc, u * 2 - 2)
                nc.scalar.activation(x1t[j % 2][:, :, 0:UT], TRU[j % 2], ACT.Copy).then_inc(u_xt, 1)

            def unit_gelu(u, j):
                for h in range(2):
                    part = slice(h * 2 * UT, (h + 1) * 2 * UT)
                    act.wait_ge(u_fc, u * 2 + 1 + h)
                    if not (isinstance(u, int) and u < 2):
                        act.wait_ge(u_hidl, u * 2 - 3 + h)
                    nc.scalar.activation(hid[j % 2][:, part], FCU[j % 2][:, part], ACT.Gelu, scale=1.0 / (SW * SX)).then_inc(u_hid, 1)

            def unit_y(u, g, j):
                act.wait_ge(u_y, u + 1)
                if not (isinstance(g, int) and g == 0):
                    act.wait_ge(y_out[j], g * (16 * UH))
                nc.scalar.activation(ys[j][:, :, :], YU[j % 2], ACT.Copy, scale=1.0 / (SW * SH)).then_inc(u_ys, 1)

            act.wait_ge(hid_done, CHUNKS * SF)
            act.wait_ge(proj_done, CHUNKS * SF)
            unit_xt(0, 0)
            for j in range(RING - 1):
                unit_xt(j + 1, j + 1)
                unit_gelu(j, j)
                if j > 0:
                    unit_y(j - 1, 0, j - 1)
            with act.Fori(1, UNITS // RING) as g:
                for j in range(RING):
                    u = g * RING + j
                    unit_xt(u, j)
                    unit_gelu(u - 1, (j - 1) % RING)
                    unit_y(u - 2, g - 1 if j < 2 else g, (j - 2) % RING)
            unit_gelu(UNITS - 1, RING - 1)
            unit_y(UNITS - 2, UNITS // RING - 1, RING - 2)
            unit_y(UNITS - 1, UNITS // RING - 1, RING - 1)

            def roots(c):
                act.wait_ge(f_var, c.n + 1)
                nc.scalar.activation(root[:, :], var_e[:, :], ACT.Sqrt).then_inc(f_root, 1)

            def finish(c):
                act.wait_ge(f_norm, c.n * 2 + 2)
                if not (isinstance(c.half, int) and c.half == 0):
                    act.wait_ge(stored[c.par], c.half * 16)
                for t in range(TILES):
                    nc.scalar.activation(fin[c.par][:, t, :], acc2[c.par][:, t, :], ACT.Identity,
                                         bias=shift[:, t:t + 1], scale=rstd[:, t:t + 1]).then_inc(fin_done, 1)
                act.wait_ge(fin_done, c.n * TILES + TILES)
                act.dma_start(out_v[bass.ds(c.n, 1)].rearrange("a p t n -> (a p) t n"), fin[c.par][:, :, :]).then_inc(stored[c.par], 16)

            roots(Chunk(0, 0))
            finish(Chunk(0, 0))
            roots(Chunk(0, 1))
            with act.Fori(1, CHUNKS // 2) as h:
                finish(Chunk(h - 1, 1))
                roots(Chunk(h, 0))
                finish(Chunk(h, 0))
                roots(Chunk(h, 1))
            finish(LAST1)
            for i in range(2):
                act.wait_ge(stored[i], CHUNKS // 2 * 16)

        @block.vector
        def _(dve):
            v = nc.vector

            def per_tile(x):
                return x.rearrange("p (t e) -> p t e", e=E)

            def scan_max(c):
                S = state[c.par]
                if c.par == 1:
                    dve.wait_ge(q_done, c.n)
                    v.tensor_copy(S[:, :, 0:1], state[0][:, :, CH:CH + 1]).then_inc(carried, 1)
                    dve.wait_ge(carried, c.half + 1)
                dve.wait_ge(k_ready, c.n + 1)
                v.tensor_tensor_scan(S[:, 0, 1:CH + 1], w_row[:, :], K, S[:, 0, 0:1], ALU.add, ALU.max).then_inc(o_done, 1)
                dve.wait_ge(o_done, c.n + 1)
                v.scalar_tensor_tensor(out=diff[:, 0, :], in0=S[:, 0, 0:CH], scalar=neg_w[:, 0:1], in1=K,
                                       op0=ALU.add, op1=ALU.subtract).then_inc(diff_done, 1)
                v.scalar_tensor_tensor(out=diff[:, 1, :], in0=K, scalar=vec[:, 1:2], in1=S[:, 0, 0:CH],
                                       op0=ALU.add, op1=ALU.subtract).then_inc(diff_done, 1)

            def values(c):
                dve.wait_ge(v_ready, c.n + 1)
                dve.wait_ge(exp_state, c.n + 1)
                v.tensor_tensor(b2v[:, :], V, expd[:, 0, 0, :], ALU.mult).then_inc(b2v_done, 1)
                dve.wait_ge(exp_out, c.n + 1)
                v.tensor_tensor(bv[:, :], V, expd[:, 1, 1, :], ALU.mult).then_inc(bv_done, 1)

            def scan_p(c):
                S = state[c.par]
                dve.wait_ge(b2v_done, c.n + 1)
                v.tensor_tensor_scan(S[:, 1, 1:CH + 1], expd[:, 1, 0, :], b2v[:, :], S[:, 1, 0:1], ALU.mult, ALU.add).then_inc(p_done, 1)

            def scan_q(c):
                S = state[c.par]
                v.tensor_tensor_scan(S[:, 2, 1:CH + 1], expd[:, 1, 0, :], expd[:, 0, 0, :], S[:, 2, 0:1], ALU.mult, ALU.add).then_inc(q_done, 1)

            def denominators(c):
                dve.wait_ge(q_done, c.n + 1)
                v.tensor_tensor(aq[:, :], state[c.par][:, 2, 0:CH], expd[:, 0, 1, :], ALU.mult).then_inc(aq_done, 1)
                dve.wait_ge(aq_done, c.n + 1)
                v.tensor_tensor(den[:, :], aq[:, :], expd[:, 1, 1, :], ALU.add).then_inc(den_done, 1)

            def invert(c):
                dve.wait_ge(gate_done, c.n + 1)
                dve.wait_ge(den_done, c.n + 1)
                v.scalar_tensor_tensor(out=both[:, :], in0=exp_r[:, :], scalar=1.0, in1=den[:, :],
                                       op0=ALU.add, op1=ALU.mult).then_inc(both_done, 1)
                dve.wait_ge(both_done, c.n + 1)
                v.reciprocal(inverse[:, :], both[:, :]).then_inc(inverse_done, 1)

            def gated_out(c):
                dve.wait_ge(num_done, c.n + 1)
                dve.wait_ge(inverse_done, c.n + 1)
                v.tensor_tensor(gated[:, :], num[:, :], inverse[:, :], ALU.mult).then_inc(gated_done, 1)

            def stats(c, src, eps, bst_s, mv_s, var_s):
                for t in range(TILES):
                    v.bn_stats(bst[:, t, :], src[t]).then_inc(bst_s, 1)
                dve.wait_ge(bst_s, c.n * TILES + TILES)
                v.tensor_tensor(ln_d[:, :], bst[:, :, 1], bst[:, :, 4], ALU.subtract).then_inc(mv_s, 1)
                v.tensor_tensor(ln_s[:, :], bst[:, :, 2], bst[:, :, 5], ALU.add).then_inc(mv_s, 1)
                v.tensor_tensor(ln_m[:, :], bst[:, :, 1], bst[:, :, 4], ALU.add).then_inc(mv_s, 1)
                dve.wait_ge(mv_s, c.n * 5 + 1)
                v.tensor_tensor(ln_q[:, :], ln_d[:, :], ln_d[:, :], ALU.mult).then_inc(mv_s, 1)
                dve.wait_ge(mv_s, c.n * 5 + 2)
                v.tensor_scalar(ln_e[:, :], ln_s[:, :], 1.0 / C, eps, ALU.mult, ALU.add).then_inc(mv_s, 1)
                dve.wait_ge(mv_s, c.n * 5 + 5)
                v.scalar_tensor_tensor(out=var_e[:, :], in0=ln_q[:, :], scalar=0.25, in1=ln_e[:, :],
                                       op0=ALU.mult, op1=ALU.add).then_inc(var_s, 1)
                dve.wait_ge(var_s, c.n + 1)

            def rsqrt(c, rs_s, norm_s):
                done = [0]

                def link(ins):
                    ins.then_inc(rs_s, 1)
                    done[0] += 1
                    dve.wait_ge(rs_s, c.n * (2 + 3 * NEWTON - 1) + done[0])

                link(v.tensor_scalar(half_bits[:, :], var_e[:, :].bitcast(I32), 1, None, ALU.logical_shift_right))
                link(v.tensor_scalar(root[:, :].bitcast(I32), half_bits[:, :], -1.0, float(0x5f3759df), ALU.mult, ALU.add))
                for i in range(NEWTON):
                    link(v.tensor_tensor(rs_a[:, :], root[:, :], root[:, :], ALU.mult))
                    link(v.scalar_tensor_tensor(out=rs_b[:, :], in0=rs_a[:, :], scalar=-0.5, in1=var_e[:, :],
                                                op0=ALU.mult, op1=ALU.mult))
                    last = v.scalar_tensor_tensor(out=rstd[:, :] if i == NEWTON - 1 else root[:, :], in0=rs_b[:, :], scalar=1.5,
                                                  in1=root[:, :], op0=ALU.add, op1=ALU.mult)
                    if i < NEWTON - 1:
                        link(last)
                last.then_inc(norm_s, 1)
                dve.wait_ge(norm_s, c.n * 2 + 1)
                v.scalar_tensor_tensor(out=shift[:, :], in0=ln_m[:, :], scalar=-0.5, in1=rstd[:, :],
                                       op0=ALU.mult, op1=ALU.mult).then_inc(norm_s, 1)

            def norm_stats(c):
                dve.wait_ge(att_ready, c.n + 1)
                stats(c, [ATT[:, t * P:(t + 1) * P] for t in range(TILES)], EPS, bst_done, mv_done, var_done)

            def split_rows(c):
                dve.wait_ge(x1_done, c.n * TILES + TILES)
                if not (isinstance(c.half, int) and c.half == 0):
                    dve.wait_ge(scattered[c.par], c.half * (TILES * TOP_K * 16))
                x = x1[c.par][:, :, :]
                v.tensor_scalar(rows[c.par][:, :, 0:C], x, SX, None, ALU.mult).then_inc(high_done, 1)
                dve.wait_ge(high_done, c.n + 1)
                v.scalar_tensor_tensor(out=rows[c.par][:, :, C:2 * C], in0=x, scalar=SX, in1=rows[c.par][:, :, 0:C],
                                       op0=ALU.mult, op1=ALU.subtract).then_inc(rows_done, 1)

            def take_logits(c):
                dve.wait_ge(logit_ready, c.n + 1)
                v.tensor_scalar(logits[:, 0, :], LOGIT, 1.0 / (SW * SX), None, ALU.mult).then_inc(logits_done, 1)
                v.scalar_tensor_tensor(out=logits[:, 1, :], in0=LOGIT, scalar=1.0 / (SW * SX), in1=bias_row[:, :],
                                       op0=ALU.mult, op1=ALU.add).then_inc(logits_done, 1)

            def choose(c):
                dve.wait_ge(expl_done, c.n + 1)
                v.tensor_scalar(exps_1[:, :, :], exps_l[:, :, :], 1.0, None, ALU.add).then_inc(exp1_done, 1)
                dve.wait_ge(exp1_done, c.n + 1)
                v.reciprocal(scores[:, :, :], exps_1[:, :, :]).then_inc(scores_done, 1)
                dve.wait_ge(scores_done, c.n + 1)

            def choose_max(c):
                for t in range(TILES):
                    v.max(top[:, t, :], scores[:, 1, t * E:(t + 1) * E]).then_inc(top_done, 1)
                dve.wait_ge(top_done, c.n * TILES + TILES)

            def choose_index(c):
                for t in range(TILES):
                    v.max_index(top_i[:, t, :], top[:, t, :], scores[:, 1, t * E:(t + 1) * E]).then_inc(topi_done, 1)
                dve.wait_ge(topi_done, c.n * TILES + TILES)
                v.tensor_copy(top_f[:, :, :].rearrange("p k t -> p t k"), top_i[:, :, 0:TOP_K]).then_inc(topf_done, 1)
                dve.wait_ge(topf_done, c.n + 1)
                for k in range(TOP_K):
                    v.tensor_tensor(per_tile(hot[:, k, :]), per_tile(iota8),
                                    top_f[:, k, :].unsqueeze(2).to_broadcast([P, TILES, E]), ALU.is_equal).then_inc(hot_done, 1)
                dve.wait_ge(hot_done, c.n * 2 + 2)
                v.tensor_tensor(chosen[:, :], hot[:, 0, :], hot[:, 1, :], ALU.add).then_inc(chosen_done, 1)

            def gaps(c):
                v.tensor_tensor(hot_s[:, :, :], hot[:, :, :],
                                scores[:, 0:1, :].to_broadcast([P, TOP_K, TILES * E]), ALU.mult).then_inc(hots_done, 1)
                dve.wait_ge(hots_done, c.n + 1)
                v.tensor_reduce(got[:, :, :], hot_s[:, :, :].rearrange("p k (t e) -> p k t e", e=E), AX_X, ALU.add).then_inc(got_done, 1)
                dve.wait_ge(got_done, c.n + 1)
                v.tensor_tensor(gap[:, bass.ds(c.n * TILES, TILES)], got[:, 0, :], got[:, 1, :], ALU.subtract).then_inc(gap_done, 1)

            def slots(c):
                dve.wait_ge(rank_ready, c.n + 1)
                if not (isinstance(c.n, int) and c.n == 0):
                    dve.wait_ge(taken_done, c.n)
                v.tensor_tensor(per_tile(slot_e[:, :]), per_tile(RANK), taken[:, :].unsqueeze(1).to_broadcast([P, TILES, E]),
                                ALU.add).then_inc(slote_done, 1)
                dve.wait_ge(slote_done, c.n + 1)
                v.tensor_tensor(taken[:, :], TOTAL, taken[:, :], ALU.add).then_inc(taken_done, 1)
                v.tensor_tensor(hot_r[:, :, :], hot[:, :, :],
                                slot_e[:, :].unsqueeze(1).to_broadcast([P, TOP_K, TILES * E]), ALU.mult).then_inc(hotr_done, 1)
                dve.wait_ge(hotr_done, c.n + 1)
                v.tensor_reduce(slot_f[:, :, :], hot_r[:, :, :].rearrange("p k (t e) -> p k t e", e=E), AX_X, ALU.add).then_inc(slotf_done, 1)
                dve.wait_ge(slotf_done, c.n + 1)
                v.tensor_copy(slot[c.par][:, :, :], slot_f[:, :, :]).then_inc(slot_done, 1)

            def low_weights(c):
                high, low = (rt_w[:, bass.ds(c.n, 1), s, :].rearrange("p a n -> p (a n)") for s in range(2))
                dve.wait_ge(w_high, c.n + 1)
                v.scalar_tensor_tensor(out=low, in0=stage[c.par][:, :], scalar=SW, in1=high,
                                       op0=ALU.mult, op1=ALU.subtract).then_inc(w_low, 1)

            def add_shared(c):
                dve.wait_ge(proj_done, c.n * SF + SF)
                v.scalar_tensor_tensor(out=base[:, bass.ds(c.n * TILES, TILES), :], in0=Y.rearrange("p (t d) -> p t d", d=C),
                                       scalar=0.5, in1=x1[c.par][:, :, :],
                                       op0=ALU.mult, op1=ALU.add).then_inc(base_done, 1)

            def step(c, q, n):
                if c is not None:
                    values(c)
                if q is not None:
                    take_logits(q)
                if c is not None:
                    scan_p(c)
                if q is not None:
                    choose(q)
                if c is not None:
                    scan_q(c)
                if q is not None:
                    choose_max(q)
                if c is not None:
                    denominators(c)
                if q is not None:
                    choose_index(q)
                if c is not None:
                    invert(c)
                    gated_out(c)
                if n is not None:
                    scan_max(n)
                if q is not None:
                    slots(q)
                if c is not None:
                    norm_stats(c)
                    rsqrt(c, rs_step, norm_done)
                if q is not None:
                    gaps(q)
                if c is not None:
                    low_weights(c)
                    split_rows(c)
                if q is not None and c is None:
                    units_table()
                if q is not None:
                    add_shared(q)

            def units_table():
                tab = [0]

                def link(ins):
                    ins.then_inc(table, 1)
                    tab[0] += 1
                    dve.wait_ge(table, tab[0])

                dve.wait_ge(taken_done, CHUNKS)
                v.tensor_copy(end_row[:, :], taken[:, :]).then_inc(ends_ready, 1)
                link(v.tensor_tensor(cnt_f[:, :], taken[:, :], consts[:, K_EN:K_EN + E], ALU.add))
                link(v.tensor_copy(cnt_i[:, :], cnt_f[:, :]))
                link(v.tensor_scalar(tile_i[:, :], cnt_i[:, :], UT.bit_length() - 1, None, ALU.logical_shift_right))
                link(v.tensor_copy(tile_f[:, :], tile_i[:, :]))
                link(v.tensor_tensor_scan(cum[:, :], ones8[:, :], tile_f[:, :], 0.0, ALU.mult, ALU.add))
                cum_b = cum[:, :].unsqueeze(1).to_broadcast([P, UNITS, E])
                link(v.tensor_tensor(past[:, :, :], iota_u.unsqueeze(2).to_broadcast([P, UNITS, E]), cum_b, ALU.is_ge))
                link(v.tensor_reduce(unit_e[:, :], past[:, :, :], AX_X, ALU.add))
                link(v.tensor_tensor(past_c[:, :, :], past[:, :, :], cum_b, ALU.mult))
                link(v.tensor_reduce(unit_s[:, :], past_c[:, :, :], AX_X, ALU.max))
                link(v.tensor_tensor(unit_j[:, :], iota_u, unit_s[:, :], ALU.subtract))
                link(v.tensor_scalar(unit_r[:, :], unit_e[:, :], float(CAP), None, ALU.mult))
                link(v.scalar_tensor_tensor(out=unit_r2[:, :], in0=unit_j[:, :], scalar=float(UT), in1=unit_r[:, :],
                                            op0=ALU.mult, op1=ALU.add))
                link(v.tensor_scalar(unit_row[:, :], unit_r2[:, :], float(DUMP), None, ALU.min))
                link(v.memset(unit_w[:, UNITS:UNITS + RING], 0.0))
                link(v.tensor_scalar(unit_w[:, 0:UNITS], unit_e[:, :], float(E - 1), None, ALU.min))
                link(v.scalar_tensor_tensor(out=unit_w2[:, :], in0=unit_w[:, 1:UNITS + 3], scalar=float(E), in1=unit_w[:, 0:UNITS + 2],
                                            op0=ALU.mult, op1=ALU.add))
                link(v.scalar_tensor_tensor(out=unit_w4[:, :], in0=unit_w2[:, 2:UNITS + 2], scalar=float(E ** 2),
                                            in1=unit_w2[:, 0:UNITS], op0=ALU.mult, op1=ALU.add))
                v.scalar_tensor_tensor(out=unit_w5[:, :], in0=unit_w[:, RING:UNITS + RING], scalar=float(E ** RING), in1=unit_w4[:, :],
                                       op0=ALU.mult, op1=ALU.add).then_inc(table_ready, 1)

            count = [0]

            def counted(ins):
                ins.then_inc(prep, 1)
                count[0] += 1

            counted(v.memset(w_row[:, :], 0.0))
            counted(v.memset(state[0][:, 0, 0:1], -1e38))
            counted(v.memset(state[0][:, 1:3, 0:1], 0.0))
            counted(v.memset(ones8[:, :], 1.0))
            dve.wait_ge(att_in, 32)
            counted(v.tensor_scalar(one_minus[:, :], vec[:, 2:5], -1.0, 1.0, ALU.mult, ALU.add))
            dve.wait_ge(prep, count[0])
            for i in range(3):
                counted(v.tensor_scalar(att_w[:, i, 0, :], att_raw[:, i, :], vec[:, 2 + i:3 + i], None, ALU.mult))
                counted(v.tensor_scalar(att_w[:, i, 1, :], att_raw[:, i, :], one_minus[:, i:i + 1], None, ALU.mult))
                if i == 0:
                    assert count[0] == PREP_K
            assert count[0] == PREP_MIX
            dve.wait_ge(decay_done, 1)
            counted(v.tensor_scalar(neg_w[:, :], decay[:, :], -1.0, None, ALU.mult))
            dve.wait_ge(prep, count[0])
            counted(v.tensor_scalar(w_row[:, :], w_row[:, :], neg_w[:, 0:1], None, ALU.add))
            dve.wait_ge(prep, count[0])
            scan_max(Chunk(0, 0))
            step(Chunk(0, 0), None, Chunk(0, 1))
            dve.wait_ge(consts_in, 48)
            dve.wait_ge(shared_in, 48)
            counted(v.tensor_copy(taken[:, :], consts[:, K_EB:K_EB + E]))
            counted(v.tensor_scalar(cent_w[:, 0, :], cent_raw[:, :], SW, None, ALU.mult))
            counted(v.tensor_scalar(sh_w[:, 0, :], sh_raw[:, 0, :], SW, None, ALU.mult))
            dve.wait_ge(prep, count[0])
            counted(v.scalar_tensor_tensor(out=cent_w[:, 1, :], in0=cent_raw[:, :], scalar=SW, in1=cent_w[:, 0, :],
                                           op0=ALU.mult, op1=ALU.subtract))
            counted(v.scalar_tensor_tensor(out=sh_w[:, 1, :], in0=sh_raw[:, 0, :], scalar=SW, in1=sh_w[:, 0, :],
                                           op0=ALU.mult, op1=ALU.subtract))
            assert count[0] == PREP_ALL, count[0]
            step(Chunk(0, 1), Chunk(0, 0), Chunk(1, 0))
            with dve.Fori(1, CHUNKS // 2 - 1) as h:
                step(Chunk(h, 0), Chunk(h - 1, 1), Chunk(h, 1))
                step(Chunk(h, 1), Chunk(h, 0), Chunk(h + 1, 0))
            step(LAST0, Chunk(CHUNKS // 2 - 2, 1), LAST1)
            step(LAST1, LAST0, None)
            step(None, LAST1, None)

            dve.wait_ge(gapt_done, 1)
            v.tensor_scalar(gap_1[:, :], gap_e[:, :], 1.0, None, ALU.add).then_inc(mix_step, 1)
            dve.wait_ge(mix_step, 1)
            v.reciprocal(gap_r[:, :], gap_1[:, :]).then_inc(mix_step, 1)
            dve.wait_ge(mix_step, 2)
            v.tensor_scalar(mix[:, 0, :], gap_r[:, :], 0.5, None, ALU.mult).then_inc(mix_done, 1)
            v.tensor_scalar(mix[:, 1, :], gap_r[:, :], -0.5, 0.5, ALU.mult, ALU.add).then_inc(mix_done, 1)

            def unit_split(u, j):
                for h in range(2):
                    part = slice(h * 2 * UT, (h + 1) * 2 * UT)
                    dve.wait_ge(u_hid, u * 2 + 1 + h)
                    if h == 0 and not (isinstance(u, int) and u < 2):
                        dve.wait_ge(u_y, u - 1)
                    v.tensor_scalar(hid_h[j % 2][:, part], hid[j % 2][:, part], SH, None, ALU.mult).then_inc(u_hidh, 1)
                    dve.wait_ge(u_hidh, u * 2 + 1 + h)
                    v.scalar_tensor_tensor(out=hid_l[j % 2][:, part], in0=hid[j % 2][:, part], scalar=SH, in1=hid_h[j % 2][:, part],
                                           op0=ALU.mult, op1=ALU.subtract).then_inc(u_hidl, 1)

            for j in range(RING):
                unit_split(j, j)
            with dve.Fori(1, UNITS // RING) as g:
                for j in range(RING):
                    unit_split(g * RING + j, j)

            def combine(c):
                dve.wait_ge(yl_in[c.par], c.half * 16 + 16)
                if not (isinstance(c.half, int) and c.half == 0):
                    dve.wait_ge(fin_done, (c.n - 1) * TILES)
                dve.wait_ge(acc_done, c.n + 1)
                for t in range(TILES):
                    n = c.n * TILES + t
                    v.scalar_tensor_tensor(out=acc2[c.par][:, t, :], in0=yl[:, bass.ds(n, 1), C:2 * C].rearrange("p a d -> p (a d)"),
                                           scalar=mix[:, 1, bass.ds(n, 1)],
                                           in1=acc[c.par][:, t, :], op0=ALU.mult, op1=ALU.add).then_inc(acc2_done, 1)

            def last_stats(c):
                dve.wait_ge(acc2_done, (c.n + 1) * TILES)
                stats(c, [acc2[c.par][:, t, :] for t in range(TILES)], EPS / 4, f_bst, f_mv, f_var)

            def last_norm(c):
                dve.wait_ge(f_root, c.n + 1)
                v.reciprocal(rs_y[:, :], root[:, :]).then_inc(f_rs, 1)
                dve.wait_ge(f_rs, c.n * 3 + 1)
                v.scalar_tensor_tensor(out=rs_a[:, :], in0=rs_y[:, :], scalar=-0.5, in1=rs_y[:, :],
                                       op0=ALU.mult, op1=ALU.mult).then_inc(f_rs, 1)
                dve.wait_ge(f_rs, c.n * 3 + 2)
                v.tensor_tensor(rs_b[:, :], rs_a[:, :], var_e[:, :], ALU.mult).then_inc(f_rs, 1)
                dve.wait_ge(f_rs, c.n * 3 + 3)
                v.scalar_tensor_tensor(out=rstd[:, :], in0=rs_b[:, :], scalar=1.5, in1=rs_y[:, :],
                                       op0=ALU.add, op1=ALU.mult).then_inc(f_norm, 1)
                dve.wait_ge(f_norm, c.n * 2 + 1)
                v.scalar_tensor_tensor(out=shift[:, :], in0=ln_m[:, :], scalar=-0.5, in1=rstd[:, :],
                                       op0=ALU.mult, op1=ALU.mult).then_inc(f_norm, 1)

            dve.wait_ge(mix_done, 2)
            combine(Chunk(0, 0))
            last_stats(Chunk(0, 0))
            combine(Chunk(0, 1))
            last_norm(Chunk(0, 0))
            last_stats(Chunk(0, 1))
            with dve.Fori(1, CHUNKS // 2) as h:
                combine(Chunk(h, 0))
                dve.wait_ge(fin_done, (h * 2 - 1) * TILES)
                last_norm(Chunk(h - 1, 1))
                last_stats(Chunk(h, 0))
                combine(Chunk(h, 1))
                dve.wait_ge(fin_done, h * 2 * TILES)
                last_norm(Chunk(h, 0))
                last_stats(Chunk(h, 1))
            dve.wait_ge(fin_done, (CHUNKS - 1) * TILES)
            last_norm(LAST1)

        @block.gpsimd
        def _(pool):
            g_ = nc.gpsimd

            def hold_wait(i):
                g_.tensor_tensor(waiter[:, i, :], no_ids[:, :], no_ids[:, :], ALU.add)

            def numerator_a(c):
                pool.wait_ge(p_done, c.n + 1)
                pool.wait_ge(exp_out, c.n + 1)
                g_.tensor_tensor(ap_[:, :], expd[:, 0, 1, :], state[c.par][:, 1, 0:CH], ALU.mult).then_inc(ap_done, 1)

            def numerator_b(c):
                pool.wait_ge(ap_done, c.n + 1)
                pool.wait_ge(bv_done, c.n + 1)
                g_.tensor_tensor(num[:, :], ap_[:, :], bv[:, :], ALU.add).then_inc(num_done, 1)

            def result_rows(c, k):
                if k == 0:
                    pool.wait_ge(rows_done, c.n + 1)
                    pool.wait_ge(slot_done, c.n + 1)
                    if not (isinstance(c.half, int) and c.half == 0):
                        pool.wait_ge(scattered[c.par], c.half * (TILES * TOP_K * 16))
                else:
                    pool.wait_ge(scattered[c.par], c.half * (TILES * TOP_K * 16) + TILES * 16)
                g_.tensor_copy(rows[c.par][:, :, 2 * C:ROW].bitcast(I32),
                               row_ids[:, bass.ds(c.n * TILES, TILES), k:k + 1]).then_inc(ids_done, 1)
                pool.wait_ge(ids_done, c.n * 2 + k + 1)

            def scatter(c, k):
                for t in range(TILES):
                    g_.indirect_dma_start(sorted_x, bass.IndirectOffsetOnAxis(ap=slot[c.par][:, k, t:t + 1].bitcast(U32), axis=0),
                                          rows[c.par][:, t, :], None).then_inc(scattered[c.par], 16)

            def step(c, q):
                if c is not None:
                    numerator_a(c)
                    numerator_b(c)
                if q is not None:
                    for k in range(TOP_K):
                        result_rows(q, k)
                        hold_wait(0)
                        scatter(q, k)

            pool.wait_ge(consts_in, 48)
            g_.memset(no_ids[:, :], 0).then_inc(ids_made, 1)
            pool.wait_ge(ids_made, 1)
            g_.memset(pad[:, :, 0:2 * C], 0.0).then_inc(pad_made, 1)
            g_.memset(pad[:, :, 2 * C:ROW].bitcast(I32), TOKENS * TOP_K).then_inc(pad_made, 1)
            step(Chunk(0, 0), None)
            step(Chunk(0, 1), Chunk(0, 0))
            with pool.Fori(1, CHUNKS // 2) as h:
                step(Chunk(h, 0), Chunk(h - 1, 1))
                step(Chunk(h, 1), Chunk(h, 0))
            step(None, Chunk(CHUNKS // 2 - 1, 1))

            def unit_ids(u, g, j):
                pool.wait_ge(xs_in[j], g * 16 + 16)
                if not (isinstance(g, int) and g == 0):
                    pool.wait_ge(y_out[j], g * (16 * UH))
                g_.tensor_tensor(unit_id[j][:, :], xs[j][:, :, 2 * C:ROW].bitcast(I32).rearrange("p k a -> p (k a)"),
                                 no_ids[:, :], ALU.add).then_inc(u_ids, 1)

            def put_results(j):
                for k in range(UH):
                    g_.indirect_dma_start(routed_y, bass.IndirectOffsetOnAxis(ap=unit_id[j][:, k:k + 1].bitcast(U32), axis=0),
                                          ys[j][:, k, :], None, bounds_check=TOKENS * TOP_K - 1,
                                          oob_is_err=False).then_inc(y_out[j], 16)

            unit_ids(0, 0, 0)
            for j in range(1, RING):
                pool.wait_ge(u_ids, j)
                pool.wait_ge(u_ys, j)
                unit_ids(j, 0, j)
                put_results(j - 1)
            with pool.Fori(1, UNITS // RING) as g:
                for j in range(RING):
                    u = g * RING + j
                    pool.wait_ge(u_ids, u)
                    pool.wait_ge(u_ys, u)
                    unit_ids(u, g, j)
                    put_results((j - 1) % RING)
            pool.wait_ge(u_ids, UNITS)
            pool.wait_ge(u_ys, UNITS)
            put_results(RING - 1)

            def first_results(c):
                pool.wait_ge(yl_in[c.par], c.half * 16 + 16)
                if not (isinstance(c.half, int) and c.half == 0):
                    pool.wait_ge(acc2_done, (c.n - 1) * TILES)
                hold_wait(1)
                tiles = bass.ds(c.n * TILES, TILES)
                g_.tensor_tensor(weighted[c.par][:, :, :], yl[:, tiles, 0:C], mix[:, 0, tiles].unsqueeze(2).to_broadcast([P, TILES, C]),
                                 ALU.mult).then_inc(weighted_done, 1)
                pool.wait_ge(weighted_done, c.n + 1)
                hold_wait(2)
                g_.tensor_tensor(acc[c.par][:, :, :], weighted[c.par][:, :, :], base[:, tiles, :], ALU.add).then_inc(acc_done, 1)

            pool.wait_ge(mix_done, 2)
            first_results(Chunk(0, 0))
            first_results(Chunk(0, 1))
            with pool.Fori(1, CHUNKS // 2) as h:
                first_results(Chunk(h, 0))
                first_results(Chunk(h, 1))


PREP_K, PREP_MIX, PREP_ALL = 7, 11, 18


def kernel(**inputs):
    import numpy as _np
    import concourse.bacc as _bacc
    from concourse import mybir as _mybir
    from concourse.bass_utils import run_bass_kernel_spmd as _run

    a = {k: _np.asarray(x) for k, x in inputs.items()}
    x = a["L0_attn_x"]
    xT = _np.zeros((C, B, T + 1), _np.float32)
    xT[:, :, 1:] = x.transpose(2, 0, 1)
    w_att = _np.stack([a[f"L0_attn_W_{n}"].T for n in ("key", "value", "receptance", "output")], axis=1)
    vecs = _np.stack([a[f"L0_attn_time_{n}"].reshape(C) for n in ("decay", "first", "mix_k", "mix_v", "mix_r")], axis=1)

    def layers(fc, proj):
        n = fc.shape[0]
        one = fc.transpose(0, 2, 1)
        two = proj.reshape(n, C, FC, P).transpose(0, 3, 2, 1).reshape(n, P, FF)
        return _np.stack([one, two], axis=2)

    w_sh = layers(a["L0_ffn_Wfc_sh"], a["L0_ffn_Wproj_sh"]).transpose(1, 2, 0, 3).reshape(P, 2, SF * P)
    w_rt = layers(a["L0_ffn_Wfc_r"], a["L0_ffn_Wproj_r"]).reshape(E, P, 2 * FF)
    cent = a["L0_ffn_centroids"].T
    bias = _np.broadcast_to(a["L0_ffn_routing_bias"][None, None, :], (P, TILES, E)).reshape(P, TILES * E)
    kf = _np.zeros((P, K_END), _np.float32)
    kf[:, K_ID:K_ID + P] = _np.eye(P)
    kf[:, K_I8:K_I8 + TILES * E] = _np.tile(_np.arange(E), TILES)
    kf[:, K_EB:K_EB + E] = _np.arange(E) * CAP
    kf[:, K_EN:K_EN + E] = UT - 1 - _np.arange(E) * CAP
    kf[:, K_IU:K_IU + UNITS] = _np.arange(UNITS)
    kh = _np.concatenate([_np.eye(P), _np.triu(_np.ones((P, P)), 1), _np.ones((P, P))], axis=1).astype(_np.float16)
    token = _np.arange(NT)[None, :, None] * P + _np.arange(P)[:, None, None]
    kid = (token * TOP_K + _np.arange(TOP_K)[None, None, :]).astype(_np.int32)

    nc = _bacc.Bacc("TRN2", target_bir_lowering=False, num_devices=1)
    arrays, args = {}, []
    for name, arr in dict(xT=xT, w_att=w_att, vecs=vecs, w_sh=w_sh, w_rt=w_rt, cent=cent, bias=bias, kf=kf, kh=kh, kid=kid).items():
        arr = _np.ascontiguousarray(arr)
        arrays[f"in_{name}"] = arr
        args.append(nc.dram_tensor(f"in_{name}", arr.shape, _mybir.dt.from_np(arr.dtype), kind="ExternalInput").ap())
    args.append(nc.dram_tensor("out_0", (B, T, C), _mybir.dt.float32, kind="ExternalOutput").ap())
    build(nc, *args)
    r = _run(nc, [arrays], core_ids=[0])
    return r.results[0]["out_0"]
```

```python
from contextlib import ExitStack

import numpy as np
import concourse.bass as bass
from concourse import mybir

ALU = mybir.AluOpType
ACT = mybir.ActivationFunctionType
AX_X = mybir.AxisListType.X
F32 = mybir.dt.float32
F16 = mybir.dt.float16
I32 = mybir.dt.int32
U32 = mybir.dt.uint32

P = 128
B, T, C = 4, 1024, 128
TOKENS = B * T
CH = 512
TILES = CH // P
CHUNKS = TOKENS // CH
HALVES = T // CH
NT = TOKENS // P
E = 8
NS = 2
TOP_K = 2
FF = 512
FC = FF // P
SF = NS * FC
UT = 256
UH = UT // P
CAP = TOKENS + UT
ROW = 2 * C + 2
DUMP = E * CAP
UNITS = (TOP_K * TOKENS + E * (UT - 1)) // UT
RING = 4
BODY = 2 * RING
assert (UNITS + 1) % BODY == 0
EXPERT_BITS = E.bit_length() - 1
EPS = 1e-5
RSQRT_LINKS = 8
SW = 64.0
SX = 64.0
SH = 16.0

K_ID, K_I8, K_EB, K_EN, K_IU, K_END = np.cumsum([0, P, TILES * E, E, E, UNITS]).tolist()


class Chunk:

    def __init__(self, half, par):
        self.half, self.par, self.n = half, par, half * 2 + par


class Unit:

    def __init__(self, g, j):
        self.g, self.j = g, j
        self.n = g * BODY + (j - 1)
        self.buf = (j - 1) % RING
        self.turn = g * (BODY // RING) + (j - 1) // RING
        self.first = isinstance(g, int) and self.n < RING

    def back(self, k):
        return Unit(self.g, self.j - k)


FIRST_UNITS = [Unit(0, j) for j in range(1, BODY)]
LAST_UNIT = Unit((UNITS + 1) // BODY - 1, BODY - 1)
PASSES = (UNITS + 1) // BODY
LAST0, LAST1 = (Chunk(CHUNKS // 2 - 1, i) for i in range(2))


def build(nc, xT, w_att, vecs, w_sh, w_rt, cent, bias, kf, kh, kid, out):
    ctx = ExitStack()
    with ctx:
        def sb(name, shape, dt=F32):
            return ctx.enter_context(nc.sbuf_tensor(name, shape, dt))

        def sem(name):
            return ctx.enter_context(nc.semaphore(name))

        sorted_x = nc.dram_tensor("sorted_x", (DUMP + UT, ROW), F16, kind="Internal").ap()
        routed_y = nc.dram_tensor("routed_y", (TOKENS * TOP_K, C), F32, kind="Internal").ap()

        consts = sb("consts", [P, K_END])
        half_consts = sb("half_consts", [P, 3 * P], F16)
        row_ids = sb("row_ids", [P, NT, TOP_K], I32)
        ident = consts[:, K_ID:K_ID + P]
        iota8 = consts[:, K_I8:K_I8 + TILES * E]
        iota_u = consts[:, K_IU:K_IU + UNITS]
        ident_h = half_consts[:, 0:P]
        before = half_consts[:, P:2 * P]
        ones_h = half_consts[:, 2 * P:3 * P]
        vec = sb("vec", [P, 5])
        att_raw = sb("att_raw", [P, 4, C])
        one_minus = sb("one_minus", [P, 3])
        att_w = sb("att_w", [P, 3, 2, C])
        decay = sb("decay", [P, 1])
        neg_w = sb("neg_w", [P, 1])
        w_row = sb("w_row", [P, CH])
        sh_raw = sb("sh_raw", [P, 2, SF * P])
        sh_w = sb("sh_w", [P, 2, SF * P], F16)
        cent_raw = sb("cent_raw", [P, E])
        cent_w = sb("cent_w", [P, 2, E], F16)
        bias_row = sb("bias_row", [P, TILES * E])
        stage = [sb(f"stage{i}", [P, 2 * FF]) for i in range(2)]
        rt_w = sb("rt_w", [P, E, 2, 2 * FF], F16)
        xt = [sb(f"xt{i}", [P, CH + 1]) for i in range(2)]
        state = [sb(f"state{i}", [P, 3, CH + 1]) for i in range(2)]
        diff = sb("diff", [P, 2, CH])
        relu = sb("relu", [P, 2, 2, CH])
        expd = sb("expd", [P, 2, 2, CH])
        b2v = sb("b2v", [P, CH])
        bv = sb("bv", [P, CH])
        ap_ = sb("ap_", [P, CH])
        num = sb("num", [P, CH])
        aq = sb("aq", [P, CH])
        den = sb("den", [P, CH])
        exp_r = sb("exp_r", [P, CH])
        both = sb("both", [P, CH])
        inverse = sb("inverse", [P, CH])
        gated = sb("gated", [P, CH])
        bst = sb("bst", [P, 2 * TILES, 6])
        ln_m = sb("ln_m", [P, 2 * TILES])
        ln_d = sb("ln_d", [P, 2 * TILES])
        ln_s = sb("ln_s", [P, 2 * TILES])
        ln_q = sb("ln_q", [P, 2 * TILES])
        ln_e = sb("ln_e", [P, 2 * TILES])
        var_e = sb("var_e", [P, 2 * TILES])
        root = sb("root", [P, 2 * TILES])
        rs_y = sb("rs_y", [P, 2 * TILES])
        rs_a = sb("rs_a", [P, 2 * TILES])
        rs_b = sb("rs_b", [P, 2 * TILES])
        rstd = sb("rstd", [P, 2 * TILES])
        shift = sb("shift", [P, 2 * TILES])
        x1 = [sb(f"x1_{i}", [P, TILES, C]) for i in range(2)]
        base = sb("base", [P, NT, C])
        rows = [sb(f"rows{i}", [P, TILES, ROW], F16) for i in range(2)]
        x1t = [sb(f"x1t{i}", [P, 2, CH], F16) for i in range(2)]
        logits = sb("logits", [P, 2, TILES * E])
        exps_l = sb("exps_l", [P, 2, TILES * E])
        exps_1 = sb("exps_1", [P, 2, TILES * E])
        scores = sb("scores", [P, 2, TILES * E])
        top = sb("top", [P, TILES, 8])
        top_i = sb("top_i", [P, TILES, 8], U32)
        top_f = sb("top_f", [P, TOP_K, TILES])
        hot = sb("hot", [P, TOP_K, TILES * E])
        chosen = sb("chosen", [P, TILES * E], F16)
        hot_s = sb("hot_s", [P, TOP_K, TILES * E])
        got = sb("got", [P, TOP_K, TILES])
        gap = sb("gap", [P, NT])
        gap_e = sb("gap_e", [P, NT])
        gap_1 = sb("gap_1", [P, NT])
        gap_r = sb("gap_r", [P, NT])
        mix = sb("mix", [P, TOP_K, NT])
        slot_e = sb("slot_e", [P, TILES * E])
        taken = sb("taken", [P, E])
        hot_r = sb("hot_r", [P, TOP_K, TILES * E])
        slot_f = sb("slot_f", [P, TOP_K, TILES])
        slot = [sb(f"slot{i}", [P, TOP_K, TILES], I32) for i in range(2)]
        cnt_f = sb("cnt_f", [P, E])
        cnt_i = sb("cnt_i", [P, E], I32)
        tile_i = sb("tile_i", [P, E], I32)
        tile_f = sb("tile_f", [P, E])
        ones8 = sb("ones8", [P, E])
        cum = sb("cum", [P, E])
        past = sb("past", [P, UNITS, E])
        past_c = sb("past_c", [P, UNITS, E])
        unit_e = sb("unit_e", [P, UNITS])
        unit_s = sb("unit_s", [P, UNITS])
        unit_j = sb("unit_j", [P, UNITS])
        unit_r = sb("unit_r", [P, UNITS])
        unit_r2 = sb("unit_r2", [P, UNITS])
        unit_row = sb("unit_row", [P, UNITS], I32)
        unit_w = sb("unit_w", [P, UNITS + 2 * RING])
        code2 = sb("code2", [P, UNITS + 2 * RING - 2])
        code4 = sb("code4", [P, UNITS + RING])
        codes = sb("codes", [P, UNITS, 2], I32)
        end_row = sb("end_row", [P, E], I32)
        pad = sb("pad", [P, UH, ROW], F16)
        xs = [sb(f"xs{i}", [P, UH, ROW], F16) for i in range(RING)]
        ys = [sb(f"ys{i}", [P, UH, C]) for i in range(RING)]
        unit_id = [sb(f"unit_id{i}", [P, UH], I32) for i in range(RING)]
        waiter = sb("waiter", [P, 3, UH], I32)
        no_ids = sb("no_ids", [P, UH], I32)
        hid = [sb(f"hid{i}", [P, FC * UT]) for i in range(2)]
        hid_h = [sb(f"hid_h{i}", [P, FC * UT], F16) for i in range(2)]
        hid_l = [sb(f"hid_l{i}", [P, FC * UT], F16) for i in range(2)]
        yl = rt_w.rearrange("p e s n -> p (e s n)").bitcast(F32).rearrange("p (n d) -> p n d", d=TOP_K * C)
        weighted = [sb(f"weighted{i}", [P, TILES, C]) for i in range(2)]
        acc = [sb(f"acc{i}", [P, TILES, C]) for i in range(4)]
        total = [buf[:, i, :, :].rearrange("p a (t d) -> p (a t) d", d=C) for buf in (relu, expd) for i in range(2)]
        f_rstd = [sb(f"f_rstd{i}", [P, 2 * TILES]) for i in range(2)]
        f_shift = [sb(f"f_shift{i}", [P, 2 * TILES]) for i in range(2)]
        fin = [sh_raw[:, i // 2, i % 2 * CH:(i % 2 + 1) * CH].rearrange("p (t d) -> p t d", d=C) for i in range(4)]

        ps = ctx.enter_context(nc.psum_tensor("ps", [P, 8, 512], F32))
        K, V, R, ATT = (ps[:, i, :] for i in range(4))
        HID = [hid[i // 2][:, i % 2 * CH:(i % 2 + 1) * CH] for i in range(4)]
        TR = ps[:, 4, :].bitcast(F16).rearrange("p (s n) -> p s n", s=2)
        FCB = [ps[:, 5 + i, :] for i in range(2)]
        Y = ps[:, 7, :]
        LOGIT = ps[:, 3, 0:TILES * E]
        RANK = ps[:, 2, 64:64 + TILES * E]
        TOTAL = ps[:, 2, 128:128 + E]
        FCU = [ps[:, 2 * i:2 * i + 2, :].rearrange("p b n -> p (b n)") for i in range(2)]
        TRU = [ps[:, 4 + i, 0:UT].bitcast(F16).rearrange("p (s n) -> p s n", s=2) for i in range(2)]
        YU = [ps[:, 6 + i, 0:UH * C] for i in range(2)]

        consts_in = sem("consts_in")
        att_in = sem("att_in")
        shared_in = sem("shared_in")
        stage_in = [sem(f"stage_in{i}") for i in range(2)]
        xt_in = [sem(f"xt_in{i}") for i in range(2)]
        decay_done = sem("decay_done")
        prep = sem("prep")
        w_high = sem("w_high")
        w_scaled = sem("w_scaled")
        w_low = sem("w_low")
        ids_made = sem("ids_made")
        pad_made = sem("pad_made")
        pads_out = sem("pads_out")
        k_ready, v_ready, r_ready = sem("k_ready"), sem("v_ready"), sem("r_ready")
        carried = sem("carried")
        sums_carried = sem("sums_carried")
        o_done, p_done, q_done = sem("o_done"), sem("p_done"), sem("q_done")
        diff_done = sem("diff_done")
        relu_done = sem("relu_done")
        first_relu = sem("first_relu")
        exp_state = sem("exp_state")
        exp_out = sem("exp_out")
        b2v_done = sem("b2v_done")
        bv_done = sem("bv_done")
        ap_done = sem("ap_done")
        num_done = sem("num_done")
        aq_done = sem("aq_done")
        den_done = sem("den_done")
        both_done = sem("both_done")
        inverse_done = sem("inverse_done")
        gate_done = sem("gate_done")
        gated_done = sem("gated_done")
        att_ready = sem("att_ready")
        bst_done = sem("bst_done")
        mv_done = sem("mv_done")
        var_done = sem("var_done")
        rs_step = sem("rs_step")
        norm_done = sem("norm_done")
        x1_done = sem("x1_done")
        high_done = sem("high_done")
        copy_done = sem("copy_done")
        rows_done = sem("rows_done")
        turned = sem("turned")
        x1t_done = sem("x1t_done")
        logit_ready = sem("logit_ready")
        logits_done = sem("logits_done")
        expl_done = sem("expl_done")
        exp1_done = sem("exp1_done")
        scores_done = sem("scores_done")
        top_done = sem("top_done")
        topi_done = sem("topi_done")
        topf_done = sem("topf_done")
        hot_done = sem("hot_done")
        chosen_done = sem("chosen_done")
        hots_done = sem("hots_done")
        got_done = sem("got_done")
        gap_done = sem("gap_done")
        rank_ready = sem("rank_ready")
        slote_done = sem("slote_done")
        taken_done = sem("taken_done")
        hotr_done = sem("hotr_done")
        slotf_done = sem("slotf_done")
        slot_done = sem("slot_done")
        ids_done = sem("ids_done")
        scattered = [sem(f"scattered{i}") for i in range(2)]
        fc_ready = sem("fc_ready")
        hid_done = sem("hid_done")
        proj_done = sem("proj_done")
        base_done = sem("base_done")
        table = sem("table")
        ends_ready = sem("ends_ready")
        table_ready = sem("table_ready")
        xs_in = [sem(f"xs_in{i}") for i in range(RING)]
        u_ids = sem("u_ids")
        u_turned = sem("u_turned")
        u_xt = sem("u_xt")
        u_fc = sem("u_fc")
        u_hid = sem("u_hid")
        u_hidh = sem("u_hidh")
        u_hidl = sem("u_hidl")
        u_y = sem("u_y")
        u_ys = sem("u_ys")
        y_out = [sem(f"y_out{i}") for i in range(RING)]
        gapt_done = sem("gapt_done")
        mix_step = sem("mix_step")
        mix_done = sem("mix_done")
        yl_in = [sem(f"yl_in{i}") for i in range(CHUNKS)]
        weighted_done = sem("weighted_done")
        acc_0 = sem("acc_0")
        acc_done = sem("acc_done")
        total_done = sem("total_done")
        f_root = sem("f_root")
        f_rs = sem("f_rs")
        f_bst = sem("f_bst")
        f_mv = sem("f_mv")
        f_var = sem("f_var")
        f_norm = sem("f_norm")
        fin_done = sem("fin_done")
        stored = [sem(f"stored{i}") for i in range(4)]
        fin_last = sem("fin_last")

        block = ctx.enter_context(nc.Block())

        out_v = out.rearrange("b (h t p) d -> (b h) p t d", p=P, t=TILES)
        yl_v = routed_y.rearrange("(c t p k) d -> c p t (k d)", p=P, t=TILES, k=TOP_K)

        @block.sync
        def _(sp):
            def load_chunk(c):
                first = isinstance(c.half, int) and c.half == 0
                if not first:
                    sp.wait_ge(att_ready, c.n - 1)
                src = xT[:, bass.ds(c.half, 1), c.par * CH:c.par * CH + CH + 1]
                sp.dma_start(xt[c.par][:, :], src.rearrange("p a n -> p (a n)")).then_inc(xt_in[c.par], 16)
                if not first:
                    sp.wait_ge(w_low, c.n - 1)
                sp.dma_start(stage[c.par][:, :],
                             w_rt[bass.ds(c.n, 1), :, :].rearrange("a p n -> (a p) n")).then_inc(stage_in[c.par], 16)

            sp.dma_start(att_raw[:, :, :], w_att).then_inc(att_in, 16)
            sp.dma_start(vec[:, :], vecs).then_inc(att_in, 16)
            load_chunk(Chunk(0, 0))
            sp.dma_start(consts[:, :], kf).then_inc(consts_in, 16)
            sp.dma_start(half_consts[:, :], kh).then_inc(consts_in, 16)
            sp.dma_start(row_ids[:, :, :], kid).then_inc(consts_in, 16)
            sp.dma_start(cent_raw[:, :], cent).then_inc(shared_in, 16)
            sp.dma_start(bias_row[:, :], bias).then_inc(shared_in, 16)
            sp.dma_start(sh_raw[:, :, :], w_sh).then_inc(shared_in, 16)
            load_chunk(Chunk(0, 1))
            sp.wait_ge(pad_made, 2)
            sp.dma_start(sorted_x[DUMP:DUMP + UT, :].rearrange("(j p) w -> p j w", p=P), pad[:, :, :]).then_inc(pads_out, 16)
            with sp.Fori(1, CHUNKS // 2) as h:
                load_chunk(Chunk(h, 0))
                load_chunk(Chunk(h, 1))

            sp.wait_ge(ends_ready, 1)
            ends = nc.values_load_multi_w_load_instructions(end_row[0:1, 0:E], engines=[mybir.EngineType.SP], min_val=0, max_val=DUMP)[1]
            for r in ends:
                sp.dma_start(sorted_x[bass.ds(r, UT), :].rearrange("(j p) w -> p j w", p=P),
                             pad[:, :, :]).then_inc(pads_out, 16)

            def load_unit(u):
                r = sp.value_load(unit_row[0:1, bass.ds(u.n, 1)], min_val=0, max_val=DUMP)
                if not u.first:
                    sp.wait_ge(u_turned, u.n - RING + 1)
                    sp.wait_ge(u_ids, u.n - RING + 1)
                sp.dma_start(xs[u.buf][:, :, :],
                             sorted_x[bass.ds(r, UT), :].rearrange("(j p) w -> p j w", p=P)).then_inc(xs_in[u.buf], 16)

            sp.wait_ge(pads_out, 16 * (E + 1))
            for i in range(2):
                sp.wait_ge(scattered[i], CHUNKS // 2 * TILES * TOP_K * 16)
            sp.wait_ge(table_ready, 1)
            for u in FIRST_UNITS:
                load_unit(u)
            with sp.Fori(1, PASSES) as g:
                for j in range(BODY):
                    load_unit(Unit(g, j))

            for j in range(RING):
                sp.wait_ge(y_out[j], len(range(j, UNITS, RING)) * 16 * UH)
            for n in range(CHUNKS):
                sp.dma_start(yl[:, n * TILES:(n + 1) * TILES, :], yl_v[n]).then_inc(yl_in[n], 16)
            for n in range(CHUNKS):
                if n < CHUNKS - 2:
                    sp.wait_ge(fin_done, (n + 1) * TILES)
                elif n == CHUNKS - 2:
                    sp.wait_ge(fin_done, (n + 1) * TILES - 1)
                    sp.wait_ge(fin_last, 1)
                else:
                    sp.wait_ge(fin_last, TILES + 1)
                sp.dma_start(out_v[n], fin[n % 4][:, :, :]).then_inc(stored[n % 4], 16)
            for i in range(4):
                sp.wait_ge(stored[i], CHUNKS // 4 * 16)

        @block.tensor
        def _(pe):
            def mix_x(c, i, bank, ready):
                nc.tensor.matmul(bank, att_w[:, i, 0, :], xt[c.par][:, 1:CH + 1], start=True, stop=False)
                nc.tensor.matmul(bank, att_w[:, i, 1, :], xt[c.par][:, 0:CH], start=False, stop=True).then_inc(ready, 1)

            def turn(c):
                pe.wait_ge(rows_done, c.n * 2 + 2)
                for s in range(2):
                    for t in range(TILES):
                        mm = nc.tensor.transpose(TR[:, s, t * P:(t + 1) * P], rows[c.par][:, t, s * C:(s + 1) * C], ident_h)
                mm.then_inc(turned, 1)

            def route(c):
                pe.wait_ge(x1t_done, c.n + 1)
                for t in range(TILES):
                    for i, (s, w) in enumerate(((0, 0), (0, 1), (1, 0))):
                        mm = nc.tensor.matmul(LOGIT[:, t * E:(t + 1) * E], x1t[c.par][:, s, t * P:(t + 1) * P], cent_w[:, w, :],
                                              start=(t == 0 and i == 0), stop=(i == 2), skip_group_check=True)
                mm.then_inc(logit_ready, 1)

            def rank(c):
                pe.wait_ge(chosen_done, c.n + 1)
                for t in range(TILES):
                    for s in range(t + 1):
                        nc.tensor.matmul(RANK[:, t * E:(t + 1) * E], before if s == t else ones_h, chosen[:, s * E:(s + 1) * E],
                                         start=(t == 0), stop=(s == t), skip_group_check=True)
                for s in range(TILES):
                    mm = nc.tensor.matmul(TOTAL, ones_h, chosen[:, s * E:(s + 1) * E], start=False, stop=(s == TILES - 1),
                                          skip_group_check=True)
                mm.then_inc(rank_ready, 1)

            def shared_fc(c, f):
                n = c.n * SF + f
                if not (isinstance(n, int) and n < 2):
                    pe.wait_ge(hid_done, n - 1)
                for i, (w, s) in enumerate(((0, 0), (0, 1), (1, 0))):
                    mm = nc.tensor.matmul(FCB[f % 2], sh_w[:, w, f * P:(f + 1) * P], x1t[c.par][:, s, :],
                                          start=(i == 0), stop=(i == 2))
                mm.then_inc(fc_ready, 1)

            def shared_proj(c, f):
                if f == 0 and not (isinstance(c.n, int) and c.n == 0):
                    pe.wait_ge(base_done, c.n)
                pe.wait_ge(hid_done, c.n * SF + f + 1)
                for t in range(TILES):
                    mm = nc.tensor.matmul(Y[:, t * C:(t + 1) * C], HID[f % 4][:, t * P:(t + 1) * P], sh_raw[:, 1, f * P:(f + 1) * P],
                                          start=(f == 0 and t == 0), stop=(f == SF - 1), skip_group_check=True)
                mm.then_inc(proj_done, 1)

            def attend_out(c):
                for t in range(TILES):
                    if t % (TILES // 2) == 0:
                        pe.wait_ge(gated_done, c.n * 2 + t // (TILES // 2) + 1)
                    o = ATT[:, t * P:(t + 1) * P]
                    nc.tensor.matmul(o, gated[:, t * P:(t + 1) * P], att_raw[:, 3, :], start=(t == 0), stop=False, skip_group_check=True)
                    mm = nc.tensor.matmul(o, xt[c.par][:, 1 + t * P:1 + (t + 1) * P], ident, start=False, stop=True,
                                          skip_group_check=True)
                mm.then_inc(att_ready, 1)

            def step(c, q, n, k):
                if q is not None:
                    route(q)
                for f in range(SF + 1):
                    if q is not None and f < SF:
                        shared_fc(q, f)
                    if f == 1 and n is not None:
                        pe.wait_ge(bv_done, n.n)
                        mix_x(n, 1, V, v_ready)
                    if f == 5 and c is not None:
                        attend_out(c)
                    if q is not None:
                        if f == 1 and c is None:
                            rank(q)
                        if f > 0:
                            shared_proj(q, f - 1)
                        if f == 5 and c is not None:
                            rank(q)
                if k is not None:
                    mix_k(k)
                if c is not None:
                    turn(c)
                if n is not None:
                    if q is not None:
                        pe.wait_ge(taken_done, q.n + 1)
                    mix_x(n, 2, R, r_ready)

            def mix_k(c):
                pe.wait_ge(xt_in[c.par], c.half * 16 + 16)
                if not (isinstance(c.n, int) and c.n == 0):
                    pe.wait_ge(diff_done, c.n * 2)
                mix_x(c, 0, K, k_ready)

            pe.wait_ge(prep, PREP_K)
            mix_k(Chunk(0, 0))
            pe.wait_ge(prep, PREP_MIX)
            mix_x(Chunk(0, 0), 1, V, v_ready)
            mix_x(Chunk(0, 0), 2, R, r_ready)
            pe.wait_ge(consts_in, 48)
            mix_k(Chunk(0, 1))
            step(Chunk(0, 0), None, Chunk(0, 1), Chunk(1, 0))
            pe.wait_ge(prep, PREP_ALL)
            pe.wait_ge(shared_in, 48)
            step(Chunk(0, 1), Chunk(0, 0), Chunk(1, 0), Chunk(1, 1))
            with pe.Fori(1, CHUNKS // 2 - 1) as h:
                step(Chunk(h, 0), Chunk(h - 1, 1), Chunk(h, 1), Chunk(h + 1, 0))
                step(Chunk(h, 1), Chunk(h, 0), Chunk(h + 1, 0), Chunk(h + 1, 1))
            step(LAST0, Chunk(CHUNKS // 2 - 2, 1), LAST1, None)
            step(LAST1, LAST0, None, None)
            step(None, LAST1, None, None)

            def unit_turn(u):
                pe.wait_ge(xs_in[u.buf], (u.turn + 1) * 16)
                if not (isinstance(u.n, int) and u.n < 2):
                    pe.wait_ge(u_xt, u.n - 1)
                for s in range(2):
                    for k in range(UH):
                        mm = nc.tensor.transpose(TRU[u.buf % 2][:, s, k * P:(k + 1) * P], xs[u.buf][:, k, s * C:(s + 1) * C], ident_h)
                mm.then_inc(u_turned, 1)

            def experts_of(n):
                words = nc.values_load_multi_w_load_instructions(
                    codes[0:1, bass.ds(n, 1), :].rearrange("p a n -> p (a n)"), engines=[mybir.EngineType.PE],
                    min_val=0, max_val=E ** (RING + 1) - 1)[1]
                return [(words[0] >> (EXPERT_BITS * i)) & (E - 1) for i in range(RING + 1)] + \
                       [(words[1] >> (EXPERT_BITS * i)) & (E - 1) for i in range(1, RING + 1)]

            def expert_weights(e, s, layer):
                return rt_w[:, bass.ds(e, 1), s, layer * FF:(layer + 1) * FF].rearrange("p a n -> p (a n)")

            def unit_fc(u, e):
                b = u.buf % 2
                w = [expert_weights(e, s, 0) for s in range(2)]
                pe.wait_ge(u_xt, u.n + 1)
                for f in range(FC):
                    if f % 2 == 0 and not (isinstance(u.n, int) and u.n < 2):
                        pe.wait_ge(u_hid, u.n * 2 - 3 + f // 2)
                    for i, (a, s) in enumerate(((0, 0), (0, 1), (1, 0))):
                        mm = nc.tensor.matmul(FCU[b][:, f * UT:(f + 1) * UT], w[a][:, f * P:(f + 1) * P], x1t[b][:, s, 0:UT],
                                              start=(f % 2 == 0 and i == 0), stop=(i == 2), skip_group_check=True)
                    if f % 2 == 1:
                        mm.then_inc(u_fc, 1)

            def unit_proj(u, e):
                b = u.buf % 2
                w = [expert_weights(e, s, 1) for s in range(2)]
                if not (isinstance(u.n, int) and u.n < 2):
                    pe.wait_ge(u_ys, u.n - 1)
                for f in range(FC):
                    if f % 2 == 0:
                        pe.wait_ge(u_hidl, u.n * 2 + 1 + f // 2)
                    for k in range(UH):
                        h = [x[b][:, f * UT + k * P:f * UT + (k + 1) * P] for x in (hid_h, hid_l)]
                        for i, (s, a) in enumerate(((0, 0), (0, 1), (1, 0))):
                            mm = nc.tensor.matmul(YU[b][:, k * C:(k + 1) * C], h[s], w[a][:, f * P:(f + 1) * P],
                                                  start=(f == 0 and k == 0 and i == 0), stop=(f == FC - 1 and i == 2),
                                                  skip_group_check=True)
                mm.then_inc(u_y, 1)

            pe.wait_ge(base_done, CHUNKS)
            pe.wait_ge(taken_done, CHUNKS)
            pe.wait_ge(w_low, E)
            pe.wait_ge(table_ready, 1)
            e = experts_of(0)
            unit_turn(FIRST_UNITS[0])
            for n, u in enumerate(FIRST_UNITS[1:], 1):
                unit_turn(u)
                unit_fc(u.back(1), e[n - 1])
                if n > 1:
                    unit_proj(u.back(2), e[n - 2])
            with pe.Fori(1, PASSES) as g:
                e = experts_of(g * BODY - 3)
                for j in range(BODY):
                    u = Unit(g, j)
                    unit_turn(u)
                    unit_fc(u.back(1), e[j + 1])
                    unit_proj(u.back(2), e[j])
            e = experts_of(UNITS - 2)
            unit_fc(LAST_UNIT, e[1])
            unit_proj(LAST_UNIT.back(1), e[0])
            unit_proj(LAST_UNIT, e[1])

        @block.scalar
        def _(act):
            def relus(c, s):
                act.wait_ge(diff_done, c.n * 2 + 2)
                nc.scalar.activation(relu[:, s, :, :], diff[:, :, :], ACT.Relu, scale=1.0 - 2.0 * s).then_inc(relu_done, 1)

            def first_relus(d):
                act.wait_ge(diff_done, d + 1)
                nc.scalar.activation(relu[:, 0, d, :], diff[:, d, :], ACT.Relu).then_inc(first_relu, 1)
                nc.scalar.activation(relu[:, 1, d, :], diff[:, d, :], ACT.Relu, scale=-1.0).then_inc(relu_done, 1)
                act.wait_ge(first_relu, d + 1)
                act.wait_ge(relu_done, d + 1)

            def exps_state():
                nc.scalar.activation(expd[:, :, 0, :], relu[:, :, 0, :], ACT.Exp, scale=-1.0).then_inc(exp_state, 1)

            def exps_out():
                nc.scalar.activation(expd[:, :, 1, :], relu[:, :, 1, :], ACT.Exp, scale=-1.0).then_inc(exp_out, 1)

            def gates(c):
                act.wait_ge(r_ready, c.n + 1)
                nc.scalar.activation(exp_r[:, :], R, ACT.Exp, scale=-1.0).then_inc(gate_done, 1)

            def high_weights(c):
                act.wait_ge(stage_in[c.par], c.half * 16 + 16)
                nc.scalar.activation(rt_w[:, bass.ds(c.n, 1), 0, :].rearrange("p a n -> p (a n)"), stage[c.par][:, :],
                                     ACT.Copy, scale=SW).then_inc(w_high, 1)

            def scaled_weights(c):
                nc.scalar.activation(stage[c.par][:, :], stage[c.par][:, :], ACT.Copy, scale=SW).then_inc(w_scaled, 1)

            def normalise(c):
                act.wait_ge(norm_done, c.n * 2 + 2)
                for t in range(TILES):
                    nc.scalar.activation(x1[c.par][:, t, :], ATT[:, t * P:(t + 1) * P], ACT.Identity,
                                         bias=shift[:, t:t + 1], scale=rstd[:, t:t + 1]).then_inc(x1_done, 1)

            def copy_turned(c):
                act.wait_ge(turned, c.n + 1)
                nc.scalar.activation(x1t[c.par][:, :, :], TR, ACT.Copy).then_inc(x1t_done, 1)

            def squash(c):
                act.wait_ge(logits_done, c.n * 2 + 2)
                nc.scalar.activation(exps_l[:, :, :], logits[:, :, :], ACT.Exp, scale=-1.0).then_inc(expl_done, 1)

            def shared_gelu(c, f):
                n = c.n * SF + f
                act.wait_ge(fc_ready, n + 1)
                if not (isinstance(n, int) and n < 4):
                    act.wait_ge(proj_done, n - 3)
                nc.scalar.activation(HID[f % 4], FCB[f % 2], ACT.Gelu, scale=1.0 / (SW * SX)).then_inc(hid_done, 1)

            def step(c, q, n):
                if q is not None:
                    squash(q)
                    shared_gelu(q, 0)
                    shared_gelu(q, 1)
                if c is not None:
                    high_weights(c)
                if q is not None:
                    shared_gelu(q, 2)
                    shared_gelu(q, 3)
                if c is not None:
                    scaled_weights(c)
                if q is not None:
                    for f in range(4, SF - 2):
                        shared_gelu(q, f)
                for s in range(2):
                    if n is not None:
                        relus(n, s)
                    if q is not None:
                        shared_gelu(q, SF - 2 + s)
                if c is not None:
                    normalise(c)
                if n is not None:
                    act.wait_ge(relu_done, n.n * 2 + 2)
                    exps_state()
                    exps_out()
                if c is not None:
                    copy_turned(c)
                if n is not None:
                    gates(n)

            act.wait_ge(att_in, 32)
            nc.scalar.activation(decay[:, :], vec[:, 0:1], ACT.Exp).then_inc(decay_done, 1)
            first_relus(0)
            exps_state()
            first_relus(1)
            exps_out()
            gates(Chunk(0, 0))
            step(Chunk(0, 0), None, Chunk(0, 1))
            step(Chunk(0, 1), Chunk(0, 0), Chunk(1, 0))
            with act.Fori(1, CHUNKS // 2 - 1) as h:
                step(Chunk(h, 0), Chunk(h - 1, 1), Chunk(h, 1))
                step(Chunk(h, 1), Chunk(h, 0), Chunk(h + 1, 0))
            step(LAST0, Chunk(CHUNKS // 2 - 2, 1), LAST1)
            step(LAST1, LAST0, None)
            step(None, LAST1, None)
            act.wait_ge(gap_done, CHUNKS)
            nc.scalar.activation(gap_e[:, :], gap[:, :], ACT.Exp, scale=-1.0).then_inc(gapt_done, 1)

            def unit_xt(u):
                act.wait_ge(u_turned, u.n + 1)
                if not (isinstance(u.n, int) and u.n < 2):
                    act.wait_ge(u_fc, u.n * 2 - 2)
                nc.scalar.activation(x1t[u.buf % 2][:, :, 0:UT], TRU[u.buf % 2], ACT.Copy).then_inc(u_xt, 1)

            def unit_gelu(u):
                b = u.buf % 2
                for h in range(2):
                    part = slice(h * 2 * UT, (h + 1) * 2 * UT)
                    act.wait_ge(u_fc, u.n * 2 + 1 + h)
                    if not (isinstance(u.n, int) and u.n < 2):
                        act.wait_ge(u_hidl, u.n * 2 - 3 + h)
                    nc.scalar.activation(hid[b][:, part], FCU[b][:, part], ACT.Gelu, scale=1.0 / (SW * SX)).then_inc(u_hid, 1)

            def unit_y(u):
                act.wait_ge(u_y, u.n + 1)
                if not u.first:
                    act.wait_ge(y_out[u.buf], u.turn * (16 * UH))
                nc.scalar.activation(ys[u.buf][:, :, :], YU[u.buf % 2], ACT.Copy, scale=1.0 / (SW * SH)).then_inc(u_ys, 1)

            act.wait_ge(hid_done, CHUNKS * SF)
            act.wait_ge(proj_done, CHUNKS * SF)
            unit_xt(FIRST_UNITS[0])
            for u in FIRST_UNITS[1:]:
                unit_xt(u)
                unit_gelu(u.back(1))
                if u.n > 1:
                    unit_y(u.back(2))
            with act.Fori(1, PASSES) as g:
                for j in range(BODY):
                    u = Unit(g, j)
                    unit_xt(u)
                    unit_gelu(u.back(1))
                    unit_y(u.back(2))
            unit_gelu(LAST_UNIT)
            unit_y(LAST_UNIT.back(1))
            unit_y(LAST_UNIT)

            def roots(n):
                act.wait_ge(f_var, n + 1)
                nc.scalar.activation(root[:, :], var_e[:, :], ACT.Sqrt).then_inc(f_root, 1)

            def finish(n, i):
                act.wait_ge(f_norm, n * 2 + 2)
                k = n * 2 + i
                if k >= 4:
                    act.wait_ge(stored[k % 4], k // 4 * 16)
                for t in range(TILES - 1 if k == CHUNKS - 2 else TILES):
                    j = i * TILES + t
                    nc.scalar.activation(fin[k % 4][:, t, :], total[n][:, j, :], ACT.Identity,
                                         bias=f_shift[n % 2][:, j:j + 1], scale=f_rstd[n % 2][:, j:j + 1]).then_inc(fin_done, 1)

            roots(0)
            for n in range(CHUNKS // 2):
                finish(n, 0)
                if n < CHUNKS // 2 - 1:
                    finish(n, 1)
                    roots(n + 1)

        @block.vector
        def _(dve):
            v = nc.vector

            def per_tile(x):
                return x.rearrange("p (t e) -> p t e", e=E)

            def scan_max(c):
                S = state[c.par]
                if c.par == 1:
                    dve.wait_ge(o_done, c.n)
                    v.tensor_copy(S[:, 0, 0:1], state[0][:, 0, CH:CH + 1]).then_inc(carried, 1)
                    dve.wait_ge(carried, c.half + 1)
                dve.wait_ge(k_ready, c.n + 1)
                v.tensor_tensor_scan(S[:, 0, 1:CH + 1], w_row[:, :], K, S[:, 0, 0:1], ALU.add, ALU.max).then_inc(o_done, 1)
                dve.wait_ge(o_done, c.n + 1)
                v.scalar_tensor_tensor(out=diff[:, 0, :], in0=S[:, 0, 0:CH], scalar=neg_w[:, 0:1], in1=K,
                                       op0=ALU.add, op1=ALU.subtract).then_inc(diff_done, 1)
                v.scalar_tensor_tensor(out=diff[:, 1, :], in0=K, scalar=vec[:, 1:2], in1=S[:, 0, 0:CH],
                                       op0=ALU.add, op1=ALU.subtract).then_inc(diff_done, 1)

            def values_state(c):
                dve.wait_ge(v_ready, c.n + 1)
                dve.wait_ge(exp_state, c.n + 1)
                v.tensor_tensor(b2v[:, :], V, expd[:, 0, 0, :], ALU.mult).then_inc(b2v_done, 1)

            def values_out(c):
                dve.wait_ge(exp_out, c.n + 1)
                v.tensor_tensor(bv[:, :], V, expd[:, 1, 1, :], ALU.mult).then_inc(bv_done, 1)

            def scan_p(c):
                S = state[c.par]
                dve.wait_ge(b2v_done, c.n + 1)
                v.tensor_tensor_scan(S[:, 1, 1:CH + 1], expd[:, 1, 0, :], b2v[:, :], S[:, 1, 0:1], ALU.mult, ALU.add).then_inc(p_done, 1)

            def scan_q(c):
                S = state[c.par]
                if c.par == 1:
                    dve.wait_ge(q_done, c.n)
                    dve.wait_ge(p_done, c.n)
                    v.tensor_copy(S[:, 1:3, 0:1], state[0][:, 1:3, CH:CH + 1]).then_inc(sums_carried, 1)
                    dve.wait_ge(sums_carried, c.half + 1)
                v.tensor_tensor_scan(S[:, 2, 1:CH + 1], expd[:, 1, 0, :], expd[:, 0, 0, :], S[:, 2, 0:1], ALU.mult, ALU.add).then_inc(q_done, 1)

            def old_part(c):
                dve.wait_ge(q_done, c.n + 1)
                v.tensor_tensor(aq[:, :], state[c.par][:, 2, 0:CH], expd[:, 0, 1, :], ALU.mult).then_inc(aq_done, 1)

            def denominators(c):
                dve.wait_ge(aq_done, c.n + 1)
                v.tensor_tensor(den[:, :], aq[:, :], expd[:, 1, 1, :], ALU.add).then_inc(den_done, 1)

            def join(c):
                dve.wait_ge(gate_done, c.n + 1)
                dve.wait_ge(den_done, c.n + 1)
                v.scalar_tensor_tensor(out=both[:, :], in0=exp_r[:, :], scalar=1.0, in1=den[:, :],
                                       op0=ALU.add, op1=ALU.mult).then_inc(both_done, 1)

            def gated_out(c, q):
                dve.wait_ge(both_done, c.n + 1)
                for i in range(2):
                    half = slice(i * CH // 2, (i + 1) * CH // 2)
                    v.reciprocal(inverse[:, half], both[:, half]).then_inc(inverse_done, 1)
                    if i == 0:
                        dve.wait_ge(num_done, c.n + 1)
                    elif q is not None:
                        choose_max(q)
                    dve.wait_ge(inverse_done, c.n * 2 + i + 1)
                    v.tensor_tensor(gated[:, half], num[:, half], inverse[:, half], ALU.mult).then_inc(gated_done, 1)

            def moments(n, w, eps, bst_s, mv_s, var_s):
                dve.wait_ge(bst_s, n * w + w)
                v.tensor_tensor(ln_d[:, 0:w], bst[:, 0:w, 1], bst[:, 0:w, 4], ALU.subtract).then_inc(mv_s, 1)
                v.tensor_tensor(ln_s[:, 0:w], bst[:, 0:w, 2], bst[:, 0:w, 5], ALU.add).then_inc(mv_s, 1)
                v.tensor_tensor(ln_m[:, 0:w], bst[:, 0:w, 1], bst[:, 0:w, 4], ALU.add).then_inc(mv_s, 1)
                dve.wait_ge(mv_s, n * 5 + 1)
                v.tensor_tensor(ln_q[:, 0:w], ln_d[:, 0:w], ln_d[:, 0:w], ALU.mult).then_inc(mv_s, 1)
                dve.wait_ge(mv_s, n * 5 + 2)
                v.tensor_scalar(ln_e[:, 0:w], ln_s[:, 0:w], 1.0 / C, eps, ALU.mult, ALU.add).then_inc(mv_s, 1)
                dve.wait_ge(mv_s, n * 5 + 5)
                v.scalar_tensor_tensor(out=var_e[:, 0:w], in0=ln_q[:, 0:w], scalar=0.25, in1=ln_e[:, 0:w],
                                       op0=ALU.mult, op1=ALU.add).then_inc(var_s, 1)

            def rsqrt(c, rs_s, norm_s, between):
                done = [0]

                def link(ins):
                    ins.then_inc(rs_s, 1)
                    if done[0] < len(between):
                        between[done[0]]()
                    done[0] += 1
                    dve.wait_ge(rs_s, c.n * RSQRT_LINKS + done[0])

                dve.wait_ge(var_done, c.n + 1)
                link(v.tensor_scalar(root[:, 0:TILES].bitcast(I32), var_e[:, 0:TILES].bitcast(I32), -0.5, float(0x5f3759df),
                                     ALU.mult, ALU.add))
                y, var, square, part = (x[:, 0:TILES] for x in (root, var_e, rs_a, rs_b))
                link(v.tensor_tensor(square, y, y, ALU.mult))
                link(v.scalar_tensor_tensor(out=part, in0=square, scalar=-0.5, in1=var, op0=ALU.mult, op1=ALU.mult))
                link(v.scalar_tensor_tensor(out=y, in0=part, scalar=1.5, in1=y, op0=ALU.add, op1=ALU.mult))
                link(v.tensor_tensor(square, y, y, ALU.mult))
                link(v.tensor_tensor(part, square, var, ALU.mult))
                link(v.tensor_scalar(square, part, 0.375, -1.25, ALU.mult, ALU.add))
                link(v.tensor_tensor(square, square, part, ALU.mult))
                last = v.scalar_tensor_tensor(out=rstd[:, 0:TILES], in0=square, scalar=1.875, in1=y, op0=ALU.add, op1=ALU.mult)
                last.then_inc(norm_s, 1)
                dve.wait_ge(norm_s, c.n * 2 + 1)
                v.scalar_tensor_tensor(out=shift[:, 0:TILES], in0=ln_m[:, 0:TILES], scalar=-0.5, in1=rstd[:, 0:TILES],
                                       op0=ALU.mult, op1=ALU.mult).then_inc(norm_s, 1)

            def norm_stats(c):
                dve.wait_ge(att_ready, c.n + 1)
                for t in range(TILES):
                    v.bn_stats(bst[:, t, :], ATT[:, t * P:(t + 1) * P]).then_inc(bst_done, 1)
                moments(c.n, TILES, EPS, bst_done, mv_done, var_done)

            def split_rows(c):
                for i in range(2):
                    half = slice(i * TILES // 2, (i + 1) * TILES // 2)
                    x = x1[c.par][:, half, :]
                    dve.wait_ge(x1_done, c.n * TILES + half.stop)
                    if i == 0 and not (isinstance(c.half, int) and c.half == 0):
                        dve.wait_ge(scattered[c.par], c.half * (TILES * TOP_K * 16))
                    v.tensor_scalar(rows[c.par][:, half, 0:C], x, SX, None, ALU.mult).then_inc(high_done, 1)
                    dve.wait_ge(high_done, c.n * 2 + i + 1)
                    v.scalar_tensor_tensor(out=rows[c.par][:, half, C:2 * C], in0=x, scalar=SX, in1=rows[c.par][:, half, 0:C],
                                           op0=ALU.mult, op1=ALU.subtract).then_inc(rows_done, 1)

            def take_logits(c):
                dve.wait_ge(logit_ready, c.n + 1)
                v.tensor_scalar(logits[:, 0, :], LOGIT, 1.0 / (SW * SX), None, ALU.mult).then_inc(logits_done, 1)
                v.scalar_tensor_tensor(out=logits[:, 1, :], in0=LOGIT, scalar=1.0 / (SW * SX), in1=bias_row[:, :],
                                       op0=ALU.mult, op1=ALU.add).then_inc(logits_done, 1)

            def choose(c):
                dve.wait_ge(expl_done, c.n + 1)
                v.tensor_scalar(exps_1[:, :, :], exps_l[:, :, :], 1.0, None, ALU.add).then_inc(exp1_done, 1)
                dve.wait_ge(exp1_done, c.n + 1)
                v.reciprocal(scores[:, :, :], exps_1[:, :, :]).then_inc(scores_done, 1)
                dve.wait_ge(scores_done, c.n + 1)

            def choose_max(c):
                for t in range(TILES):
                    v.max(top[:, t, :], scores[:, 1, t * E:(t + 1) * E]).then_inc(top_done, 1)
                dve.wait_ge(top_done, c.n * TILES + TILES)

            def choose_index(c):
                for t in range(TILES):
                    v.max_index(top_i[:, t, :], top[:, t, :], scores[:, 1, t * E:(t + 1) * E]).then_inc(topi_done, 1)

            def top_floats(c):
                dve.wait_ge(topi_done, c.n * TILES + TILES)
                v.tensor_copy(top_f[:, :, :].rearrange("p k t -> p t k"), top_i[:, :, 0:TOP_K]).then_inc(topf_done, 1)

            def one_hots(c):
                dve.wait_ge(topf_done, c.n + 1)
                for k in range(TOP_K):
                    v.tensor_tensor(per_tile(hot[:, k, :]), per_tile(iota8),
                                    top_f[:, k, :].unsqueeze(2).to_broadcast([P, TILES, E]), ALU.is_equal).then_inc(hot_done, 1)

            def either(c):
                dve.wait_ge(hot_done, c.n * 2 + 2)
                v.tensor_tensor(chosen[:, :], hot[:, 0, :], hot[:, 1, :], ALU.add).then_inc(chosen_done, 1)

            def gaps(c):
                v.tensor_tensor(hot_s[:, :, :], hot[:, :, :],
                                scores[:, 0:1, :].to_broadcast([P, TOP_K, TILES * E]), ALU.mult).then_inc(hots_done, 1)
                dve.wait_ge(hots_done, c.n + 1)
                v.tensor_reduce(got[:, :, :], hot_s[:, :, :].rearrange("p k (t e) -> p k t e", e=E), AX_X, ALU.add).then_inc(got_done, 1)
                dve.wait_ge(got_done, c.n + 1)
                v.tensor_tensor(gap[:, bass.ds(c.n * TILES, TILES)], got[:, 0, :], got[:, 1, :], ALU.subtract).then_inc(gap_done, 1)

            def slot_steps(c):
                def add_taken():
                    dve.wait_ge(rank_ready, c.n + 1)
                    if not (isinstance(c.n, int) and c.n == 0):
                        dve.wait_ge(taken_done, c.n)
                    v.tensor_tensor(per_tile(slot_e[:, :]), per_tile(RANK), taken[:, :].unsqueeze(1).to_broadcast([P, TILES, E]),
                                    ALU.add).then_inc(slote_done, 1)

                def take():
                    dve.wait_ge(slote_done, c.n + 1)
                    v.tensor_tensor(taken[:, :], TOTAL, taken[:, :], ALU.add).then_inc(taken_done, 1)

                def pick():
                    v.tensor_tensor(hot_r[:, :, :], hot[:, :, :],
                                    slot_e[:, :].unsqueeze(1).to_broadcast([P, TOP_K, TILES * E]), ALU.mult).then_inc(hotr_done, 1)

                def reduce():
                    dve.wait_ge(hotr_done, c.n + 1)
                    v.tensor_reduce(slot_f[:, :, :], hot_r[:, :, :].rearrange("p k (t e) -> p k t e", e=E), AX_X, ALU.add).then_inc(slotf_done, 1)

                def to_int():
                    dve.wait_ge(slotf_done, c.n + 1)
                    v.tensor_copy(slot[c.par][:, :, :], slot_f[:, :, :]).then_inc(slot_done, 1)

                return [add_taken, take, pick, reduce, to_int]

            def add_shared(c):
                dve.wait_ge(proj_done, c.n * SF + SF)
                v.scalar_tensor_tensor(out=base[:, bass.ds(c.n * TILES, TILES), :], in0=Y.rearrange("p (t d) -> p t d", d=C),
                                       scalar=0.5, in1=x1[c.par][:, :, :],
                                       op0=ALU.mult, op1=ALU.add).then_inc(base_done, 1)

            def step(c, q, n):
                if n is not None and q is not None:
                    dve.wait_ge(relu_done, n.n * 2)
                    scan_max(n)
                if c is not None:
                    values_state(c)
                if c is not None and q is not None:
                    values_out(c)
                if q is not None:
                    take_logits(q)
                if c is not None:
                    scan_q(c)
                if q is not None:
                    choose(q)
                if c is not None:
                    if q is None:
                        scan_p(c)
                        values_out(c)
                    old_part(c)
                    if q is not None:
                        scan_p(c)
                    denominators(c)
                    join(c)
                    gated_out(c, q)
                elif q is not None:
                    choose_max(q)
                if q is not None:
                    choose_index(q)
                    top_floats(q)
                    one_hots(q)
                    either(q)
                if n is not None and q is None:
                    scan_max(n)
                steps = slot_steps(q) if q is not None else []
                if c is not None:
                    norm_stats(c)
                    rsqrt(c, rs_step, norm_done, steps)
                else:
                    for s in steps:
                        s()
                if q is None:
                    low_shared()
                if q is not None:
                    gaps(q)
                if c is not None:
                    split_rows(c)
                if q is not None and c is None:
                    units_table()
                if q is not None:
                    add_shared(q)

            def low_shared():
                v.scalar_tensor_tensor(out=sh_w[:, 1, :], in0=sh_raw[:, 0, :], scalar=SW, in1=sh_w[:, 0, :],
                                       op0=ALU.mult, op1=ALU.subtract).then_inc(prep, 1)

            def units_table():
                tab = [0]

                def link(ins):
                    ins.then_inc(table, 1)
                    tab[0] += 1
                    dve.wait_ge(table, tab[0])

                dve.wait_ge(taken_done, CHUNKS)
                v.tensor_copy(end_row[:, :], taken[:, :]).then_inc(ends_ready, 1)
                dve.wait_ge(scattered[0], CHUNKS // 2 * (TILES * TOP_K * 16))
                v.tensor_copy(rows[0][:, :, 0:2 * C], rows[1][:, :, 0:2 * C]).then_inc(copy_done, 1)
                link(v.tensor_tensor(cnt_f[:, :], taken[:, :], consts[:, K_EN:K_EN + E], ALU.add))
                link(v.tensor_copy(cnt_i[:, :], cnt_f[:, :]))
                link(v.tensor_scalar(tile_i[:, :], cnt_i[:, :], UT.bit_length() - 1, None, ALU.logical_shift_right))
                link(v.tensor_copy(tile_f[:, :], tile_i[:, :]))
                link(v.tensor_tensor_scan(cum[:, :], ones8[:, :], tile_f[:, :], 0.0, ALU.mult, ALU.add))
                cum_b = cum[:, :].unsqueeze(1).to_broadcast([P, UNITS, E])
                link(v.tensor_tensor(past[:, :, :], iota_u.unsqueeze(2).to_broadcast([P, UNITS, E]), cum_b, ALU.is_ge))
                link(v.tensor_reduce(unit_e[:, :], past[:, :, :], AX_X, ALU.add))
                link(v.tensor_tensor(past_c[:, :, :], past[:, :, :], cum_b, ALU.mult))
                link(v.tensor_reduce(unit_s[:, :], past_c[:, :, :], AX_X, ALU.max))
                link(v.tensor_tensor(unit_j[:, :], iota_u, unit_s[:, :], ALU.subtract))
                link(v.tensor_scalar(unit_r[:, :], unit_e[:, :], float(CAP), None, ALU.mult))
                link(v.scalar_tensor_tensor(out=unit_r2[:, :], in0=unit_j[:, :], scalar=float(UT), in1=unit_r[:, :],
                                            op0=ALU.mult, op1=ALU.add))
                link(v.tensor_scalar(unit_row[:, :], unit_r2[:, :], float(DUMP), None, ALU.min))
                link(v.memset(unit_w[:, UNITS:UNITS + 2 * RING], 0.0))
                link(v.tensor_scalar(unit_w[:, 0:UNITS], unit_e[:, :], float(E - 1), None, ALU.min))
                link(v.scalar_tensor_tensor(out=code2[:, :], in0=unit_w[:, 1:UNITS + 2 * RING - 1], scalar=float(E),
                                            in1=unit_w[:, 0:UNITS + 2 * RING - 2], op0=ALU.mult, op1=ALU.add))
                link(v.scalar_tensor_tensor(out=code4[:, :], in0=code2[:, 2:UNITS + RING + 2], scalar=float(E ** 2),
                                            in1=code2[:, 0:UNITS + RING], op0=ALU.mult, op1=ALU.add))
                link(v.scalar_tensor_tensor(out=codes[:, :, 0], in0=unit_w[:, RING:UNITS + RING], scalar=float(E ** RING),
                                            in1=code4[:, 0:UNITS], op0=ALU.mult, op1=ALU.add))
                v.scalar_tensor_tensor(out=codes[:, :, 1], in0=unit_w[:, 2 * RING:UNITS + 2 * RING], scalar=float(E ** RING),
                                       in1=code4[:, RING:UNITS + RING], op0=ALU.mult, op1=ALU.add).then_inc(table_ready, 1)

            count = [0]

            def counted(ins):
                ins.then_inc(prep, 1)
                count[0] += 1

            counted(v.memset(w_row[:, :], 0.0))
            counted(v.memset(state[0][:, 0, 0:1], -1e38))
            counted(v.memset(state[0][:, 1:3, 0:1], 0.0))
            counted(v.memset(ones8[:, :], 1.0))
            dve.wait_ge(att_in, 32)
            counted(v.tensor_scalar(one_minus[:, :], vec[:, 2:5], -1.0, 1.0, ALU.mult, ALU.add))
            dve.wait_ge(prep, count[0])
            for i in range(3):
                counted(v.tensor_scalar(att_w[:, i, 0, :], att_raw[:, i, :], vec[:, 2 + i:3 + i], None, ALU.mult))
                counted(v.tensor_scalar(att_w[:, i, 1, :], att_raw[:, i, :], one_minus[:, i:i + 1], None, ALU.mult))
                if i == 0:
                    assert count[0] == PREP_K
            assert count[0] == PREP_MIX
            dve.wait_ge(decay_done, 1)
            counted(v.tensor_scalar(neg_w[:, :], decay[:, :], -1.0, None, ALU.mult))
            dve.wait_ge(prep, count[0])
            counted(v.tensor_scalar(w_row[:, :], w_row[:, :], neg_w[:, 0:1], None, ALU.add))
            dve.wait_ge(prep, count[0])
            scan_max(Chunk(0, 0))
            dve.wait_ge(consts_in, 48)
            dve.wait_ge(shared_in, 48)
            counted(v.tensor_copy(taken[:, :], consts[:, K_EB:K_EB + E]))
            counted(v.tensor_scalar(cent_w[:, 0, :], cent_raw[:, :], SW, None, ALU.mult))
            counted(v.tensor_scalar(sh_w[:, 0, :], sh_raw[:, 0, :], SW, None, ALU.mult))
            dve.wait_ge(prep, count[0])
            counted(v.scalar_tensor_tensor(out=cent_w[:, 1, :], in0=cent_raw[:, :], scalar=SW, in1=cent_w[:, 0, :],
                                           op0=ALU.mult, op1=ALU.subtract))
            assert count[0] == PREP_ALL - 1, count[0]
            step(Chunk(0, 0), None, Chunk(0, 1))
            step(Chunk(0, 1), Chunk(0, 0), Chunk(1, 0))
            with dve.Fori(1, CHUNKS // 2 - 1) as h:
                step(Chunk(h, 0), Chunk(h - 1, 1), Chunk(h, 1))
                step(Chunk(h, 1), Chunk(h, 0), Chunk(h + 1, 0))
            step(LAST0, Chunk(CHUNKS // 2 - 2, 1), LAST1)
            step(LAST1, LAST0, None)
            step(None, LAST1, None)

            dve.wait_ge(gapt_done, 1)
            v.tensor_scalar(gap_1[:, :], gap_e[:, :], 1.0, None, ALU.add).then_inc(mix_step, 1)
            dve.wait_ge(mix_step, 1)
            v.reciprocal(gap_r[:, :], gap_1[:, :]).then_inc(mix_step, 1)
            dve.wait_ge(mix_step, 2)
            v.tensor_scalar(mix[:, 0, :], gap_r[:, :], 0.5, None, ALU.mult).then_inc(mix_done, 1)
            v.tensor_scalar(mix[:, 1, :], gap_r[:, :], -0.5, 0.5, ALU.mult, ALU.add).then_inc(mix_done, 1)

            def unit_split(u):
                b = u.buf % 2
                for h in range(2):
                    part = slice(h * 2 * UT, (h + 1) * 2 * UT)
                    dve.wait_ge(u_hid, u.n * 2 + 1 + h)
                    if h == 0 and not (isinstance(u.n, int) and u.n < 2):
                        dve.wait_ge(u_y, u.n - 1)
                    v.tensor_scalar(hid_h[b][:, part], hid[b][:, part], SH, None, ALU.mult).then_inc(u_hidh, 1)
                    dve.wait_ge(u_hidh, u.n * 2 + 1 + h)
                    v.scalar_tensor_tensor(out=hid_l[b][:, part], in0=hid[b][:, part], scalar=SH, in1=hid_h[b][:, part],
                                           op0=ALU.mult, op1=ALU.subtract).then_inc(u_hidl, 1)

            for u in FIRST_UNITS:
                unit_split(u)
            with dve.Fori(1, PASSES) as g:
                for j in range(BODY):
                    unit_split(Unit(g, j))

            def first_result(t):
                v.scalar_tensor_tensor(out=acc[0][:, t, :], in0=yl[:, t, 0:C], scalar=mix[:, 0, t:t + 1], in1=base[:, t, :],
                                       op0=ALU.mult, op1=ALU.add).then_inc(acc_0, 1)

            def second_result(k, t):
                j = k * TILES + t
                v.scalar_tensor_tensor(out=total[k // 2][:, k % 2 * TILES + t, :], in0=yl[:, j, C:2 * C], scalar=mix[:, 1, j:j + 1],
                                       in1=acc[k % 4][:, t, :], op0=ALU.mult, op1=ALU.add).then_inc(total_done, 1)

            def chunk_stats(k):
                dve.wait_ge(total_done, (k + 1) * TILES)
                for t in range(TILES):
                    j = k % 2 * TILES + t
                    v.bn_stats(bst[:, j, :], total[k // 2][:, j, :]).then_inc(f_bst, 1)

            def norm_steps(n):
                def guess():
                    dve.wait_ge(f_root, n + 1)
                    v.reciprocal(rs_y[:, :], root[:, :]).then_inc(f_rs, 1)

                def half_square():
                    dve.wait_ge(f_rs, n * 3 + 1)
                    v.scalar_tensor_tensor(out=rs_a[:, :], in0=rs_y[:, :], scalar=-0.5, in1=rs_y[:, :],
                                           op0=ALU.mult, op1=ALU.mult).then_inc(f_rs, 1)

                def times_var():
                    dve.wait_ge(f_rs, n * 3 + 2)
                    v.tensor_tensor(rs_b[:, :], rs_a[:, :], var_e[:, :], ALU.mult).then_inc(f_rs, 1)

                def newton():
                    dve.wait_ge(f_rs, n * 3 + 3)
                    if n > 1:
                        dve.wait_ge(fin_done, (n - 1) * 2 * TILES)
                    v.scalar_tensor_tensor(out=f_rstd[n % 2][:, :], in0=rs_b[:, :], scalar=1.5, in1=rs_y[:, :],
                                           op0=ALU.add, op1=ALU.mult).then_inc(f_norm, 1)

                def shifts():
                    dve.wait_ge(f_norm, n * 2 + 1)
                    v.scalar_tensor_tensor(out=f_shift[n % 2][:, :], in0=ln_m[:, :], scalar=-0.5, in1=f_rstd[n % 2][:, :],
                                           op0=ALU.mult, op1=ALU.mult).then_inc(f_norm, 1)
                return [guess, half_square, times_var, newton, shifts]

            dve.wait_ge(mix_done, 2)
            dve.wait_ge(yl_in[0], 16)
            for t in range(TILES):
                first_result(t)
            for n in range(CHUNKS // 2):
                steps = norm_steps(n - 1) if n > 0 else []
                for k in (2 * n, 2 * n + 1):
                    if k == 0:
                        dve.wait_ge(acc_0, TILES)
                    else:
                        dve.wait_ge(acc_done, k)
                    for t in range(TILES):
                        second_result(k, t)
                        if k % 2 == 0 and t < len(steps):
                            steps[t]()
                    if k % 2 == 0:
                        for step_left in steps[TILES:]:
                            step_left()
                    chunk_stats(k)
                moments(n, 2 * TILES, EPS / 4, f_bst, f_mv, f_var)
            n = CHUNKS // 2 - 1
            for last_step in norm_steps(n):
                last_step()
            dve.wait_ge(f_norm, n * 2 + 2)
            for i in range(2):
                dve.wait_ge(stored[2 + i], 16)
            for j in range(TILES - 1, 2 * TILES):
                k = n * 2 + j // TILES
                v.tensor_scalar(fin[k % 4][:, j % TILES, :], total[n][:, j, :], f_rstd[n % 2][:, j:j + 1], f_shift[n % 2][:, j:j + 1],
                                ALU.mult, ALU.add).then_inc(fin_last, 1)

        @block.gpsimd
        def _(pool):
            g_ = nc.gpsimd

            def hold_wait(i):
                g_.tensor_tensor(waiter[:, i, :], no_ids[:, :], no_ids[:, :], ALU.add)

            def numerator_a(c):
                pool.wait_ge(p_done, c.n + 1)
                pool.wait_ge(exp_out, c.n + 1)
                g_.tensor_tensor(ap_[:, :], expd[:, 0, 1, :], state[c.par][:, 1, 0:CH], ALU.mult).then_inc(ap_done, 1)

            def numerator_b(c):
                pool.wait_ge(ap_done, c.n + 1)
                pool.wait_ge(bv_done, c.n + 1)
                g_.tensor_tensor(num[:, :], ap_[:, :], bv[:, :], ALU.add).then_inc(num_done, 1)

            def low_weights(c):
                high, low = (rt_w[:, bass.ds(c.n, 1), s, :].rearrange("p a n -> p (a n)") for s in range(2))
                pool.wait_ge(w_high, c.n + 1)
                pool.wait_ge(w_scaled, c.n + 1)
                hold_wait(0)
                g_.tensor_tensor(low, stage[c.par][:, :], high, ALU.subtract).then_inc(w_low, 1)

            def result_rows(c, k, src):
                if k == 0:
                    pool.wait_ge(rows_done, c.n * 2 + 2)
                    pool.wait_ge(slot_done, c.n + 1)
                    if not (isinstance(c.half, int) and c.half == 0):
                        pool.wait_ge(scattered[c.par], c.half * (TILES * TOP_K * 16))
                elif src == c.par:
                    pool.wait_ge(scattered[c.par], c.half * (TILES * TOP_K * 16) + TILES * 16)
                else:
                    pool.wait_ge(copy_done, 1)
                g_.tensor_copy(rows[src][:, :, 2 * C:ROW].bitcast(I32),
                               row_ids[:, bass.ds(c.n * TILES, TILES), k:k + 1]).then_inc(ids_done, 1)
                pool.wait_ge(ids_done, c.n * 2 + k + 1)

            def scatter(c, k, src):
                for t in range(TILES):
                    g_.indirect_dma_start(sorted_x, bass.IndirectOffsetOnAxis(ap=slot[c.par][:, k, t:t + 1].bitcast(U32), axis=0),
                                          rows[src][:, t, :], None).then_inc(scattered[c.par], 16)

            def step(c, q):
                if c is not None:
                    numerator_a(c)
                    numerator_b(c)
                    low_weights(c)
                if q is not None:
                    for k in range(TOP_K):
                        src = 0 if c is None and k == 1 else q.par
                        result_rows(q, k, src)
                        hold_wait(0)
                        scatter(q, k, src)

            pool.wait_ge(consts_in, 48)
            g_.memset(no_ids[:, :], 0).then_inc(ids_made, 1)
            pool.wait_ge(ids_made, 1)
            g_.memset(pad[:, :, 0:2 * C], 0.0).then_inc(pad_made, 1)
            g_.memset(pad[:, :, 2 * C:ROW].bitcast(I32), TOKENS * TOP_K).then_inc(pad_made, 1)
            step(Chunk(0, 0), None)
            step(Chunk(0, 1), Chunk(0, 0))
            with pool.Fori(1, CHUNKS // 2) as h:
                step(Chunk(h, 0), Chunk(h - 1, 1))
                step(Chunk(h, 1), Chunk(h, 0))
            step(None, Chunk(CHUNKS // 2 - 1, 1))

            def unit_ids(u):
                pool.wait_ge(xs_in[u.buf], (u.turn + 1) * 16)
                if not u.first:
                    pool.wait_ge(y_out[u.buf], u.turn * (16 * UH))
                g_.tensor_tensor(unit_id[u.buf][:, :], xs[u.buf][:, :, 2 * C:ROW].bitcast(I32).rearrange("p k a -> p (k a)"),
                                 no_ids[:, :], ALU.add).then_inc(u_ids, 1)

            def put_results(u):
                for k in range(UH):
                    g_.indirect_dma_start(routed_y, bass.IndirectOffsetOnAxis(ap=unit_id[u.buf][:, k:k + 1].bitcast(U32), axis=0),
                                          ys[u.buf][:, k, :], None, bounds_check=TOKENS * TOP_K - 1,
                                          oob_is_err=False).then_inc(y_out[u.buf], 16)

            def ids_and_put(u):
                pool.wait_ge(u_ids, u.n)
                pool.wait_ge(u_ys, u.n)
                unit_ids(u)
                put_results(u.back(1))

            unit_ids(FIRST_UNITS[0])
            for u in FIRST_UNITS[1:]:
                ids_and_put(u)
            with pool.Fori(1, PASSES) as g:
                for j in range(BODY):
                    ids_and_put(Unit(g, j))
            pool.wait_ge(u_ids, UNITS)
            pool.wait_ge(u_ys, UNITS)
            put_results(LAST_UNIT)

            def first_results(n):
                tiles = slice(n * TILES, (n + 1) * TILES)
                pool.wait_ge(yl_in[n], 16)
                if n >= 3:
                    pool.wait_ge(acc_done, n - 2)
                g_.tensor_tensor(weighted[n % 2][:, :, :], yl[:, tiles, 0:C], mix[:, 0, tiles].unsqueeze(2).to_broadcast([P, TILES, C]),
                                 ALU.mult).then_inc(weighted_done, 1)
                pool.wait_ge(weighted_done, n)
                if n >= 4:
                    pool.wait_ge(total_done, (n - 3) * TILES)
                g_.tensor_tensor(acc[n % 4][:, :, :], weighted[n % 2][:, :, :], base[:, tiles, :], ALU.add).then_inc(acc_done, 1)

            pool.wait_ge(mix_done, 2)
            for n in range(1, CHUNKS):
                first_results(n)


PREP_K, PREP_MIX, PREP_ALL = 7, 11, 18


def kernel(**inputs):
    import numpy as _np
    import concourse.bacc as _bacc
    from concourse import mybir as _mybir
    from concourse.bass_utils import run_bass_kernel_spmd as _run

    a = {k: _np.asarray(x) for k, x in inputs.items()}
    x = a["L0_attn_x"]
    xT = _np.zeros((C, B, T + 1), _np.float32)
    xT[:, :, 1:] = x.transpose(2, 0, 1)
    w_att = _np.stack([a[f"L0_attn_W_{n}"].T for n in ("key", "value", "receptance", "output")], axis=1)
    vecs = _np.stack([a[f"L0_attn_time_{n}"].reshape(C) for n in ("decay", "first", "mix_k", "mix_v", "mix_r")], axis=1)

    def layers(fc, proj):
        n = fc.shape[0]
        one = fc.transpose(0, 2, 1)
        two = proj.reshape(n, C, FC, P).transpose(0, 3, 2, 1).reshape(n, P, FF)
        return _np.stack([one, two], axis=2)

    w_sh = layers(a["L0_ffn_Wfc_sh"], a["L0_ffn_Wproj_sh"]).transpose(1, 2, 0, 3).reshape(P, 2, SF * P)
    w_rt = layers(a["L0_ffn_Wfc_r"], a["L0_ffn_Wproj_r"]).reshape(E, P, 2 * FF)
    cent = a["L0_ffn_centroids"].T
    bias = _np.broadcast_to(a["L0_ffn_routing_bias"][None, None, :], (P, TILES, E)).reshape(P, TILES * E)
    kf = _np.zeros((P, K_END), _np.float32)
    kf[:, K_ID:K_ID + P] = _np.eye(P)
    kf[:, K_I8:K_I8 + TILES * E] = _np.tile(_np.arange(E), TILES)
    kf[:, K_EB:K_EB + E] = _np.arange(E) * CAP
    kf[:, K_EN:K_EN + E] = UT - 1 - _np.arange(E) * CAP
    kf[:, K_IU:K_IU + UNITS] = _np.arange(UNITS)
    kh = _np.concatenate([_np.eye(P), _np.triu(_np.ones((P, P)), 1), _np.ones((P, P))], axis=1).astype(_np.float16)
    token = _np.arange(NT)[None, :, None] * P + _np.arange(P)[:, None, None]
    kid = (token * TOP_K + _np.arange(TOP_K)[None, None, :]).astype(_np.int32)

    nc = _bacc.Bacc("TRN2", target_bir_lowering=False, num_devices=1)
    arrays, args = {}, []
    for name, arr in dict(xT=xT, w_att=w_att, vecs=vecs, w_sh=w_sh, w_rt=w_rt, cent=cent, bias=bias, kf=kf, kh=kh, kid=kid).items():
        arr = _np.ascontiguousarray(arr)
        arrays[f"in_{name}"] = arr
        args.append(nc.dram_tensor(f"in_{name}", arr.shape, _mybir.dt.from_np(arr.dtype), kind="ExternalInput").ap())
    args.append(nc.dram_tensor("out_0", (B, T, C), _mybir.dt.float32, kind="ExternalOutput").ap())
    build(nc, *args)
    r = _run(nc, [arrays], core_ids=[0])
    return r.results[0]["out_0"]
```
